# Optimizing a Trainium2 kernel written in Bass

```python
import numpy as np
import jax
import jax.numpy as jnp

def _softmax(x, axis=-1):
    return jax.nn.softmax(x, axis=axis)

def _gelu(x):
    return jax.nn.gelu(x, approximate=True)

def _silu(x):
    return jax.nn.silu(x)

def _sigmoid(x):
    return jax.nn.sigmoid(x)

def _layernorm(x, axis=-1, eps=1e-05):
    m = jnp.mean(x, axis=axis, keepdims=True)
    v = jnp.var(x, axis=axis, keepdims=True)
    return (x - m) / jnp.sqrt(v + eps)

def _scatter_add(tgt, idx, src, axis=0):
    return tgt.at[idx].add(src)

def _segment_sum(src, seg, n):
    return jax.ops.segment_sum(src, seg, n)
kernel_name = 'mk_flamingo_gated_d2_seqx_r8_9cee99'

def setup_inputs(seed: int=0):
    np.random.seed(seed)
    _w = jnp.asarray

    def _rec_inputs():
        import jax
        import jax.numpy as jnp
        _rk = jax.random.key(seed)
        x = -0.0005207 + 1.001 * jax.random.normal(jax.random.fold_in(_rk, 1), (64, 64, 256), jnp.float32)
        _lenS = 64 - jax.random.randint(jax.random.fold_in(_rk, 7), (64,), 0, max(1, 64 // 4) + 1, jnp.int32)
        _lenS2 = 64 - jax.random.randint(jax.random.fold_in(_rk, 8), (64,), 0, max(1, 64 // 4) + 1, jnp.int32)
        _ctx_2048P = jax.random.normal(jax.random.fold_in(_rk, 11), (64, 16, 256), jnp.float32)
        _ctx_2048c = jax.random.dirichlet(jax.random.fold_in(_rk, 511), 0.3 * jnp.ones((16,), jnp.float32), (64, 64))
        _ctx_2048t = jnp.einsum('bsk,bkd->bsd', _ctx_2048c, _ctx_2048P)
        _ctx_2048t = _ctx_2048t * jax.lax.rsqrt(jnp.mean(jnp.square(_ctx_2048t)) + 1e-12) * 0.953939
        ctx_2048 = 2.81802e-05 + 1.00001 * (_ctx_2048t + 0.3 * jax.random.normal(jax.random.fold_in(_rk, 611), (64, 64, 256), jnp.float32))
        pos_BxS2 = jnp.broadcast_to(jnp.arange(64, dtype=jnp.int32), (64, 64))
        itok_BxS_4096_4607 = jax.random.randint(jax.random.fold_in(_rk, 13), (64, 64), 512, 576, jnp.int32)
        _validS = jnp.arange(64)[None, :] < _lenS[:, None]
        _validS2 = jnp.arange(64)[None, :] < _lenS2[:, None]
        _causal = jnp.tril(jnp.ones((64, 64), dtype=bool))
        mask_BxS2_ik0 = jnp.where(jnp.broadcast_to(_validS2[:, :], (64, 64)), 0, 1).astype(jnp.int32)
        _g = jax.random.normal(jax.random.fold_in(_rk, 9001), (2, 2), jnp.float32)
        _g = jnp.sign(_g) * jnp.maximum(jnp.abs(_g), 1.0) + (_g == 0) * 1.0
        g_xattn = _g[0]
        g_ffn = _g[1]
        return (x, ctx_2048, pos_BxS2, itok_BxS_4096_4607, mask_BxS2_ik0, g_xattn, g_ffn)
    x, ctx_2048, pos_BxS2, itok_BxS_4096_4607, mask_BxS2_ik0, g_xattn, g_ffn = _rec_inputs()

    def _L0_xattn_setup():
        import jax, jax.numpy as jnp
        import numpy as np
        B, CTX, DRAFT, D = (2, 512, 64, 256)
        H, KVH, HD = (16, 4, 128)
        N_REP = H // KVH
        EPS = 1e-06
        THETA = 10000.0
        SCALE = 1.0 / np.sqrt(HD).astype(np.float32)

        def _rms_norm(x, w):
            v = jnp.mean(jnp.square(x.astype(jnp.float32)), axis=-1, keepdims=True)
            return (w * (x.astype(jnp.float32) * jax.lax.rsqrt(v + EPS))).astype(x.dtype)

        def _rotate_half(x):
            x1, x2 = jnp.split(x, 2, axis=-1)
            return jnp.concatenate((-x2, x1), axis=-1)

        def _rope(x, pos):
            inv_freq = 1.0 / THETA ** (jnp.arange(0, HD, 2, dtype=jnp.float32) / HD)
            freqs = pos.astype(jnp.float32)[:, None, :, None] * inv_freq
            emb = jnp.concatenate((freqs, freqs), axis=-1)
            return x * jnp.cos(emb) + _rotate_half(x) * jnp.sin(emb)
        key = jax.random.key(seed)
        ks = jax.random.split(key, 6)
        return {'draft_hidden': jax.random.normal(ks[0], (B, DRAFT, D), jnp.float32), 'context_hidden': jax.random.normal(ks[1], (B, CTX, D), jnp.float32), 'Wq': jax.random.normal(ks[2], (H * HD, D), jnp.float32) * 0.02, 'Wk': jax.random.normal(ks[3], (KVH * HD, D), jnp.float32) * 0.02, 'Wv': jax.random.normal(ks[4], (KVH * HD, D), jnp.float32) * 0.02, 'Wo': jax.random.normal(ks[5], (D, H * HD), jnp.float32) * 0.02, 'q_norm_w': jnp.ones((HD,), jnp.float32), 'k_norm_w': jnp.ones((HD,), jnp.float32), 'context_position_ids': jnp.broadcast_to(jnp.arange(CTX, dtype=jnp.int32), (B, CTX)), 'draft_position_ids': jnp.broadcast_to(CTX + jnp.arange(DRAFT, dtype=jnp.int32), (B, DRAFT))}
    _L0_xattn_all = _L0_xattn_setup()
    _L0_xattn_in = {k: v for k, v in _L0_xattn_all.items() if k in ('Wq', 'Wk', 'Wv', 'Wo', 'q_norm_w', 'k_norm_w')}
    del _L0_xattn_all

    def _L0_ffn_setup():
        import jax, jax.numpy as jnp
        import numpy as np
        NUM_EXPERTS = 8
        TOP_K = 2
        EMB = 256
        MLP = 512
        B, S = (4, 128)
        key = jax.random.key(seed)
        ks = jax.random.split(key, 5)
        scale_x = 1.0
        return {'x': jax.random.normal(ks[0], (B, S, EMB), dtype=jnp.float32), 'gate_kernel': jax.random.normal(ks[1], (EMB, NUM_EXPERTS), dtype=jnp.float32) / np.sqrt(EMB), 'w0_kernel': jax.random.normal(ks[2], (NUM_EXPERTS, EMB, MLP), dtype=jnp.float32) / np.sqrt(EMB), 'w1_kernel': jax.random.normal(ks[3], (NUM_EXPERTS, EMB, MLP), dtype=jnp.float32) / np.sqrt(EMB), 'wo_kernel': jax.random.normal(ks[4], (NUM_EXPERTS, MLP, EMB), dtype=jnp.float32) / np.sqrt(MLP)}
    _L0_ffn_all = _L0_ffn_setup()
    _L0_ffn_in = {k: v for k, v in _L0_ffn_all.items() if k in ('gate_kernel', 'w0_kernel', 'w1_kernel', 'wo_kernel')}
    del _L0_ffn_all

    def _L1_xattn_setup():
        import jax, jax.numpy as jnp
        import numpy as np
        import math
        H = 256
        NH = 16
        HD = H // NH
        EPS_LN = 1e-05
        RES_SCALE_MAX = 0.3

        def _nan_clean(x, lim=10000.0):
            return jnp.nan_to_num(x, nan=0.0, posinf=lim, neginf=-lim)
        key = jax.random.key(seed)
        ks = jax.random.split(key, 12)
        B, S, T = (4, 256, 32)
        std = 1.0 / math.sqrt(H)
        return {'hidden_states': jax.random.normal(ks[0], (B, S, H), jnp.float32), 'audio_tokens': jax.random.normal(ks[1], (B, T, H), jnp.float32), 'attention_mask': jax.random.randint(ks[2], (B, T), 0, 2, jnp.int32), 'Wq': jax.random.normal(ks[3], (H, H), jnp.float32) * std, 'bq': jnp.zeros((H,), jnp.float32), 'Wk': jax.random.normal(ks[4], (H, H), jnp.float32) * std, 'bk': jnp.zeros((H,), jnp.float32), 'Wv': jax.random.normal(ks[5], (H, H), jnp.float32) * std, 'bv': jnp.zeros((H,), jnp.float32), 'Wo': jax.random.normal(ks[6], (H, H), jnp.float32) * std, 'bo': jnp.zeros((H,), jnp.float32), 'ln_gamma': jnp.ones((H,), jnp.float32), 'ln_beta': jnp.zeros((H,), jnp.float32), 'residual_scale': jnp.float32(0.05)}
    _L1_xattn_all = _L1_xattn_setup()
    _L1_xattn_in = {k: v for k, v in _L1_xattn_all.items() if k in ('Wq', 'bq', 'Wk', 'bk', 'Wv', 'bv', 'Wo', 'bo', 'ln_gamma', 'ln_beta', 'residual_scale')}
    del _L1_xattn_all

    def _L1_ffn_setup():
        import jax, jax.numpy as jnp
        import numpy as np
        import math
        NUM_EXPERTS = 12
        TOP_K = 2
        CAP_FACTOR = 1.25
        key = jax.random.key(seed)
        k0, k1, k2, k3, k4 = jax.random.split(key, 5)
        B, S, H, F = (4, 512, 256, 32)
        hidden_states = jax.random.normal(k0, (B, S, H), jnp.float32)
        gate_w = jax.random.normal(k1, (NUM_EXPERTS, H), jnp.float32) * 0.02
        w1 = jax.random.normal(k2, (NUM_EXPERTS, F, H), jnp.float32) * 0.02
        w2 = jax.random.normal(k3, (NUM_EXPERTS, H, F), jnp.float32) * 0.02
        w3 = jax.random.normal(k4, (NUM_EXPERTS, F, H), jnp.float32) * 0.02
        return dict(hidden_states=hidden_states, gate_w=gate_w, w1=w1, w2=w2, w3=w3)
    _L1_ffn_all = _L1_ffn_setup()
    _L1_ffn_in = {k: v for k, v in _L1_ffn_all.items() if k in ('gate_w', 'w1', 'w2', 'w3')}
    del _L1_ffn_all
    return {'x': x, 'ctx_2048': ctx_2048, 'pos_BxS2': pos_BxS2, 'itok_BxS_4096_4607': itok_BxS_4096_4607, 'mask_BxS2_ik0': mask_BxS2_ik0, 'g_xattn': g_xattn, 'g_ffn': g_ffn, 'L0_xattn_Wq': _L0_xattn_in['Wq'], 'L0_xattn_Wk': _L0_xattn_in['Wk'], 'L0_xattn_Wv': _L0_xattn_in['Wv'], 'L0_xattn_Wo': _L0_xattn_in['Wo'], 'L0_xattn_q_norm_w': _L0_xattn_in['q_norm_w'], 'L0_xattn_k_norm_w': _L0_xattn_in['k_norm_w'], 'L0_ffn_gate_kernel': _L0_ffn_in['gate_kernel'], 'L0_ffn_w0_kernel': _L0_ffn_in['w0_kernel'], 'L0_ffn_w1_kernel': _L0_ffn_in['w1_kernel'], 'L0_ffn_wo_kernel': _L0_ffn_in['wo_kernel'], 'L1_xattn_Wq': _L1_xattn_in['Wq'], 'L1_xattn_bq': _L1_xattn_in['bq'], 'L1_xattn_Wk': _L1_xattn_in['Wk'], 'L1_xattn_bk': _L1_xattn_in['bk'], 'L1_xattn_Wv': _L1_xattn_in['Wv'], 'L1_xattn_bv': _L1_xattn_in['bv'], 'L1_xattn_Wo': _L1_xattn_in['Wo'], 'L1_xattn_bo': _L1_xattn_in['bo'], 'L1_xattn_ln_gamma': _L1_xattn_in['ln_gamma'], 'L1_xattn_ln_beta': _L1_xattn_in['ln_beta'], 'L1_xattn_residual_scale': _L1_xattn_in['residual_scale'], 'L1_ffn_gate_w': _L1_ffn_in['gate_w'], 'L1_ffn_w1': _L1_ffn_in['w1'], 'L1_ffn_w2': _L1_ffn_in['w2'], 'L1_ffn_w3': _L1_ffn_in['w3']}

def reference(x, ctx_2048, pos_BxS2, itok_BxS_4096_4607, mask_BxS2_ik0, g_xattn, g_ffn, L0_xattn_Wq, L0_xattn_Wk, L0_xattn_Wv, L0_xattn_Wo, L0_xattn_q_norm_w, L0_xattn_k_norm_w, L0_ffn_gate_kernel, L0_ffn_w0_kernel, L0_ffn_w1_kernel, L0_ffn_wo_kernel, L1_xattn_Wq, L1_xattn_bq, L1_xattn_Wk, L1_xattn_bk, L1_xattn_Wv, L1_xattn_bv, L1_xattn_Wo, L1_xattn_bo, L1_xattn_ln_gamma, L1_xattn_ln_beta, L1_xattn_residual_scale, L1_ffn_gate_w, L1_ffn_w1, L1_ffn_w2, L1_ffn_w3):
    import jax
    import jax.numpy as jnp

    def _L0_xattn_ref(draft_hidden, context_hidden, Wq, Wk, Wv, Wo, q_norm_w, k_norm_w, context_position_ids, draft_position_ids):
        import jax, jax.numpy as jnp
        import numpy as np
        B, CTX, DRAFT, D = (2, 512, 64, 256)
        H, KVH, HD = (16, 4, 128)
        N_REP = H // KVH
        EPS = 1e-06
        THETA = 10000.0
        SCALE = 1.0 / np.sqrt(HD).astype(np.float32)

        def _rms_norm(x, w):
            v = jnp.mean(jnp.square(x.astype(jnp.float32)), axis=-1, keepdims=True)
            return (w * (x.astype(jnp.float32) * jax.lax.rsqrt(v + EPS))).astype(x.dtype)

        def _rotate_half(x):
            x1, x2 = jnp.split(x, 2, axis=-1)
            return jnp.concatenate((-x2, x1), axis=-1)

        def _rope(x, pos):
            inv_freq = 1.0 / THETA ** (jnp.arange(0, HD, 2, dtype=jnp.float32) / HD)
            freqs = pos.astype(jnp.float32)[:, None, :, None] * inv_freq
            emb = jnp.concatenate((freqs, freqs), axis=-1)
            return x * jnp.cos(emb) + _rotate_half(x) * jnp.sin(emb)
        bsz, draft_len, _ = draft_hidden.shape
        ctx_len = context_hidden.shape[1]
        total_len = ctx_len + draft_len
        q = (draft_hidden @ Wq.T).reshape(bsz, draft_len, H, HD)
        q = _rms_norm(q, q_norm_w).transpose(0, 2, 1, 3)
        kv_in = jnp.concatenate([context_hidden, draft_hidden], axis=1)
        k = (kv_in @ Wk.T).reshape(bsz, total_len, KVH, HD)
        v = (kv_in @ Wv.T).reshape(bsz, total_len, KVH, HD).transpose(0, 2, 1, 3)
        k = _rms_norm(k, k_norm_w).transpose(0, 2, 1, 3)
        full_position_ids = jnp.concatenate([context_position_ids, draft_position_ids], axis=1)
        q = _rope(q, draft_position_ids)
        k = _rope(k, full_position_ids)
        k = jnp.repeat(k, N_REP, axis=1)
        v = jnp.repeat(v, N_REP, axis=1)
        scores = jnp.einsum('bhqd,bhkd->bhqk', q, k) * SCALE
        probs = jax.nn.softmax(scores, axis=-1)
        attn = jnp.einsum('bhqk,bhkd->bhqd', probs, v)
        attn = attn.transpose(0, 2, 1, 3).reshape(bsz, draft_len, H * HD)
        return attn @ Wo.T

    def _L0_ffn_ref(x, gate_kernel, w0_kernel, w1_kernel, wo_kernel):
        import jax, jax.numpy as jnp
        import numpy as np
        NUM_EXPERTS = 8
        TOP_K = 2
        EMB = 256
        MLP = 512
        B, S = (4, 128)
        gate_logits = jnp.einsum('bsd,de->bse', x, gate_kernel)
        top_k_weights, top_k_indices = jax.lax.top_k(gate_logits, TOP_K)
        top_k_weights = jax.nn.softmax(top_k_weights.astype(jnp.float32), axis=-1).astype(x.dtype)
        one_hot = jax.nn.one_hot(top_k_indices, NUM_EXPERTS, dtype=x.dtype)
        combine = jnp.einsum('bsk,bske->bse', top_k_weights, one_hot)
        h0 = jnp.einsum('bsd,edm->bsem', x, w0_kernel)
        h1 = jnp.einsum('bsd,edm->bsem', x, w1_kernel)
        inter = jax.nn.silu(h0) * h1
        out = jnp.einsum('bse,bsem,emd->bsd', combine, inter, wo_kernel)
        return out

    def _L1_xattn_ref(hidden_states, audio_tokens, attention_mask, Wq, bq, Wk, bk, Wv, bv, Wo, bo, ln_gamma, ln_beta, residual_scale):
        import jax, jax.numpy as jnp
        import numpy as np
        import math
        H = 256
        NH = 16
        HD = H // NH
        EPS_LN = 1e-05
        RES_SCALE_MAX = 0.3

        def _nan_clean(x, lim=10000.0):
            return jnp.nan_to_num(x, nan=0.0, posinf=lim, neginf=-lim)
        B, S, _ = hidden_states.shape
        T = audio_tokens.shape[1]
        hs = _nan_clean(hidden_states).astype(jnp.float32)
        at = _nan_clean(audio_tokens).astype(jnp.float32)

        def proj(x, W, b, L):
            y = x @ W.T + b
            return y.reshape(B, L, NH, HD).transpose(0, 2, 1, 3)
        q = _nan_clean(proj(hs, Wq, bq, S))
        k = _nan_clean(proj(at, Wk, bk, T))
        v = _nan_clean(proj(at, Wv, bv, T))
        scale = max(math.sqrt(HD), 1e-08)
        scores = jnp.einsum('bhsd,bhtd->bhst', q, k) / scale
        scores = jnp.clip(scores, -50.0, 50.0)
        scores = jnp.nan_to_num(scores, nan=0.0, posinf=50.0, neginf=-50.0)
        attend = (attention_mask.astype(jnp.float32) > 0.5)[:, None, None, :]
        scores = jnp.where(attend, scores, -10000.0)
        scores = jnp.clip(scores, -50.0, 50.0)
        probs = jax.nn.softmax(scores, axis=-1)
        probs = jnp.nan_to_num(probs, nan=0.0, posinf=1.0, neginf=0.0)
        probs = probs / (probs.sum(axis=-1, keepdims=True) + 1e-08)
        ctx = jnp.einsum('bhst,bhtd->bhsd', probs, v)
        ctx = ctx.transpose(0, 2, 1, 3).reshape(B, S, H)
        delta = _nan_clean(ctx @ Wo.T + bo)
        rs = jnp.clip(residual_scale, 0.0, RES_SCALE_MAX)
        delta = rs * delta
        mu = delta.mean(axis=-1, keepdims=True)
        var = jnp.mean((delta - mu) ** 2, axis=-1, keepdims=True)
        delta = (delta - mu) / jnp.sqrt(var + EPS_LN) * ln_gamma + ln_beta
        return delta

    def _L1_ffn_ref(hidden_states, gate_w, w1, w2, w3):
        import jax, jax.numpy as jnp
        import numpy as np
        import math
        NUM_EXPERTS = 12
        TOP_K = 2
        CAP_FACTOR = 1.25
        B, S, H = hidden_states.shape
        T = B * S
        E = gate_w.shape[0]
        cap = math.ceil(T / E * CAP_FACTOR)
        x = hidden_states.reshape(T, H)
        logits = x @ gate_w.T
        probs = jax.nn.softmax(logits, axis=-1)
        rw, sel = jax.lax.top_k(probs, TOP_K)
        rw = rw / rw.sum(axis=-1, keepdims=True)
        ar_cap = jnp.arange(cap)
        ar_flat = jnp.arange(TOP_K * T, dtype=jnp.int32)

        def per_expert(e, we1, we2, we3):
            mask = sel.T == e
            fm = mask.ravel()
            pos = jnp.cumsum(fm) - 1
            slot_idx = jnp.where(fm & (pos < cap), pos, cap)
            buf = jnp.zeros(cap + 1, jnp.int32).at[slot_idx].set(ar_flat)
            flat = buf[:cap]
            valid = ar_cap < fm.sum()
            tok = flat % T
            slot = flat // T
            xs = x[tok]
            h = jax.nn.silu(xs @ we1.T * (xs @ we3.T)) @ we2.T
            w = jnp.where(valid, rw[tok, slot], 0.0)
            return (tok, h * w[:, None])
        toks, contribs = jax.vmap(per_expert)(jnp.arange(E), w1, w2, w3)
        out = jnp.zeros((T, H), x.dtype).at[toks.ravel()].add(contribs.reshape(-1, H))
        return out.reshape(B, S, H)
    x = x + jnp.tanh(g_xattn[0]) * _L0_xattn_ref(_layernorm(x, axis=-1), ctx_2048, L0_xattn_Wq, L0_xattn_Wk, L0_xattn_Wv, L0_xattn_Wo, L0_xattn_q_norm_w, L0_xattn_k_norm_w, pos_BxS2, itok_BxS_4096_4607)
    x = x + jnp.tanh(g_ffn[0]) * _L0_ffn_ref(_layernorm(x, axis=-1), L0_ffn_gate_kernel, L0_ffn_w0_kernel, L0_ffn_w1_kernel, L0_ffn_wo_kernel)
    x = x + jnp.tanh(g_xattn[1]) * _L1_xattn_ref(_layernorm(x, axis=-1), ctx_2048, mask_BxS2_ik0, L1_xattn_Wq, L1_xattn_bq, L1_xattn_Wk, L1_xattn_bk, L1_xattn_Wv, L1_xattn_bv, L1_xattn_Wo, L1_xattn_bo, L1_xattn_ln_gamma, L1_xattn_ln_beta, L1_xattn_residual_scale)
    x = x + jnp.tanh(g_ffn[1]) * _L1_ffn_ref(_layernorm(x, axis=-1), L1_ffn_gate_w, L1_ffn_w1, L1_ffn_w2, L1_ffn_w3)
    return x

_drawn_inputs = setup_inputs


def setup_inputs(seed=0):
    import zlib

    import numpy as np

    out = dict(_drawn_inputs(seed))
    spreads = {'g_ffn': (-1.0, 0.6),
     'L0_xattn_q_norm_w': (1.0, 0.6),
     'L0_xattn_k_norm_w': (1.0, 0.6),
     'L1_xattn_bq': (0.0, 0.283),
     'L1_xattn_bk': (0.0, 0.8),
     'L1_xattn_bv': (0.0, 0.1),
     'L1_xattn_bo': (0.0, 0.1),
     'L1_xattn_ln_gamma': (1.0, 0.2),
     'L1_xattn_ln_beta': (0.0, 0.1)}
    factors = {'L1_ffn_gate_w': 8.0, 'L1_ffn_w1': 8.0, 'L1_ffn_w2': 8.0, 'L1_ffn_w3': 8.0}
    for name, (base, spread) in spreads.items():
        noise = np.random.default_rng([zlib.crc32(name.encode()), seed]).standard_normal(out[name].shape)
        drawn = base * np.exp(spread * noise) if base else spread * noise
        out[name] = jnp.asarray(drawn.astype(out[name].dtype))
    for name, factor in factors.items():
        out[name] = (out[name] * factor).astype(out[name].dtype)
    return out
```

```python
from contextlib import ExitStack

import numpy as np
import concourse.bass as bass
from concourse import mybir

F32 = mybir.dt.float32
F16 = mybir.dt.float16
I32 = mybir.dt.int32
ALU = mybir.AluOpType
ACT = mybir.ActivationFunctionType
AX_X = mybir.AxisListType.X

P = 128
D = 256
DC = D // P
S = 64
NB = 2
H0, KV0, HD0 = 16, 4, 128
GROUP = H0 // KV0
E0, F0 = 8, 512
FC = F0 // P
E1, F1 = 12, 32
HALF = HD0 // 2
WSCALE = 64.0
EPS_LN = 1e-5
EPS_RMS = 1e-6
THETA = 10000.0
TWO_PI = 2.0 * np.pi
PI_A = 6.28125
PI_B = float(np.float32(np.round((TWO_PI - PI_A) * 2.0**21) / 2.0**21))
PI_C = float(TWO_PI - PI_A - PI_B)
ROUND = 1.5 * 2.0**23


def this(n, t, k):
    return n * t + n + k


def last(n, t, k):
    return n * t + k


def rope_tables(nc, NT, pos, freq_dram, rope_dram):
    W = NT * 2 * HALF
    with ExitStack() as ctx:
        sb = lambda name, shape, dt: ctx.enter_context(nc.sbuf_tensor(name, shape, dt))
        sem = lambda name: ctx.enter_context(nc.semaphore(name))
        pos_i = sb("pos_i", [P, NT * 2], I32)
        pos_f = sb("pos_f", [P, NT * 2, 1], F32)
        freq = sb("freq", [P, 1, HALF], F32)
        angle = sb("angle", [P, NT * 2, HALF], F32)
        turns = sb("turns", [P, NT * 2, HALF], F32)
        table = sb("table", [P, NT * 2, 2, HALF], F32)
        pos_in, freq_set, step, shifted, tables_made, stored = map(sem, (
            "pos_in", "freq_set", "rope_step", "rope_shifted", "tables_made", "rope_stored"))
        block = ctx.enter_context(nc.Block())

        @block.sync
        def _(sp):
            sp.dma_start(pos_i[:, :], pos).then_inc(pos_in, 16)
            sp.dma_start(freq[:, 0, :], freq_dram).then_inc(freq_set, 16)
            sp.wait_ge(tables_made, 2)
            sp.dma_start(rope_dram.rearrange("(t p) w -> p t w", p=P),
                         table[:, :, :, :].rearrange("p (t s) c d -> p t (s c d)", s=2)).then_inc(stored, 16)
            sp.wait_ge(stored, 16)

        @block.vector
        def _(dve):
            dve.wait_ge(pos_in, 16)
            dve.tensor_copy(pos_f[:, :, 0], pos_i[:, :]).then_inc(step, 1)
            dve.wait_ge(freq_set, 16)
            dve.wait_ge(step, 1)
            shape = [P, NT * 2, HALF]
            dve.tensor_tensor(angle[:, :, :], pos_f[:, :, :].broadcast_to(shape), freq[:, :, :].broadcast_to(shape),
                              ALU.mult).then_inc(step, 1)
            dve.wait_ge(step, 2)
            dve.tensor_scalar(turns[:, :, :], angle[:, :, :], 1.0 / TWO_PI, ROUND, ALU.mult, ALU.add).then_inc(step, 1)
            dve.wait_ge(step, 3)
            dve.tensor_scalar(turns[:, :, :], turns[:, :, :], -ROUND, None, ALU.add).then_inc(step, 1)
            for n, part in enumerate((PI_A, PI_B, PI_C)):
                dve.wait_ge(step, 4 + n)
                dve.scalar_tensor_tensor(out=angle[:, :, :], in0=turns[:, :, :], scalar=-part, in1=angle[:, :, :],
                                         op0=ALU.mult, op1=ALU.add).then_inc(step, 1)
            dve.wait_ge(step, 7)
            dve.tensor_scalar(angle[:, :, :], angle[:, :, :], -3.1415925, 3.1415925, ALU.max, ALU.min).then_inc(step, 1)
            dve.wait_ge(step, 8)
            dve.tensor_scalar(turns[:, :, :], angle[:, :, :], np.pi / 2, -TWO_PI, ALU.is_gt, ALU.mult).then_inc(step, 1)
            dve.wait_ge(step, 9)
            dve.scalar_tensor_tensor(out=turns[:, :, :], in0=angle[:, :, :], scalar=np.pi / 2, in1=turns[:, :, :],
                                     op0=ALU.add, op1=ALU.add).then_inc(step, 1)
            dve.wait_ge(step, 10)
            dve.tensor_scalar(turns[:, :, :], turns[:, :, :], -3.1415925, 3.1415925, ALU.max,
                              ALU.min).then_inc(shifted, 1)

        @block.scalar
        def _(act):
            act.wait_ge(shifted, 1)
            act.activation(table[:, :, 0, :], turns[:, :, :], ACT.Sin).then_inc(tables_made, 1)
            act.activation(table[:, :, 1, :], angle[:, :, :], ACT.Sin).then_inc(tables_made, 1)


class WeightSplitter:

    def __init__(self, nc, stack):
        self.nc, self.calls, self.before = nc, 0, 0
        sem = lambda name: stack.enter_context(nc.semaphore(name))
        self.w_in = [sem(f"w_in{j}") for j in range(2)]
        self.w_high, self.w_low = sem("w_high"), sem("w_low")

    def __call__(self, *jobs):
        nc, before = self.nc, self.before
        w_in, w_high, w_low = self.w_in, self.w_high, self.w_low
        pieces = []
        for src, high, low in jobs:
            n = src.shape[1]
            for c in range(0, n, 2048):
                pieces.append((src[:, c:min(n, c + 2048)], high[:, c:min(n, c + 2048)], low[:, c:min(n, c + 2048)]))
        with ExitStack() as ctx:
            stage = ctx.enter_context(nc.sbuf_tensor(f"w_stage{self.calls}", [P, 2, 2048], F32))
            block = ctx.enter_context(nc.Block())

            @block.sync
            def _(sp):
                for n, (src, _, _) in enumerate(pieces, before):
                    if n >= 2:
                        sp.wait_ge(w_low, n - 1)
                    sp.dma_start(stage[:, n % 2, 0:src.shape[1]], src).then_inc(w_in[n % 2], 16)

            @block.scalar
            def _(act):
                for n, (src, high, _) in enumerate(pieces, before):
                    act.wait_ge(w_in[n % 2], 16 * (n // 2 + 1))
                    act.activation(high, stage[:, n % 2, 0:src.shape[1]], ACT.Copy, scale=WSCALE).then_inc(w_high, 1)

            @block.vector
            def _(dve):
                for n, (src, high, low) in enumerate(pieces, before):
                    dve.wait_ge(w_high, n + 1)
                    dve.scalar_tensor_tensor(out=low, in0=stage[:, n % 2, 0:src.shape[1]], scalar=WSCALE, in1=high,
                                             op0=ALU.mult, op1=ALU.subtract).then_inc(w_low, 1)

        self.calls += 1
        self.before += len(pieces)


def attention0(nc, NT, x, ctxT, rope_dram, qnw, knw, g_xattn, wq, wk, wv, wo_dram, gate_dram, ident, x1, y1, logits):
    with ExitStack() as ctx:
        sb = lambda name, shape, dt=F32: ctx.enter_context(nc.sbuf_tensor(name, shape, dt))
        ps = lambda name, shape=[P, 512]: ctx.enter_context(nc.psum_tensor(name, shape, F32))
        sem = lambda name: ctx.enter_context(nc.semaphore("a0_" + name))

        wo = sb("wo0", [P, H0, D])
        gate = sb("gate0", [P, 2])
        tgate = sb("tgate0", [P, 1])
        half_neg = sb("half_neg0", [P, H0])
        qw = sb("qw0", [P, 2, HD0])
        kw = sb("kw0", [P, 2, HD0])
        xt = sb("xt0", [P, D])
        xres = sb("xres0", [P, D])
        xn = sb("xn0", [P, D])
        ctx32 = sb("ctx32", [P, DC, NB, S])
        raw = sb("raw0", [P, 3, 2, HALF])
        tab = sb("tab0", [P, 3, 2, 2, HALF])
        kv_hi = sb("kv_hi", [P, DC, 4, S], F16)
        kv_lo = sb("kv_lo", [P, DC, 4, S], F16)
        stats = sb("stats0", [P, 6])
        mv = sb("mv0", [P, 2])
        rstd = sb("rstd0", [P, 1])
        sq = sb("sq0", [P, 2, 512])
        ssk = sb("ssk", [P, NB * KV0])
        ssq = sb("ssq", [P, H0])
        rk = sb("rk", [P, NB * KV0])
        rq = sb("rq", [P, H0])
        rqT = sb("rqT", [P, NB, H0 // 2])
        k1 = sb("k1", [P, NB, KV0 * HD0])
        k2 = sb("k2", [P, NB, KV0 * HD0])
        q1 = sb("q1", [P, H0 * HD0])
        q2 = sb("q2", [P, H0 * HD0])
        qT = sb("qT0", [P, NB, H0, S])
        kT = sb("kT0", [P, NB, KV0, P])
        v = sb("v0", [P, NB, KV0 * HD0])
        E = sb("E0", [P, 2, 2, P])
        PT = sb("PT0", [P, 2, 2, P])
        mx = sb("mx0", [P, 2, 2])
        nb = sb("nb0", [P, 2, 2])
        es = sb("es0", [P, 2, 2])
        er = sb("er0", [P, 2, 2])
        attnT = sb("attnT0", [P, H0, NB, S])
        x1t = sb("x1t", [P, D])

        stats_y = sb("stats_y0", [P, 6])
        mv_y = sb("mv_y0", [P, 2])
        rstd_y = sb("rstd_y0", [P, 1])
        yn = sb("yn0", [P, D])
        ynT = sb("ynT0", [P, D])
        router = sb("router0", [P, DC, E0])
        eps_q = sb("eps_q", [P, H0])
        eps_ln = sb("eps_ln0", [P, 1])

        proj = [ps("proj0"), ps("proj1")]
        turnA = ps("turnA")
        score = [ps("score0"), ps("score1")]
        turnB = [ps("turnB0"), ps("turnB1")]
        outp = ps("outp0")

        x_in, ctx_in, raw_in, xres_in, x1_out, y1_out, const_in = map(sem, (
            "x_in", "ctx_in", "raw_in", "xres_in", "x1_out", "y1_out", "const_in"))
        pe_xT = sem("pe_xT")
        pe_proj = sem("pe_proj")
        pe_rq = sem("pe_rq")
        pe_score = sem("pe_score")
        pe_PT = sem("pe_PT")
        pe_out = sem("pe_out")
        pe_yT = sem("pe_yT")
        pe_gate = sem("pe_gate")
        dv_y = sem("dv_y")
        dv_gate = sem("dv_gate")
        dv_ln = sem("dv_ln")
        dv_stats = sem("dv_stats")
        dv_xlo = sem("dv_xlo")
        dv_rope = sem("dv_rope")
        dv_ss = sem("dv_ss")
        dv_max = sem("dv_max")
        dv_norm = sem("dv_norm")
        dv_x1 = sem("dv_x1")
        ac_xhi = sem("ac_xhi")
        ac_sq = sem("ac_sq")
        ac_v = sem("ac_v")
        ac_turn = sem("ac_turn")
        ac_rq = sem("ac_rq")
        ac_exp = sem("ac_exp")
        ac_PT = sem("ac_PT")
        ac_out = sem("ac_out")
        ac_yT = sem("ac_yT")
        po_y = sem("po_y")
        po_rstd = sem("po_rstd")
        po_clo = sem("po_clo")
        po_tab = sem("po_tab")
        po_add = sem("po_add")
        po_r = sem("po_r")
        po_const = sem("po_const")
        dv_const = sem("dv_const")
        ac_const = sem("ac_const")
        block = ctx.enter_context(nc.Block())

        @block.sync
        def _(sp):
            for dst, src in ((wo[:, :, :], wo_dram.rearrange("p (h d) -> p h d", h=H0)),
                             (router[:, :, :], gate_dram.rearrange("p (c e) -> p c e", c=DC)),
                             (gate[:, :], g_xattn.partition_broadcast(P)),
                             (qw[:, 0, :], qnw.partition_broadcast(P)), (kw[:, 0, :], knw.partition_broadcast(P)),
                             (qw[:, 1, 0:HALF], qnw[HALF:].partition_broadcast(P)),
                             (qw[:, 1, HALF:], qnw[0:HALF].partition_broadcast(P)),
                             (kw[:, 1, 0:HALF], knw[HALF:].partition_broadcast(P)),
                             (kw[:, 1, HALF:], knw[0:HALF].partition_broadcast(P))):
                sp.dma_start(dst, src).then_inc(const_in, 16)
            for s in (x_in, ctx_in, raw_in, xres_in, x1_out, y1_out):
                sp.sem_inc(s, 16)

            def load(t):
                sp.wait_ge(dv_ln, last(2, t, 2))
                sp.dma_start(xt[:, :], x[bass.ds(t * P, P), :]).then_inc(x_in, 16)
                sp.wait_ge(po_clo, last(1, t, 1))
                sp.dma_start(ctx32[:, :, :, :], ctxT[:, bass.ds(t * D, D)]
                             .rearrange("p (c b s) -> p c b s", c=DC, b=NB)).then_inc(ctx_in, 16)
                sp.wait_ge(po_tab, last(6, t, 6))
                r = rope_dram[bass.ds(t * P, P), :].rearrange("(b s) (o a d) -> b s o a d", b=NB, o=2, a=2)
                for h in range(NB):
                    sp.dma_start(raw[h * S:(h + 1) * S, 0, :, :], r[h, :, 0, :, :]).then_inc(raw_in, 16)
                    context, own = (slice(0, S), slice(S, P))[::1 - 2 * h]
                    sp.dma_start(raw[context, 1 + h, :, :], r[h, :, 1, :, :]).then_inc(raw_in, 16)
                    sp.dma_start(raw[own, 1 + h, :, :], r[h, :, 0, :, :]).then_inc(raw_in, 16)

            def load_res(p):
                sp.wait_ge(dv_x1, last(1, p, 1))
                sp.dma_start(xres[:, :], x[bass.ds(p * P, P), :]).then_inc(xres_in, 16)

            load(0)
            with sp.Fori(0, NT - 1) as p:
                load(p + 1)
                load_res(p)
            load_res(NT - 1)

        @block.gpsimd
        def _(pool):
            pool.memset(half_neg[:, :], -0.5).then_inc(po_const, 1)
            pool.memset(eps_q[:, :], EPS_RMS * WSCALE**2 * HD0).then_inc(po_const, 1)
            pool.memset(eps_ln[:, :], EPS_LN).then_inc(po_const, 1)
            for s, n in ((po_y, 2), (po_rstd, 2), (po_clo, 1), (po_tab, 6), (po_add, 8), (po_r, 6)):
                pool.sem_inc(s, n)
            pool.wait_ge(po_const, 3)

            def part_a(t):
                pool.wait_ge(dv_ln, this(2, t, 1))
                pool.tensor_tensor(rstd[:, :], mv[:, 1:2], eps_ln[:, :], ALU.add).then_inc(po_rstd, 1)
                pool.wait_ge(po_rstd, this(2, t, 1))
                pool.tensor_tensor(rstd[:, :], rstd[:, :], half_neg[:, 0:1], ALU.pow).then_inc(po_rstd, 1)
                pool.wait_ge(ac_xhi, this(2, t, 1))
                pool.wait_ge(ctx_in, this(16, t, 16))
                pool.tensor_tensor(kv_lo[:, :, 0::3, :], ctx32[:, :, :, :], kv_hi[:, :, 0::3, :],
                                   ALU.subtract).then_inc(po_clo, 1)
                pool.wait_ge(raw_in, 96 * t + 16 + 96)
                pool.wait_ge(dv_rope, last(6, t, 6))
                for n in range(3):
                    w = qw if n == 0 else kw
                    pool.tensor_tensor(tab[:, n, 0, :, :], raw[:, n, 0:1, :].broadcast_to([P, 2, HALF]),
                                       w[:, 0, :].rearrange("p (a d) -> p a d", a=2), ALU.mult).then_inc(po_tab, 1)
                    pool.tensor_tensor(tab[:, n, 1, :, :], raw[:, n, 1:2, :].broadcast_to([P, 2, HALF]),
                                       w[:, 1, :].rearrange("p (a d) -> p a d", a=2), ALU.mult).then_inc(po_tab, 1)
                for b in range(NB):
                    pool.wait_ge(dv_rope, this(6, t, b + 1))
                    pool.tensor_tensor(k1[:, b, :], k1[:, b, :], k2[:, b, :], ALU.add).then_inc(po_add, 1)
                    pool.wait_ge(dv_ss, this(6, t, b + 1))
                    part = slice(b * KV0, (b + 1) * KV0)
                    pool.tensor_tensor(rk[:, part], ssk[:, part], eps_q[:, 0:KV0], ALU.add).then_inc(po_r, 1)
                    pool.wait_ge(po_r, this(6, t, 2 * b + 1))
                    pool.tensor_tensor(rk[:, part], rk[:, part], half_neg[:, 0:KV0], ALU.pow).then_inc(po_r, 1)
                    pool.wait_ge(po_r, this(6, t, 2 * b + 2))
                    pool.wait_ge(po_add, this(8, t, 2 * b + 1))
                    kb = k1[:, b, :].rearrange("p (h d) -> p h d", h=KV0)
                    r = rk[:, part].unsqueeze(2).broadcast_to([P, KV0, HD0])
                    pool.tensor_tensor(kb, kb, r, ALU.mult).then_inc(po_add, 1)
                for j in range(4):
                    pool.wait_ge(dv_rope, this(6, t, 3 + j))
                    part = slice(512 * j, 512 * (j + 1))
                    pool.tensor_tensor(q1[:, part], q1[:, part], q2[:, part], ALU.add).then_inc(po_add, 1)
                pool.wait_ge(dv_ss, this(6, t, 6))
                pool.tensor_tensor(rq[:, :], ssq[:, :], eps_q[:, :], ALU.add).then_inc(po_r, 1)
                pool.wait_ge(po_r, this(6, t, 5))
                pool.tensor_tensor(rq[:, :], rq[:, :], half_neg[:, :], ALU.pow).then_inc(po_r, 1)

            def part_b(p):
                pool.wait_ge(dv_y, this(2, p, 1))
                pool.tensor_tensor(rstd_y[:, :], mv_y[:, 1:2], eps_ln[:, :], ALU.add).then_inc(po_y, 1)
                pool.wait_ge(po_y, this(2, p, 1))
                pool.tensor_tensor(rstd_y[:, :], rstd_y[:, :], half_neg[:, 0:1], ALU.pow).then_inc(po_y, 1)

            pool.wait_ge(const_in, 16 * 9)
            for w in (qw, kw):
                pool.tensor_scalar(w[:, 1, 0:HALF], w[:, 1, 0:HALF], -1.0, None, ALU.mult).then_inc(po_const, 1)
            pool.wait_ge(po_const, 5)
            part_a(0)
            with pool.Fori(0, NT - 1) as p:
                part_a(p + 1)
                part_b(p)
            part_b(NT - 1)

        @block.tensor
        def _(pe):
            for s, n in ((pe_xT, 1), (pe_proj, 14), (pe_rq, 1), (pe_score, 8), (pe_PT, 8), (pe_out, 9), (pe_yT, 1), (pe_gate, 1)):
                pe.sem_inc(s, n)
            pe.wait_ge(const_in, 16 * 9)

            def x_turn(t):
                pe.wait_ge(dv_ln, this(2, t, 2))
                pe.wait_ge(ac_rq, last(1, t, 1))
                for c in range(DC):
                    i = pe.transpose(turnA[:, c * P:(c + 1) * P], xn[:, c * P:(c + 1) * P], ident[:, :])
                i.then_inc(pe_xT, 1)

            def mm3(out, left, right):
                steps = [(c, a, b) for c in range(DC) for a, b in ((0, 0), (0, 1), (1, 0))]
                for n, (c, a, b) in enumerate(steps):
                    i = pe.matmul(out, left(c, a), right(c, b), start=(n == 0), stop=(n == len(steps) - 1))
                return i

            kv = (kv_hi, kv_lo)

            def block_k(t, b):
                if b == 0:
                    pe.wait_ge(po_clo, this(1, t, 1))
                    pe.wait_ge(dv_xlo, this(1, t, 1))
                    pe.wait_ge(ac_xhi, this(2, t, 2))
                pe.wait_ge(ac_turn, last(6, t, 5 + b))
                mm3(proj[b][:, :], lambda c, a: kv[a][:, c, 2 * b:2 * b + 2, :], lambda c, a: wk[a][:, c * 512:(c + 1) * 512]
                    ).then_inc(pe_proj, 1)

            def block_q(t, j):
                pe.wait_ge(dv_rope, this(6, t, j + 1))
                pe.wait_ge(ac_sq, this(6, t, j + 1))
                mm3(proj[j % 2][:, :], lambda c, a: kv[a][:, c, 1:3, :],
                    lambda c, a: wq[a][:, c * 2048 + j * 512:c * 2048 + (j + 1) * 512]).then_inc(pe_proj, 1)

            def block_v(t, b):
                pe.wait_ge(dv_rope, this(6, t, 5 + b))
                pe.wait_ge(ac_sq, this(6, t, 5 + b))
                mm3(proj[b][:, :], lambda c, a: kv[a][:, c, 2 * b:2 * b + 2, :], lambda c, a: wv[a][:, c * 512:(c + 1) * 512]
                    ).then_inc(pe_proj, 1)

            def turn_k(t, b):
                pe.wait_ge(po_add, this(8, t, 2 * b + 2))
                pe.wait_ge(ac_v, this(2, t, b + 1))
                for g in range(KV0):
                    i = pe.transpose(proj[b][:, g * P:(g + 1) * P], k1[:, b, g * HD0:(g + 1) * HD0], ident[:, :])
                i.then_inc(pe_proj, 1)

            def turn_q(t, j):
                pe.wait_ge(po_add, this(8, t, 5 + j))
                pe.wait_ge(ac_turn, this(6, t, j + 1))
                for g in range(4):
                    h = 4 * j + g
                    i = pe.transpose(proj[j % 2][:, g * P:(g + 1) * P], q1[:, h * HD0:(h + 1) * HD0], ident[:, :])
                i.then_inc(pe_proj, 1)

            def move_rq(t, c):
                pe.wait_ge(po_r, this(6, t, 6))
                if c is not None:
                    pe.wait_ge(dv_gate, this(1, c, 1))
                pe.wait_ge(dv_xlo, this(1, t, 1))
                pe.wait_ge(ac_xhi, this(2, t, 2))
                r = rq[:, :].rearrange("p (m j) -> p j m", j=2)
                for j in range(2):
                    for b in range(NB):
                        i = pe.matmul(turnA[j * S:(j + 1) * S, b * 8:(b + 1) * 8], ident[:, b * S:(b + 1) * S],
                                      r[:, j, :], start=True, stop=True)
                i.then_inc(pe_rq, 1)

            def scores(p, u):
                b, g = divmod(u, KV0)
                if u == 0:
                    pe.wait_ge(ac_turn, this(6, p, 6))
                pe.wait_ge(ac_exp, this(8, p, u - 1) if u >= 2 else last(8, p, 7 + u))
                for m in range(2):
                    h = GROUP * g + 2 * m
                    i = pe.matmul(score[u % 2][:, m * P:(m + 1) * P], qT[:, b, h:h + 2, :], kT[:, b, g, :],
                                  start=True, stop=True)
                i.then_inc(pe_score, 1)

            def turn_P(p, u):
                pe.wait_ge(dv_norm, this(16, p, 2 * u + 2))
                pe.wait_ge(ac_PT, this(8, p, u - 1) if u >= 2 else last(8, p, 7 + u))
                for m in range(2):
                    i = pe.transpose(turnB[u % 2][:, m * P:(m + 1) * P], E[:, u % 2, m, :], ident[:, :])
                i.then_inc(pe_PT, 1)

            def weigh_v(p, u):
                b, g = divmod(u, KV0)
                pe.wait_ge(ac_PT, this(8, p, u + 1))
                if u == 0:
                    pe.wait_ge(dv_x1, last(1, p, 1))
                    pe.wait_ge(ac_v, this(2, p, 2))
                else:
                    pe.wait_ge(ac_out, this(8, p, u))
                pe.matmul(outp[:, 0:256], v[:, b, g * HD0:(g + 1) * HD0], PT[:, u % 2, :, :], start=True,
                          stop=True).then_inc(pe_out, 1)

            def out_projection(p):
                pe.wait_ge(ac_out, this(8, p, 8))
                for h in range(H0):
                    i = pe.matmul(outp[:, 0:D], attnT[:, h, :, :], wo[:, h, :], start=(h == 0), stop=(h == H0 - 1))
                i.then_inc(pe_out, 1)

            def y_turn(c, t):
                pe.wait_ge(dv_y, this(2, c, 2))
                if t is not None:
                    pe.wait_ge(dv_xlo, this(1, t, 1))
                for k in range(DC):
                    i = pe.transpose(turnA[:, k * P:(k + 1) * P], yn[:, k * P:(k + 1) * P], ident[:, :])
                i.then_inc(pe_yT, 1)

            def route(c):
                pe.wait_ge(ac_yT, this(1, c, 1))
                for k in range(DC):
                    i = pe.matmul(turnA[:, 0:E0], ynT[:, k * P:(k + 1) * P], router[:, k, :], start=(k == 0),
                                  stop=(k == DC - 1))
                i.then_inc(pe_gate, 1)

            def iteration(t, p, c):
                if p is not None:
                    scores(p, 0)
                    scores(p, 1)
                if t is not None:
                    x_turn(t)
                for u in range(8):
                    if t is not None and u < 2:
                        block_k(t, u)
                    elif t is not None and u < 6:
                        block_q(t, u - 2)
                    if p is not None:
                        if u + 2 < 8:
                            scores(p, u + 2)
                        turn_P(p, u)
                        weigh_v(p, u)
                    if c is not None and u == 3:
                        y_turn(c, t)
                    if c is not None and u == 5:
                        route(c)
                if t is not None:
                    block_v(t, 0)
                    block_v(t, 1)
                if p is not None:
                    out_projection(p)
                if t is not None:
                    turn_k(t, 0)
                    turn_k(t, 1)
                    move_rq(t, c)
                    for j in range(4):
                        turn_q(t, j)

            iteration(0, None, None)
            iteration(1, 0, None)
            with pe.Fori(0, NT - 2) as c:
                iteration(c + 2, c + 1, c)
            iteration(None, NT - 1, NT - 2)
            iteration(None, None, NT - 1)

        @block.vector
        def _(dve):
            for s, n in ((dv_ln, 2), (dv_xlo, 1), (dv_rope, 6), (dv_ss, 6), (dv_max, 16), (dv_norm, 16), (dv_x1, 1), (dv_y, 2), (dv_gate, 1)):
                dve.sem_inc(s, n)

            def layernorm(t):
                dve.sem_clear(dv_stats)
                dve.wait_ge(x_in, this(16, t, 16))
                dve.bn_stats(stats[:, :], xt[:, :]).then_inc(dv_stats, 1)
                dve.wait_ge(dv_stats, 1)
                dve.bn_aggr(mv[:, :], stats[:, :]).then_inc(dv_ln, 1)
                dve.wait_ge(po_rstd, this(2, t, 2))
                dve.wait_ge(pe_xT, last(1, t, 1))
                dve.tensor_scalar(xn[:, :], xt[:, :], mv[:, 0:1], rstd[:, 0:1], ALU.subtract,
                                  ALU.mult).then_inc(dv_ln, 1)

            def low_x(t):
                dve.wait_ge(ac_xhi, this(2, t, 2))
                dve.tensor_tensor(kv_lo[:, :, 1:3, :], turnA[:, 0:D].rearrange("p (c b s) -> p c b s", c=DC, b=NB),
                                  kv_hi[:, :, 1:3, :], ALU.subtract).then_inc(dv_xlo, 1)

            def rope(t, n):
                dve.wait_ge(pe_proj, this(14, t, n + 1))
                if n == 0:
                    dve.wait_ge(po_tab, this(6, t, 6))
                    dve.wait_ge(pe_proj, last(14, t, 14))
                which = 0 if n >= 2 else 1 + n
                if n < 2:
                    o1, o2, ss = k1[:, n, :], k2[:, n, :], ssk[:, n * KV0:(n + 1) * KV0]
                else:
                    part = slice(512 * (n - 2), 512 * (n - 1))
                    o1, o2, ss = q1[:, part], q2[:, part], ssq[:, 4 * (n - 2):4 * (n - 1)]
                y = proj[n % 2][:, :].rearrange("p (h a d) -> p h a d", a=2, d=HALF)
                shape = [P, 4, 2, HALF]
                cos, sin = (tab[:, which, s:s + 1, :, :].broadcast_to(shape) for s in range(2))
                dve.tensor_tensor(o1.rearrange("p (h a d) -> p h a d", a=2, d=HALF), y, cos, ALU.mult)
                dve.tensor_tensor(o2.rearrange("p (h a d) -> p h a d", a=2, d=HALF), y[:, :, ::-1, :], sin,
                                  ALU.mult).then_inc(dv_rope, 1)
                dve.wait_ge(ac_sq, this(6, t, n + 1))
                if n == 2:
                    dve.wait_ge(po_r, last(6, t, 6))
                dve.tensor_reduce(ss, sq[:, n % 2, :].rearrange("p (h d) -> p h d", h=4), AX_X,
                                  ALU.add).then_inc(dv_ss, 1)

            def maximum(p, u):
                b, g = divmod(u, KV0)
                dve.wait_ge(pe_score, this(8, p, u + 1))
                dve.tensor_reduce(mx[:, u % 2, :], score[u % 2][:, 0:256].rearrange("p (m k) -> p m k", m=2), AX_X,
                                  ALU.max).then_inc(dv_max, 1)
                dve.wait_ge(dv_max, this(16, p, 2 * u + 1))
                if u == 0:
                    dve.wait_ge(ac_rq, this(1, p, 1))
                dve.wait_ge(ac_exp, this(8, p, u - 1) if u >= 2 else last(8, p, 7 + u))
                dve.scalar_tensor_tensor(out=nb[:, u % 2, :], in0=mx[:, u % 2, :], scalar=-1.0,
                                         in1=rqT[:, b, 2 * g:2 * g + 2], op0=ALU.mult,
                                         op1=ALU.mult).then_inc(dv_max, 1)

            def normalize(p, u):
                dve.wait_ge(ac_exp, this(8, p, u + 1))
                dve.reciprocal(er[:, u % 2, :], es[:, u % 2, :]).then_inc(dv_norm, 1)
                dve.wait_ge(dv_norm, this(16, p, 2 * u + 1))
                dve.tensor_tensor(E[:, u % 2, :, :], E[:, u % 2, :, :],
                                  er[:, u % 2, :].unsqueeze(2).broadcast_to([P, 2, P]), ALU.mult).then_inc(dv_norm, 1)

            def residual(p):
                dve.wait_ge(pe_out, this(9, p, 9))
                dve.wait_ge(xres_in, this(16, p, 16))
                dve.wait_ge(x1_out, last(16, p, 16))
                dve.scalar_tensor_tensor(out=x1t[:, :], in0=outp[:, 0:D], scalar=tgate[:, 0:1], in1=xres[:, :],
                                         op0=ALU.mult, op1=ALU.add).then_inc(dv_x1, 1)
                dve.sem_clear(dv_stats)
                dve.wait_ge(dv_x1, this(1, p, 1))
                dve.bn_stats(stats_y[:, :], x1t[:, :]).then_inc(dv_stats, 1)
                dve.wait_ge(dv_stats, 1)
                dve.bn_aggr(mv_y[:, :], stats_y[:, :]).then_inc(dv_y, 1)
                dve.wait_ge(po_y, this(2, p, 2))
                dve.wait_ge(pe_yT, last(1, p, 1))
                dve.wait_ge(y1_out, last(16, p, 16))
                dve.tensor_scalar(yn[:, :], x1t[:, :], mv_y[:, 0:1], rstd_y[:, 0:1], ALU.subtract,
                                  ALU.mult).then_inc(dv_y, 1)

            def keep_logits(c):
                dve.wait_ge(pe_gate, this(1, c, 1))
                dve.tensor_scalar(logits[:, bass.ds(c * E0, E0)], turnA[:, 0:E0], 1.0, None,
                                  ALU.mult).then_inc(dv_gate, 1)

            def iteration(t, p, c):
                if p is not None:
                    maximum(p, 0)
                    maximum(p, 1)
                if t is not None:
                    layernorm(t)
                    low_x(t)
                for u in range(8):
                    if p is not None:
                        normalize(p, u)
                    if t is not None and u < 6:
                        rope(t, u)
                    if p is not None and u + 2 < 8:
                        maximum(p, u + 2)
                if c is not None:
                    keep_logits(c)
                if p is not None:
                    residual(p)

            dve.wait_ge(ac_const, 1)
            iteration(0, None, None)
            iteration(1, 0, None)
            with dve.Fori(0, NT - 2) as c:
                iteration(c + 2, c + 1, c)
            iteration(None, NT - 1, NT - 2)
            iteration(None, None, NT - 1)

        @block.scalar
        def _(act):
            for s, n in ((ac_xhi, 2), (ac_sq, 6), (ac_v, 2), (ac_turn, 6), (ac_rq, 1), (ac_exp, 8), (ac_PT, 8),
                         (ac_out, 8), (ac_yT, 1)):
                act.sem_inc(s, n)
            act.wait_ge(const_in, 16 * 9)
            act.activation(tgate[:, :], gate[:, 0:1], ACT.Tanh).then_inc(ac_const, 1)

            def high_context(t):
                act.wait_ge(ctx_in, this(16, t, 16))
                act.wait_ge(pe_proj, last(14, t, 8))
                act.activation(kv_hi[:, :, 0::3, :], ctx32[:, :, :, :], ACT.Copy).then_inc(ac_xhi, 1)

            def high_x(t):
                act.wait_ge(pe_xT, this(1, t, 1))
                act.activation(kv_hi[:, :, 1:3, :], turnA[:, 0:D].rearrange("p (c b s) -> p c b s", c=DC, b=NB),
                               ACT.Copy).then_inc(ac_xhi, 1)

            def squares(t, n):
                act.wait_ge(pe_proj, this(14, t, n + 1))
                act.wait_ge(dv_rope, this(6, t, n + 1))
                act.wait_ge(dv_ss, this(6, t, n - 1) if n >= 2 else last(6, t, 5 + n))
                act.activation(sq[:, n % 2, :], proj[n % 2][:, :], ACT.Square).then_inc(ac_sq, 1)

            def values(t, b):
                act.wait_ge(pe_proj, this(14, t, 7 + b))
                act.activation(v[:, b, :], proj[b][:, :], ACT.Copy, scale=1.0 / WSCALE).then_inc(ac_v, 1)

            def turned_k(t, b):
                act.wait_ge(pe_proj, this(14, t, 9 + b))
                act.activation(kT[:, b, :, :], proj[b][:, :].rearrange("p (g k) -> p g k", g=KV0),
                               ACT.Copy).then_inc(ac_turn, 1)

            def turned_q(t, j):
                act.wait_ge(pe_proj, this(14, t, 11 + j))
                act.activation(qT[:, :, 4 * j:4 * j + 4, :].rearrange("p b h s -> p h b s"),
                               proj[j % 2][:, :].rearrange("p (h b s) -> p h b s", h=4, b=NB),
                               ACT.Copy).then_inc(ac_turn, 1)

            def moved_rq(t):
                act.wait_ge(pe_rq, this(1, t, 1))
                act.activation(rqT[:, :, :], turnA[:, 0:16].rearrange("p (b m) -> p b m", b=NB),
                               ACT.Copy, scale=HD0**0.5).then_inc(ac_rq, 1)

            def exponentials(p, u):
                b, g = divmod(u, KV0)
                act.wait_ge(dv_max, this(16, p, 2 * u + 2))
                act.wait_ge(pe_PT, this(8, p, u - 1) if u >= 2 else last(8, p, 7 + u))
                for m in range(2):
                    i = act.activation(E[:, u % 2, m, :], score[u % 2][:, m * P:(m + 1) * P], ACT.Exp,
                                       bias=nb[:, u % 2, m:m + 1], scale=rqT[:, b, 2 * g + m:2 * g + m + 1],
                                       accum_out=es[:, u % 2, m:m + 1])
                i.then_inc(ac_exp, 1)

            def turned_P(p, u):
                act.wait_ge(pe_PT, this(8, p, u + 1))
                act.wait_ge(pe_out, this(9, p, u - 1) if u >= 2 else last(9, p, 7 + u))
                act.activation(PT[:, u % 2, :, :], turnB[u % 2][:, 0:256].rearrange("p (m q) -> p m q", m=2),
                               ACT.Copy).then_inc(ac_PT, 1)

            def turned_out(p, u):
                b, g = divmod(u, KV0)
                act.wait_ge(pe_out, this(9, p, u + 1))
                act.activation(attnT[:, GROUP * g:GROUP * (g + 1), b, :],
                               outp[:, 0:256].rearrange("p (h s) -> p h s", h=GROUP), ACT.Copy).then_inc(ac_out, 1)

            def store(p):
                act.wait_ge(dv_x1, this(1, p, 1))
                act.dma_start(x1[bass.ds(p * P, P), :], x1t[:, :]).then_inc(x1_out, 16)
                act.wait_ge(dv_y, this(2, p, 2))
                act.dma_start(y1[bass.ds(p * P, P), :], yn[:, :]).then_inc(y1_out, 16)

            def turned_y(c):
                act.wait_ge(pe_yT, this(1, c, 1))
                act.wait_ge(pe_gate, last(1, c, 1))
                act.activation(ynT[:, :], turnA[:, 0:D], ACT.Copy).then_inc(ac_yT, 1)

            def iteration(t, p, c):
                if p is not None:
                    exponentials(p, 0)
                    exponentials(p, 1)
                if t is not None:
                    high_context(t)
                    high_x(t)
                for u in range(8):
                    if p is not None:
                        turned_P(p, u)
                    if t is not None and u < 6:
                        squares(t, u)
                    if p is not None:
                        turned_out(p, u)
                        if u + 2 < 8:
                            exponentials(p, u + 2)
                    if c is not None and u == 3:
                        turned_y(c)
                if t is not None:
                    values(t, 0)
                    values(t, 1)
                    turned_k(t, 0)
                    turned_k(t, 1)
                    moved_rq(t)
                    for j in range(4):
                        turned_q(t, j)
                if p is not None:
                    store(p)

            iteration(0, None, None)
            iteration(1, 0, None)
            with act.Fori(0, NT - 2) as c:
                iteration(c + 2, c + 1, c)
            iteration(None, NT - 1, NT - 2)
            iteration(None, None, NT - 1)
            act.wait_ge(x1_out, 16 * (NT + 1))
            act.wait_ge(y1_out, 16 * (NT + 1))


class Chain:

    def __init__(self, engine, semaphore):
        self.engine, self.semaphore, self.steps = engine, semaphore, 0

    def __call__(self, instruction):
        self.steps += 1
        instruction.then_inc(self.semaphore, 1)
        self.engine.wait_ge(self.semaphore, self.steps)


def top2(dve, chain, values, order, hot, best, t, m):
    shape = list(values.shape)
    wide = lambda y: y.unsqueeze(2).broadcast_to(shape)
    for slot in range(2):
        chain(dve.tensor_reduce(best[:, slot, :], values, AX_X, ALU.max))
        chain(dve.tensor_tensor(t, values, wide(best[:, slot, :]), ALU.is_equal))
        chain(dve.tensor_tensor(t, t, order, ALU.mult))
        chain(dve.tensor_reduce(m, t, AX_X, ALU.max))
        chain(dve.tensor_tensor(hot[:, slot, :, :], t, wide(m), ALU.is_equal))
        if slot == 0:
            chain(dve.scalar_tensor_tensor(out=values, in0=hot[:, 0, :, :], scalar=-1e30, in1=values, op0=ALU.mult,
                                           op1=ALU.add))


def route0(nc, NT, J, logits, consts, dest, weight, expert, index):
    B = 2 * NT
    with ExitStack() as ctx:
        sb = lambda name, shape, dt=F32: ctx.enter_context(nc.sbuf_tensor(name, shape, dt))
        sem = lambda name: ctx.enter_context(nc.semaphore("r0_" + name))
        hot = sb("r0_hot", [P, 2, NT, E0])
        hot16 = sb("r0_hot16", [P, B * E0], F16)
        best = sb("r0_best", [P, 2, NT])
        t = sb("r0_t", [P, NT, E0])
        m = sb("r0_m", [P, NT])
        diff = sb("r0_diff", [P, NT])
        zero = sb("r0_zero", [P, B])
        upto = sb("r0_upto", [P, E0, B])
        row = sb("r0_row", [P, B, E0])
        tiles = sb("r0_tiles", [P, E0])
        end = sb("r0_end", [P, E0])
        base = sb("r0_base", [P, E0])
        behind = sb("r0_behind", [P, J, E0])
        expf = sb("r0_expf", [P, J])
        rowf = sb("r0_rowf", [P, B])
        tile_of = sb("r0_tile_of", [P, B])
        place_of = sb("r0_place_of", [P, B])
        here = sb("r0_here", [P, 2, 4, P])
        token = sb("r0_token", [P, 2, 4, J])
        rank = ctx.enter_context(nc.psum_tensor("r0_rank", [P, B * E0], F32))
        total = ctx.enter_context(nc.psum_tensor("r0_total", [P, B * E0], F32))
        table = ctx.enter_context(nc.psum_tensor("r0_table", [P, 512], F32))
        dv_step, dv_hot, dv_diff, ac_exp, pe_count, dv_dest, dv_pick, pe_pick = map(sem, (
            "dv_step", "dv_hot", "dv_diff", "ac_exp", "pe_count", "dv_dest", "dv_pick", "pe_pick"))
        block = ctx.enter_context(nc.Block())
        order = consts["order"][:, 0:E0].unsqueeze(1).broadcast_to([P, NT, E0])

        @block.vector
        def _(dve):
            chain = Chain(dve, dv_step)
            values = logits[:, :].rearrange("p (t e) -> p t e", e=E0)
            top2(dve, chain, values, order, hot, best, t[:, :, :], m[:, :])
            dve.tensor_copy(hot16[:, :], hot[:, :, :, :].rearrange("p k t e -> p (k t e)")).then_inc(dv_hot, 1)
            dve.tensor_tensor(diff[:, :], best[:, 1, :], best[:, 0, :], ALU.subtract).then_inc(dv_diff, 1)
            dve.wait_ge(ac_exp, 1)
            chain(dve.tensor_scalar(m[:, :], diff[:, :], 1.0, None, ALU.add))
            chain(dve.reciprocal(weight[:, 0, :], m[:, :]))
            chain(dve.tensor_tensor(weight[:, 1, :], weight[:, 0, :], diff[:, :], ALU.mult))
            chain(dve.memset(zero[:, :], 0.0))
            dve.wait_ge(pe_count, 2)
            counts = total[:, :].rearrange("p (b e) -> p e b", e=E0)
            for e in range(E0):
                i = dve.tensor_tensor_scan(upto[:, e, :], counts[:, e, :], zero[:, :], 0.0, ALU.add, ALU.add)
            chain(i)
            chain(dve.tensor_scalar(tiles[:, :], upto[:, :, B - 1], 1.0 / P, (P - 1) / P - 0.5 + 0.5 / P, ALU.mult,
                                    ALU.add))
            chain(dve.tensor_scalar(tiles[:, :], tiles[:, :], ROUND, -ROUND, ALU.add, ALU.add))
            chain(dve.tensor_tensor_scan(end[:, :], tiles[:, :], zero[:, 0:E0], 0.0, ALU.add, ALU.add))
            chain(dve.tensor_tensor(base[:, :], end[:, :], tiles[:, :], ALU.subtract))
            chain(dve.tensor_scalar(base[:, :], base[:, :], float(P), None, ALU.mult))
            chain(dve.tensor_tensor(row[:, :, :], upto[:, :, :].rearrange("p e b -> p b e"),
                                    total[:, :].rearrange("p (b e) -> p b e", e=E0), ALU.subtract))
            chain(dve.tensor_tensor(row[:, :, :], row[:, :, :], rank[:, :].rearrange("p (b e) -> p b e", e=E0), ALU.add))
            chain(dve.tensor_tensor(row[:, :, :], row[:, :, :], base[:, :].unsqueeze(1).broadcast_to([P, B, E0]),
                                    ALU.add))
            chain(dve.tensor_tensor(row[:, :, :], row[:, :, :], hot[:, :, :, :].rearrange("p k t e -> p (k t) e"),
                                    ALU.mult))
            chain(dve.tensor_reduce(rowf[:, :], row[:, :, :], AX_X, ALU.add))
            chain(dve.tensor_copy(dest[:, :, :].rearrange("p k t -> p (k t)"), rowf[:, :]))
            chain(dve.tensor_tensor(behind[:, :, :], end[:, :].unsqueeze(1).broadcast_to([P, J, E0]),
                                    consts["count"][:, 0:J].unsqueeze(2).broadcast_to([P, J, E0]), ALU.is_le))
            chain(dve.tensor_reduce(expf[:, :], behind[:, :, :], AX_X, ALU.add))
            chain(dve.tensor_scalar(expf[:, :], expf[:, :], E0 - 1.0, None, ALU.min))
            chain(dve.tensor_copy(expert[:, :], expf[:, :]))
            chain(dve.tensor_scalar(tile_of[:, :], rowf[:, :], 1.0 / P, -0.5 + 0.5 / P, ALU.mult, ALU.add))
            chain(dve.tensor_scalar(tile_of[:, :], tile_of[:, :], ROUND, -ROUND, ALU.add, ALU.add))
            chain(dve.scalar_tensor_tensor(out=place_of[:, :], in0=tile_of[:, :], scalar=-float(P), in1=rowf[:, :],
                                           op0=ALU.mult, op1=ALU.add))
            dve.sem_inc(dv_pick, 2)
            dve.sem_inc(dv_dest, 1)
            with dve.Fori(0, B // 8) as r2:
                for k in range(2):
                    r = r2 * 2 + k
                    part = bass.ds(r * 4, 4)
                    dve.wait_ge(pe_pick, r2 * 2 + 1 + k)
                    dve.tensor_tensor(here[:, k, :, :], consts["count"][:, 0:P].unsqueeze(1).broadcast_to([P, 4, P]),
                                      place_of[:, part].unsqueeze(2).broadcast_to([P, 4, P]),
                                      ALU.is_equal).then_inc(dv_pick, 1)
                    dve.tensor_tensor(token[:, k, :, :], consts["count"][:, 0:J].unsqueeze(1).broadcast_to([P, 4, J]),
                                      tile_of[:, part].unsqueeze(2).broadcast_to([P, 4, J]),
                                      ALU.is_equal).then_inc(dv_dest, 1)
                    dve.wait_ge(dv_dest, r2 * 2 + 2 + k)
                    dve.tensor_tensor(token[:, k, :, :], token[:, k, :, :],
                                      consts["token"][:, part].unsqueeze(2).broadcast_to([P, 4, J]),
                                      ALU.mult).then_inc(dv_pick, 1)
            dve.wait_ge(pe_pick, B // 4 + 2)
            chain(dve.tensor_copy(index[:, :], table[:, 0:J]))

        @block.scalar
        def _(act):
            act.wait_ge(dv_diff, 1)
            act.activation(diff[:, :], diff[:, :], ACT.Exp).then_inc(ac_exp, 1)

        @block.tensor
        def _(pe):
            pe.wait_ge(dv_hot, 1)
            pe.matmul(rank[:, :], consts["before"][:, :], hot16[:, :], start=True, stop=True).then_inc(pe_count, 1)
            pe.matmul(total[:, :], consts["ones"][:, :], hot16[:, :], start=True, stop=True).then_inc(pe_count, 1)
            pe.sem_inc(pe_pick, 2)

            def pick(r2, k, first, final):
                pe.wait_ge(dv_pick, (r2 * 2 + k) * 2 + 4)
                for q in range(4):
                    i = pe.matmul(table[:, 0:J], here[:, k, q, :], token[:, k, q, :], start=first and q == 0,
                                  stop=final and q == 3)
                i.then_inc(pe_pick, 1)

            pick(0, 0, True, False)
            pick(0, 1, False, B // 8 == 1)
            if B // 8 > 2:
                with pe.Fori(1, B // 8 - 1) as r2:
                    pick(r2, 0, False, False)
                    pick(r2, 1, False, False)
            if B // 8 > 1:
                pick(B // 8 - 1, 0, False, False)
                pick(B // 8 - 1, 1, False, True)


def experts0(nc, NT, J, y1, w0, w1, wo, expert, index, ident, out):
    with ExitStack() as ctx:
        sb = lambda name, shape, dt=F32: ctx.enter_context(nc.sbuf_tensor(name, shape, dt))
        ps = lambda name: ctx.enter_context(nc.psum_tensor(name, [P, 512], F32))
        sem = lambda name: ctx.enter_context(nc.semaphore("e0_" + name))
        now = sb("e0_now", [P, 2], I32)
        rows = sb("e0_rows", [P, 2, D])
        xT = [sb(f"e0_xT{h}", [P, 2, D], F16) for h in ("hi", "lo")]
        silu = sb("e0_silu", [P, 2, F0])
        inter = sb("e0_inter", [P, 2, F0])
        iT = [sb(f"e0_iT{h}", [P, 2, F0], F16) for h in ("hi", "lo")]
        result = sb("e0_result", [P, 2, D])
        turn_x = ps("e0_turn_x")
        up0 = [ps(f"e0_up0{k}") for k in range(2)]
        up1 = [ps(f"e0_up1{k}") for k in range(2)]
        turn_i = [ps(f"e0_turn_i{k}") for k in range(2)]
        down = ps("e0_down")
        rows_in = [sem(f"rows_in{k}") for k in range(2)]
        rows_out = [sem(f"rows_out{k}") for k in range(2)]
        po_turn = sem("po_turn")
        dv_now = sem("dv_now")
        pe_x = sem("pe_x")
        ac_x = sem("ac_x")
        dv_x = sem("dv_x")
        pe_up0 = sem("pe_up0")
        pe_up1 = sem("pe_up1")
        ac_silu = sem("ac_silu")
        dv_inter = sem("dv_inter")
        pe_i = sem("pe_i")
        ac_i = sem("ac_i")
        dv_i = sem("dv_i")
        pe_down = sem("pe_down")
        dv_down = sem("dv_down")
        block = ctx.enter_context(nc.Block())
        def done(t, ago=0):
            return t + 3 - ago

        def landed(n):
            return n * 16 + 32

        def walk(engine, step):
            step(0, 0, 0, True, False, True)
            with engine.Fori(0, J // 2 - 1) as n:
                step(n * 2 + 1, n, 1, True, True, True)
                step(n * 2 + 2, n + 1, 0, True, True, True)
            step(J - 1, J // 2 - 1, 1, True, True, False)
            step(J, J // 2, 0, False, True, False)

        @block.gpsimd
        def _(pool):
            with pool.Fori(0, J // 2) as n:
                for k in range(2):
                    pool.wait_ge(dv_now, done(n * 2 + k))
                    pool.wait_ge(pe_x, done(n * 2 + k, 2))
                    pool.sem_inc(po_turn, 1)
                    pool.indirect_dma_start(rows[:, k, :], None, y1,
                                            bass.IndirectOffsetOnAxis(ap=now[:, k:k + 1], axis=0)
                                            ).then_inc(rows_in[k], 16)

        @block.sync
        def _(sp):
            for k in range(2):
                sp.sem_inc(rows_out[k], 16)
            with sp.Fori(0, J // 2) as n:
                for k in range(2):
                    sp.wait_ge(dv_down, done(n * 2 + k))
                    sp.dma_start(out[bass.ds((n * 2 + k) * P, P), :], result[:, k, :]).then_inc(rows_out[k], 16)
            for k in range(2):
                sp.wait_ge(rows_out[k], 16 * (J // 2) + 16)

        @block.tensor
        def _(pe):
            for s in (pe_x, pe_up0, pe_up1, pe_i, pe_down):
                pe.sem_inc(s, 2)

            def turn_rows(t, n, k):
                pe.wait_ge(rows_in[k], n * 16 + 16)
                pe.wait_ge(ac_x, done(t, 1))
                pe.wait_ge(dv_x, done(t, 1))
                for c in range(DC):
                    i = pe.transpose(turn_x[:, c * P:(c + 1) * P], rows[:, k, c * P:(c + 1) * P], ident[:, :])
                i.then_inc(pe_x, 1)

            def product(bank, k, left, right, chunks, width, e):
                trio = [(c, a, b) for c in range(chunks) for a, b in ((0, 0), (0, 1), (1, 0))]
                for q, (c, a, b) in enumerate(trio):
                    i = pe.matmul(bank[:, 0:width], left[a][:, k, c * P:(c + 1) * P],
                                  right[b][:, bass.ds(e * (chunks * width) + c * width, width)], start=(q == 0),
                                  stop=(q == len(trio) - 1))
                return i

            def step(t, n, k, up, rest, more):
                if up:
                    e = pe.value_load(expert[0:1, bass.ds(t, 1)], min_val=0, max_val=E0 - 1)
                    pe.wait_ge(ac_x, done(t))
                    pe.wait_ge(dv_x, done(t))
                    pe.wait_ge(ac_silu, done(t, 2))
                    product(up0[k], k, xT, w0, DC, F0, e).then_inc(pe_up0, 1)
                if rest:
                    pe.wait_ge(dv_inter, done(t, 1))
                    pe.wait_ge(ac_i, done(t, 3))
                    pe.wait_ge(dv_i, done(t, 3))
                    for c in range(FC):
                        i = pe.transpose(turn_i[1 - k][:, c * P:(c + 1) * P], inter[:, 1 - k, c * P:(c + 1) * P],
                                         ident[:, :])
                    i.then_inc(pe_i, 1)
                if up:
                    pe.wait_ge(dv_inter, done(t, 2))
                    product(up1[k], k, xT, w1, DC, F0, e).then_inc(pe_up1, 1)
                if more:
                    turn_rows(t + 1, n + k, 1 - k)
                if rest:
                    e = pe.value_load(expert[0:1, bass.ds(t - 1, 1)], min_val=0, max_val=E0 - 1)
                    pe.wait_ge(ac_i, done(t, 1))
                    pe.wait_ge(dv_i, done(t, 1))
                    pe.wait_ge(dv_down, done(t, 2))
                    product(down, 1 - k, iT, wo, FC, D, e).then_inc(pe_down, 1)

            turn_rows(0, 0, 0)
            walk(pe, step)

        @block.scalar
        def _(act):
            for s in (ac_x, ac_silu, ac_i):
                act.sem_inc(s, 2)

            def high_x(t, k):
                act.wait_ge(pe_x, done(t))
                act.wait_ge(pe_up1, done(t, 2))
                act.activation(xT[0][:, k, :], turn_x[:, 0:D], ACT.Copy).then_inc(ac_x, 1)

            def step(t, n, k, up, rest, more):
                if up:
                    act.wait_ge(pe_up0, done(t))
                    act.wait_ge(dv_inter, done(t, 2))
                    act.activation(silu[:, k, :], up0[k][:, :], ACT.Silu, scale=1.0 / WSCALE).then_inc(ac_silu, 1)
                if rest:
                    act.wait_ge(pe_i, done(t, 1))
                    act.wait_ge(pe_down, done(t, 3))
                    act.activation(iT[0][:, 1 - k, :], turn_i[1 - k][:, :], ACT.Copy).then_inc(ac_i, 1)
                if more:
                    high_x(t + 1, 1 - k)

            high_x(0, 0)
            walk(act, step)

        @block.vector
        def _(dve):
            for s in (dv_now, dv_x, dv_inter, dv_i, dv_down):
                dve.sem_inc(s, 2)

            def fetch(t, n, k):
                if not (isinstance(t, int) and t < 2):
                    dve.wait_ge(rows_in[k], n * 16)
                dve.tensor_scalar(now[:, k:k + 1], index[:, bass.ds(t, 1)], 0.0, None, ALU.add).then_inc(dv_now, 1)

            def low_x(t, k):
                dve.wait_ge(ac_x, done(t))
                dve.tensor_tensor(xT[1][:, k, :], turn_x[:, 0:D], xT[0][:, k, :], ALU.subtract).then_inc(dv_x, 1)

            def step(t, n, k, up, rest, more, fetches=True):
                if rest:
                    dve.wait_ge(ac_i, done(t, 1))
                    dve.tensor_tensor(iT[1][:, 1 - k, :], turn_i[1 - k][:, :], iT[0][:, 1 - k, :],
                                      ALU.subtract).then_inc(dv_i, 1)
                if up:
                    dve.wait_ge(ac_silu, done(t))
                    dve.wait_ge(pe_up1, done(t))
                    dve.wait_ge(pe_i, done(t, 2))
                    dve.tensor_tensor(inter[:, k, :], silu[:, k, :], up1[k][:, :], ALU.mult).then_inc(dv_inter, 1)
                if more:
                    low_x(t + 1, 1 - k)
                if more and fetches:
                    fetch(t + 2, n + 1, k)
                if rest:
                    dve.wait_ge(pe_down, done(t, 1))
                    dve.wait_ge(rows_out[1 - k], landed(n + k) - 32)
                    dve.tensor_scalar(result[:, 1 - k, :], down[:, 0:D], 1.0 / WSCALE**2, None,
                                      ALU.mult).then_inc(dv_down, 1)

            fetch(0, 0, 0)
            fetch(1, 0, 1)
            low_x(0, 0)
            step(0, 0, 0, True, False, True)
            with dve.Fori(0, J // 2 - 2) as n:
                step(n * 2 + 1, n, 1, True, True, True)
                step(n * 2 + 2, n + 1, 0, True, True, True)
            step(J - 3, J // 2 - 2, 1, True, True, True)
            step(J - 2, J // 2 - 1, 0, True, True, True, fetches=False)
            step(J - 1, J // 2 - 1, 1, True, True, False)
            step(J, J // 2, 0, False, True, False)



H1, HD1 = 16, 16
STRIP = 32
STRIPS = P // STRIP
LIMIT = 50.0
SCALE1 = HD1**-0.5


def attention1(nc, NT, a, consts, x1, sorted0, dest, weight, wq, wk, wv, router, ident, tgates, x3, logits, yT):
    with ExitStack() as ctx:
        sb = lambda name, shape, dt=F32: ctx.enter_context(nc.sbuf_tensor("a1_" + name, shape, dt))
        ps = lambda name: ctx.enter_context(nc.psum_tensor("a1_" + name, [P, 512], F32))
        sem = lambda name: ctx.enter_context(nc.semaphore("a1_" + name))
        wo = sb("wo", [P, DC, D])
        bq = sb("bq", [P, DC])
        bk = sb("bk", [P, DC])
        bv = sb("bv", [P, D])
        bo = sb("bo", [P, D])
        gamma = sb("gamma", [P, D])
        beta = sb("beta", [P, D])
        rs = sb("rs", [P, 1])
        gates = sb("gates", [P, 4])
        half_neg = sb("half_neg", [P, 1])
        eps = sb("eps", [P, 1])
        mask_i = sb("mask_i", [P, NT, S], I32)
        bound = sb("bound", [P, NT, S])
        share = sb("share", [P, 2, NT])
        now = sb("now", [P, 2], I32)
        x1t = sb("x1t", [P, D])
        rows = sb("rows", [P, 2, D])
        x2 = sb("x2", [P, D])
        x2b = sb("x2b", [P, D])
        xn = sb("xn", [P, D])
        stats = sb("stats", [P, 6])
        mv = sb("mv", [P, 3, 2])
        rstd = sb("rstd", [P, 3])
        xT = [sb(f"xT{h}", [P, DC, P], F16) for h in ("hi", "lo")]
        ctx32 = sb("ctx32", [P, DC, NB, 2, S])
        cT = [sb(f"cT{h}", [P, DC, NB, 2, S], F16) for h in ("hi", "lo")]
        qT = sb("qT", [P, DC, P])
        kT = sb("kT", [P, DC, P])
        kz = sb("kz", [P, DC, NB, 2, S])
        vz = sb("vz", [P, NB, D])
        E = sb("E", [P, STRIPS, DC, 2, S])
        sums = sb("sums", [P, H1])
        PT = sb("PT", [P, STRIPS, DC, P])
        cxT = sb("cxT", [P, DC, P])
        delta = sb("delta", [P, D])
        x3t = sb("x3t", [P, D])
        yn = sb("yn", [P, D])
        score = [ps(f"score{r}") for r in range(STRIPS)]
        turn = ps("turn")
        proj = ps("proj")
        turnP = ps("turnP")
        outp = ps("outp")

        x1_in, ctx_in, const_in, x3_out = map(sem, ("x1_in", "ctx_in", "const_in", "x3_out"))
        rows_in = [sem(f"rows_in{k}") for k in range(2)]
        v_const, a_const, a_turn, p_const, p_turn, v_stats = map(sem, (
            "v_const", "a_const", "a_turn", "p_const", "p_turn", "v_stats"))
        e_x, e_qk, e_v, e_sc, e_PT, e_cx, e_d, e_y, e_log = map(sem, (
            "e_x",
            "e_qk",
            "e_v",
            "e_sc",
            "e_PT",
            "e_cx",
            "e_d",
            "e_y",
            "e_log"))
        v_now, v_x2, v_ln, v_xlo, v_cap, v_sum, v_norm, v_v, v_d, v_y, v_ylo, v_log = map(sem, (
            "v_now",
            "v_x2",
            "v_ln",
            "v_xlo",
            "v_cap",
            "v_sum",
            "v_norm",
            "v_v",
            "v_d",
            "v_y",
            "v_ylo",
            "v_log"))
        a_chi, a_xhi, a_qk, a_exp, a_PT, a_cx, a_yhi = map(sem, (
            "a_chi",
            "a_xhi",
            "a_qk",
            "a_exp",
            "a_PT",
            "a_cx",
            "a_yhi"))
        p_clo, p_rstd, p_rstd_d, p_rstd_y, p_kz, p_x2b = map(sem, (
            "p_clo",
            "p_rstd",
            "p_rstd_d",
            "p_rstd_y",
            "p_kz",
            "p_x2b"))
        block = ctx.enter_context(nc.Block())

        def walk(engine, iteration):
            iteration(0, None, None)
            iteration(1, 0, None)
            with engine.Fori(0, NT - 2) as c:
                iteration(c + 2, c + 1, c)
            iteration(None, NT - 1, NT - 2)
            iteration(None, None, NT - 1)

        loads = [(wo[:, :, :], a["a1_wo"].rearrange("p (c d) -> p c d", c=DC)), (bq[:, :], a["a1_bq"]),
                 (bk[:, :], a["a1_bk"])]
        loads += [(dst[:, :], a[name].partition_broadcast(P)) for dst, name in (
            (bv, "a1_bv"), (bo, "a1_bo"), (gamma, "a1_gamma"), (beta, "a1_beta"), (rs, "a1_rs"))]
        loads += [(gates[:, 0:2], a["g_ffn"].partition_broadcast(P)), (gates[:, 2:4], a["g_xattn"].partition_broadcast(P))]
        loads += [(mask_i[b * S:(b + 1) * S, :, :],
                   a["mask"].rearrange("(t b) k -> b t k", b=NB)[b].partition_broadcast(S)) for b in range(NB)]
        LOADED = 16 * len(loads)

        @block.sync
        def _(sp):
            for dst, src in loads:
                sp.dma_start(dst, src).then_inc(const_in, 16)
            sp.sem_inc(x1_in, 16)
            sp.sem_inc(ctx_in, 32)
            sp.sem_inc(x3_out, 16)

            def iteration(t, p, c):
                if t is not None:
                    sp.wait_ge(v_x2, last(2, t, 1))
                    sp.dma_start(x1t[:, :], x1[bass.ds(t * P, P), :]).then_inc(x1_in, 16)
                    sp.wait_ge(p_clo, last(1, t, 1))
                    for k in range(2):
                        sp.dma_start(ctx32[:, :, :, k, :], a["ctxT"][:, bass.ds(t * D, D)]
                                     .rearrange("p (c b s) -> p c b s", c=DC, b=NB)).then_inc(ctx_in, 16)
                if p is not None:
                    sp.wait_ge(v_d, this(5, p, 5))
                    sp.dma_start(x3[bass.ds(p * P, P), :], x3t[:, :]).then_inc(x3_out, 16)

            walk(sp, iteration)
            sp.wait_ge(x3_out, 16 * (NT + 1))

        @block.gpsimd
        def _(pool):
            pool.memset(half_neg[:, :], -0.5).then_inc(p_const, 1)
            pool.memset(eps[:, :], EPS_LN).then_inc(p_const, 1)
            pool.memset(vz[:, :, :], 0.0).then_inc(p_const, 1)
            for s, n in ((p_clo, 1), (p_rstd, 2), (p_rstd_d, 2), (p_rstd_y, 2), (p_kz, 1), (p_x2b, 1)):
                pool.sem_inc(s, n)
            pool.wait_ge(p_const, 3)
            pool.wait_ge(v_const, 1)

            def power(n, s, t):
                pool.tensor_tensor(rstd[:, n:n + 1], mv[:, n, 1:2], eps[:, :], ALU.add).then_inc(s, 1)
                pool.wait_ge(s, this(2, t, 1))
                pool.tensor_tensor(rstd[:, n:n + 1], rstd[:, n:n + 1], half_neg[:, :], ALU.pow).then_inc(s, 1)

            def gather(t):
                pool.wait_ge(v_now, this(1, t, 1))
                pool.wait_ge(v_x2, last(2, t, 2))
                pool.sem_inc(p_turn, 1)
                for k in range(2):
                    pool.indirect_dma_start(rows[:, k, :], None, sorted0,
                                            bass.IndirectOffsetOnAxis(ap=now[:, k:k + 1], axis=0)
                                            ).then_inc(rows_in[k], 16)

            def iteration(t, p, c):
                if t is not None:
                    gather(t)
                    pool.wait_ge(v_ln, this(2, t, 1))
                    power(0, p_rstd, t)
                    pool.wait_ge(a_chi, this(1, t, 1))
                    pool.wait_ge(ctx_in, this(32, t, 32))
                    pool.tensor_tensor(cT[1][:, :, :, :, :], ctx32[:, :, :, :, :], cT[0][:, :, :, :, :],
                                       ALU.subtract).then_inc(p_clo, 1)
                    pool.wait_ge(a_qk, this(1, t, 1))
                    if p is not None:
                        pool.wait_ge(e_sc, this(2, p, 2))
                    for h in range(DC):
                        pair = consts["pair"][:, :].unsqueeze(2).broadcast_to([P, 2, S])
                        for b in range(NB):
                            i = pool.tensor_tensor(kz[:, h, b, :, :], kT[:, h:h + 1, b * S:(b + 1) * S]
                                                   .broadcast_to([P, 2, S]), pair, ALU.mult)
                    i.then_inc(p_kz, 1)
                if p is not None:
                    pool.wait_ge(v_d, this(5, p, 2))
                    power(1, p_rstd_d, p)
                    pool.wait_ge(v_y, this(2, p, 1))
                    power(2, p_rstd_y, p)
                if t is not None:
                    if p is not None:
                        pool.wait_ge(v_d, this(5, p, 5))
                    pool.wait_ge(v_x2, this(2, t, 2))
                    pool.tensor_tensor(x2b[:, :], x2[:, :], beta[:, :], ALU.add).then_inc(p_x2b, 1)

            walk(pool, iteration)

        @block.tensor
        def _(pe):
            for s, n in ((e_x, 1), (e_qk, 1), (e_v, 1), (e_sc, 2), (e_PT, 2), (e_cx, 1), (e_d, 1), (e_y, 1), (e_log, 1)):
                pe.sem_inc(s, n)
            pe.wait_ge(const_in, LOADED)
            trio = [(c, i, j) for c in range(DC) for i, j in ((0, 0), (0, 1), (1, 0))]

            def mm3(out, left, right):
                for n, (c, i, j) in enumerate(trio):
                    m = pe.matmul(out, left(c, i), right(c, j), start=(n == 0), stop=(n == len(trio) - 1))
                return m

            def turn_x(t):
                pe.wait_ge(v_ln, this(2, t, 2))
                for c in range(DC):
                    i = pe.transpose(turn[:, c * P:(c + 1) * P], xn[:, c * P:(c + 1) * P], ident[:, :])
                i.then_inc(e_x, 1)

            def scores(p, half):
                if half == 0:
                    pe.wait_ge(p_kz, this(1, p, 1))
                    pe.wait_ge(a_qk, this(1, p, 1))
                pe.wait_ge(v_cap, last(2, p, half + 1))
                for r in (2 * half, 2 * half + 1):
                    strip = slice(r * STRIP, (r + 1) * STRIP)
                    for b in range(NB):
                        for h in range(DC):
                            i = pe.matmul(score[r][b * S:(b + 1) * S, h * P:(h + 1) * P],
                                          qT[strip, h, b * S:(b + 1) * S], kz[strip, h, b, :, :], start=True, stop=True)
                i.then_inc(e_sc, 1)

            def query_key(t):
                pe.wait_ge(v_xlo, this(1, t, 1))
                pe.wait_ge(p_clo, this(1, t, 1))
                pe.wait_ge(v_v, last(1, t, 1))
                for h in range(DC):
                    part = lambda c: slice(c * D + h * P, c * D + (h + 1) * P)
                    mm3(proj[:, h * P:(h + 1) * P], lambda c, i: wq[i][:, part(c)], lambda c, j: xT[j][:, c, :])
                    i = mm3(proj[:, D + h * P:D + (h + 1) * P], lambda c, i: wk[i][:, part(c)],
                            lambda c, j: cT[j][:, c, :, 0, :])
                i.then_inc(e_qk, 1)

            def value(t):
                pe.wait_ge(a_qk, this(1, t, 1))
                for b in range(NB):
                    i = mm3(proj[:, b * D:(b + 1) * D], lambda c, i: cT[i][:, c, b, :, :],
                            lambda c, j: wv[j][:, c * D:(c + 1) * D])
                i.then_inc(e_v, 1)

            def turn_P(p, half):
                pe.wait_ge(v_norm, this(2, p, half + 1))
                pe.wait_ge(a_PT, last(2, p, 2) if half == 0 else this(2, p, 1))
                for n in range(4):
                    r, h = 2 * half + n // 2, n % 2
                    i = pe.transpose(turnP[:, n * P:(n + 1) * P], E[:, r, h, :, :], ident[:, :])
                i.then_inc(e_PT, 1)

            def weigh(p, half):
                pe.wait_ge(a_PT, this(2, p, half + 1))
                if half == 0:
                    pe.wait_ge(v_d, last(5, p, 1))
                    pe.wait_ge(v_v, this(1, p, 1))
                for r in (2 * half, 2 * half + 1):
                    strip = slice(r * STRIP, (r + 1) * STRIP)
                    for h in range(DC):
                        for b in range(NB):
                            i = pe.matmul(outp[strip, h * P + b * S:h * P + (b + 1) * S],
                                          vz[:, b, h * P + r * STRIP:h * P + (r + 1) * STRIP],
                                          PT[:, r, h, b * S:(b + 1) * S], start=True, stop=True)
                if half == 1:
                    i.then_inc(e_cx, 1)

            def result(p):
                pe.wait_ge(a_cx, this(1, p, 1))
                for h in range(DC):
                    i = pe.matmul(outp[:, 0:D], cxT[:, h, :], wo[:, h, :], start=(h == 0), stop=(h == DC - 1))
                i.then_inc(e_d, 1)

            def turn_y(c, t):
                pe.wait_ge(v_y, this(2, c, 2))
                pe.wait_ge(v_log, last(1, c, 1))
                if t is not None:
                    pe.wait_ge(v_xlo, this(1, t, 1))
                for k in range(DC):
                    i = pe.transpose(turn[:, k * P:(k + 1) * P], yn[:, k * P:(k + 1) * P], ident[:, :])
                i.then_inc(e_y, 1)

            def route(c):
                pe.wait_ge(v_ylo, this(1, c, 1))
                for n, (k, i, j) in enumerate(trio):
                    m = pe.matmul(turn[:, 0:E1], yT[i][:, k, bass.ds(c * P, P)], router[j][:, k * E1:(k + 1) * E1],
                                  start=(n == 0), stop=(n == len(trio) - 1))
                m.then_inc(e_log, 1)

            def iteration(t, p, c):
                if p is not None:
                    scores(p, 0)
                    scores(p, 1)
                if t is not None:
                    if c is not None:
                        pe.wait_ge(v_log, last(1, c, 1))
                    turn_x(t)
                if t is not None:
                    query_key(t)
                if c is not None:
                    turn_y(c, t)
                if p is not None:
                    turn_P(p, 0)
                    weigh(p, 0)
                if c is not None:
                    route(c)
                if p is not None:
                    turn_P(p, 1)
                    weigh(p, 1)
                    result(p)
                if t is not None:
                    value(t)

            walk(pe, iteration)

        @block.vector
        def _(dve):
            chain = Chain(dve, v_const)
            for s, n in ((v_now, 1), (v_x2, 2), (v_ln, 2), (v_xlo, 1), (v_cap, 2), (v_sum, 6), (v_norm, 2), (v_v, 1),
                         (v_d, 5), (v_y, 2), (v_ylo, 1), (v_log, 1)):
                dve.sem_inc(s, n)
            dve.wait_ge(const_in, LOADED)
            dve.wait_ge(a_const, 1)
            chain(dve.tensor_scalar(beta[:, :], beta[:, :], tgates[:, 3:4], None, ALU.mult))
            chain(dve.tensor_scalar(gamma[:, :], gamma[:, :], tgates[:, 3:4], None, ALU.mult))
            chain(dve.tensor_scalar(rs[:, :], rs[:, :], 0.0, 0.3, ALU.max, ALU.min))
            chain(dve.tensor_scalar(bo[:, :], bo[:, :], rs[:, 0:1], None, ALU.mult))
            chain(dve.tensor_scalar(share[:, :, :], weight[:, :, :], tgates[:, 0:1], None, ALU.mult))
            chain(dve.tensor_scalar(bound[:, :, :], mask_i[:, :, :], 0.5, 2 * LIMIT / SCALE1, ALU.is_gt, ALU.mult))
            chain(dve.tensor_scalar(bound[:, :, :], bound[:, :, :], -LIMIT / SCALE1, None, ALU.add))

            def fetch(t):
                if not (isinstance(t, int) and t == 0):
                    for k in range(2):
                        dve.wait_ge(rows_in[k], t * 16)
                dve.tensor_scalar(now[:, :].unsqueeze(2), dest[:, :, bass.ds(t, 1)], 0.0, None,
                                  ALU.add).then_inc(v_now, 1)

            def sum_x2(t):
                dve.wait_ge(x1_in, this(16, t, 16))
                dve.wait_ge(rows_in[0], t * 16 + 16)
                dve.wait_ge(p_x2b, last(1, t, 1))
                dve.scalar_tensor_tensor(out=x2[:, :], in0=rows[:, 0, :], scalar=share[:, 0, bass.ds(t, 1)],
                                         in1=x1t[:, :], op0=ALU.mult, op1=ALU.add).then_inc(v_x2, 1)
                dve.wait_ge(rows_in[1], t * 16 + 16)
                dve.wait_ge(v_x2, this(2, t, 1))
                dve.scalar_tensor_tensor(out=x2[:, :], in0=rows[:, 1, :], scalar=share[:, 1, bass.ds(t, 1)],
                                         in1=x2[:, :], op0=ALU.mult, op1=ALU.add).then_inc(v_x2, 1)

            def moments(n, source, before, value, s):
                dve.sem_clear(v_stats)
                dve.wait_ge(before, value)
                dve.bn_stats(stats[:, :], source).then_inc(v_stats, 1)
                dve.wait_ge(v_stats, 1)
                dve.bn_aggr(mv[:, n, :], stats[:, :]).then_inc(s, 1)

            def standard(n, out, source, s):
                dve.tensor_scalar(out, source, mv[:, n, 0:1], rstd[:, n:n + 1], ALU.subtract, ALU.mult).then_inc(s, 1)

            def cap(p, half):
                dve.wait_ge(e_sc, this(2, p, half + 1))
                dve.wait_ge(e_PT, last(2, p, half + 1))
                for r in (2 * half, 2 * half + 1):
                    i = dve.scalar_tensor_tensor(
                        out=E[:, r, :, :, :].rearrange("p h j k -> p (h j) k"),
                        in0=score[r][:, 0:D].rearrange("p (n k) -> p n k", k=S), scalar=-LIMIT / SCALE1,
                        in1=bound[:, bass.ds(p, 1), :].broadcast_to([P, 4, S]), op0=ALU.max, op1=ALU.min)
                i.then_inc(v_cap, 1)

            def normalize(p, half):
                dve.wait_ge(a_exp, this(2, p, half + 1))
                e = E[:, 2 * half:2 * half + 2, :, :, :].rearrange("p r h j k -> p (r h j) k")
                s = sums[:, 8 * half:8 * half + 8]
                dve.tensor_reduce(s, e, AX_X, ALU.add).then_inc(v_sum, 1)
                dve.wait_ge(v_sum, this(6, p, 3 * half + 1))
                dve.scalar_tensor_tensor(out=s, in0=s, scalar=1e-8, in1=s, op0=ALU.mult, op1=ALU.add).then_inc(v_sum, 1)
                dve.wait_ge(v_sum, this(6, p, 3 * half + 2))
                dve.reciprocal(s, s).then_inc(v_sum, 1)
                dve.wait_ge(v_sum, this(6, p, 3 * half + 3))
                dve.tensor_tensor(e, e, s.unsqueeze(2).broadcast_to([P, 8, S]), ALU.mult).then_inc(v_norm, 1)

            def keep_value(t):
                dve.wait_ge(e_v, this(1, t, 1))
                for b in range(NB):
                    for j in range(2):
                        half = slice(j * S, (j + 1) * S)
                        view = lambda y: y.rearrange("p (m j d) -> p m j d", j=2, d=HD1)[:, :, j, :]
                        i = dve.scalar_tensor_tensor(out=view(vz[half, b, :]), in0=view(proj[half, b * D:(b + 1) * D]),
                                                     scalar=1.0 / WSCALE, in1=view(bv[half, :]), op0=ALU.mult,
                                                     op1=ALU.add)
                i.then_inc(v_v, 1)

            def residual(p):
                dve.wait_ge(e_d, this(1, p, 1))
                dve.scalar_tensor_tensor(out=delta[:, :], in0=outp[:, 0:D], scalar=rs[:, 0:1], in1=bo[:, :],
                                         op0=ALU.mult, op1=ALU.add).then_inc(v_d, 1)
                moments(1, delta[:, :], v_d, this(5, p, 1), v_d)
                dve.wait_ge(p_rstd_d, this(2, p, 2))
                standard(1, delta[:, :], delta[:, :], v_d)
                dve.wait_ge(v_d, this(5, p, 3))
                dve.tensor_tensor(delta[:, :], delta[:, :], gamma[:, :], ALU.mult).then_inc(v_d, 1)
                dve.wait_ge(v_d, this(5, p, 4))
                dve.wait_ge(p_x2b, this(1, p, 1))
                dve.wait_ge(x3_out, last(16, p, 16))
                dve.tensor_tensor(x3t[:, :], delta[:, :], x2b[:, :], ALU.add).then_inc(v_d, 1)
                moments(2, x3t[:, :], v_d, this(5, p, 5), v_y)
                dve.wait_ge(p_rstd_y, this(2, p, 2))
                dve.wait_ge(e_y, last(1, p, 1))
                standard(2, yn[:, :], x3t[:, :], v_y)

            def iteration(t, p, c):
                if t is not None:
                    sum_x2(t)
                    moments(0, x2[:, :], v_x2, this(2, t, 2), v_ln)
                if p is not None:
                    cap(p, 0)
                    cap(p, 1)
                if t is not None:
                    dve.wait_ge(p_rstd, this(2, t, 2))
                    dve.wait_ge(e_x, last(1, t, 1))
                    standard(0, xn[:, :], x2[:, :], v_ln)
                    dve.wait_ge(a_xhi, this(1, t, 1))
                    dve.tensor_tensor(xT[1][:, :, :], turn[:, 0:D].rearrange("p (c k) -> p c k", c=DC), xT[0][:, :, :],
                                      ALU.subtract).then_inc(v_xlo, 1)
                if t is not None and not (isinstance(t, int) and t == NT - 1):
                    fetch(t + 1)
                if p is not None:
                    normalize(p, 0)
                    normalize(p, 1)
                if c is not None:
                    dve.wait_ge(a_yhi, this(1, c, 1))
                    dve.tensor_tensor(yT[1][:, :, bass.ds(c * P, P)], turn[:, 0:D].rearrange("p (c k) -> p c k", c=DC),
                                      yT[0][:, :, bass.ds(c * P, P)], ALU.subtract).then_inc(v_ylo, 1)
                    dve.wait_ge(e_log, this(1, c, 1))
                    dve.tensor_scalar(logits[:, bass.ds(c * E1, E1)], turn[:, 0:E1], 1.0 / WSCALE, None,
                                      ALU.mult).then_inc(v_log, 1)
                if p is not None:
                    residual(p)
                if t is not None:
                    keep_value(t)

            fetch(0)
            iteration(0, None, None)
            iteration(1, 0, None)
            with dve.Fori(0, NT - 3) as c:
                iteration(c + 2, c + 1, c)
            iteration(NT - 1, NT - 2, NT - 3)
            iteration(None, NT - 1, NT - 2)
            iteration(None, None, NT - 1)

        @block.scalar
        def _(act):
            for s, n in ((a_chi, 1), (a_xhi, 1), (a_qk, 1), (a_exp, 2), (a_PT, 2), (a_cx, 1), (a_yhi, 1)):
                act.sem_inc(s, n)
            act.wait_ge(const_in, LOADED)
            act.activation(tgates[:, :], gates[:, :], ACT.Tanh).then_inc(a_const, 1)

            def iteration(t, p, c):
                if t is not None:
                    act.wait_ge(ctx_in, this(32, t, 32))
                    act.wait_ge(e_v, last(1, t, 1))
                    act.activation(cT[0][:, :, :, :, :], ctx32[:, :, :, :, :], ACT.Copy).then_inc(a_chi, 1)
                if p is not None:
                    act.wait_ge(v_cap, this(2, p, 1))
                    act.activation(E[:, 0:2, :, :, :], E[:, 0:2, :, :, :], ACT.Exp, scale=SCALE1).then_inc(a_exp, 1)
                if t is not None:
                    act.wait_ge(e_x, this(1, t, 1))
                    act.wait_ge(e_qk, last(1, t, 1))
                    act.activation(xT[0][:, :, :], turn[:, 0:D].rearrange("p (c k) -> p c k", c=DC),
                                   ACT.Copy).then_inc(a_xhi, 1)
                if p is not None:
                    act.wait_ge(v_cap, this(2, p, 2))
                    act.activation(E[:, 2:4, :, :, :], E[:, 2:4, :, :, :], ACT.Exp, scale=SCALE1).then_inc(a_exp, 1)
                if t is not None:
                    act.wait_ge(e_qk, this(1, t, 1))
                    if p is not None:
                        act.wait_ge(e_sc, this(2, p, 2))
                    act.wait_ge(p_kz, last(1, t, 1))
                    for h in range(DC):
                        act.activation(qT[:, h, :], proj[:, h * P:(h + 1) * P], ACT.Identity, bias=bq[:, h:h + 1],
                                       scale=1.0 / WSCALE)
                        i = act.activation(kT[:, h, :], proj[:, D + h * P:D + (h + 1) * P], ACT.Identity,
                                           bias=bk[:, h:h + 1], scale=1.0 / WSCALE)
                    i.then_inc(a_qk, 1)
                if c is not None:
                    act.wait_ge(e_y, this(1, c, 1))
                    act.sem_inc(a_turn, 1)
                    act.activation(yT[0][:, :, bass.ds(c * P, P)], turn[:, 0:D].rearrange("p (c k) -> p c k", c=DC),
                                   ACT.Copy).then_inc(a_yhi, 1)
                if p is not None:
                    for half in range(2):
                        act.wait_ge(e_PT, this(2, p, half + 1))
                        act.wait_ge(e_cx, last(1, p, 1))
                        act.activation(PT[:, 2 * half:2 * half + 2, :, :].rearrange("p r h q -> p (r h) q"),
                                       turnP[:, :].rearrange("p (n q) -> p n q", q=P), ACT.Copy).then_inc(a_PT, 1)
                    act.wait_ge(e_cx, this(1, p, 1))
                    act.activation(cxT[:, :, :], outp[:, 0:D].rearrange("p (h q) -> p h q", h=DC),
                                   ACT.Copy).then_inc(a_cx, 1)

            walk(act, iteration)


def route1(nc, NT, CAP, logits, consts, tgate, share):
    B = 2 * NT
    BANK = 512 // E1
    banks = [(b, min(B, b + BANK)) for b in range(0, B, BANK)]
    with ExitStack() as ctx:
        sb = lambda name, shape, dt=F32: ctx.enter_context(nc.sbuf_tensor("r1_" + name, shape, dt))
        sem = lambda name: ctx.enter_context(nc.semaphore("r1_" + name))
        hot = sb("hot", [P, 2, NT, E1])
        hot16 = sb("hot16", [P, B * E1], F16)
        best = sb("best", [P, 2, NT])
        t = sb("t", [P, NT, E1])
        m = sb("m", [P, NT])
        zero = sb("zero", [P, B])
        count = sb("count", [P, B, E1])
        rank_sb = sb("rank_sb", [P, B, E1])
        upto = sb("upto", [P, E1, B])
        rank = [ctx.enter_context(nc.psum_tensor(f"r1_rank{n}", [P, 512], F32)) for n in range(len(banks))]
        total = [ctx.enter_context(nc.psum_tensor(f"r1_total{n}", [P, 512], F32)) for n in range(len(banks))]
        dv_step, dv_shift, ac_exp, dv_hot, pe_count = map(sem, ("dv_step", "dv_shift", "ac_exp", "dv_hot", "pe_count"))
        block = ctx.enter_context(nc.Block())

        @block.vector
        def _(dve):
            chain = Chain(dve, dv_step)
            values = logits[:, :].rearrange("p (t e) -> p t e", e=E1)
            wide = lambda y: y.unsqueeze(2).broadcast_to([P, NT, E1])
            chain(dve.tensor_reduce(m[:, :], values, AX_X, ALU.max))
            dve.tensor_tensor(values, values, wide(m[:, :]), ALU.subtract).then_inc(dv_shift, 1)
            dve.wait_ge(ac_exp, 1)
            chain(dve.tensor_reduce(m[:, :], values, AX_X, ALU.add))
            chain(dve.reciprocal(m[:, :], m[:, :]))
            chain(dve.tensor_tensor(values, values, wide(m[:, :]), ALU.mult))
            order = consts["order"][:, :].unsqueeze(1).broadcast_to([P, NT, E1])
            top2(dve, chain, values, order, hot, best, t[:, :, :], m[:, :])
            dve.tensor_copy(hot16[:, :], hot[:, :, :, :].rearrange("p k t e -> p (k t e)")).then_inc(dv_hot, 1)
            chain(dve.tensor_tensor(m[:, :], best[:, 0, :], best[:, 1, :], ALU.add))
            chain(dve.reciprocal(m[:, :], m[:, :]))
            chain(dve.tensor_scalar(m[:, :], m[:, :], tgate, None, ALU.mult))
            chain(dve.tensor_tensor(best[:, :, :], best[:, :, :], m[:, :].unsqueeze(1).broadcast_to([P, 2, NT]), ALU.mult))
            chain(dve.memset(zero[:, :], 0.0))
            dve.wait_ge(pe_count, 2 * len(banks))
            for n, (b0, b1) in enumerate(banks):
                dve.tensor_copy(rank_sb[:, b0:b1, :].rearrange("p b e -> p (b e)"), rank[n][:, 0:(b1 - b0) * E1])
                i = dve.tensor_copy(count[:, b0:b1, :].rearrange("p b e -> p (b e)"), total[n][:, 0:(b1 - b0) * E1])
            chain(i)
            for e in range(E1):
                i = dve.tensor_tensor_scan(upto[:, e, :], count[:, :, e], zero[:, :], 0.0, ALU.add, ALU.add)
            chain(i)
            chain(dve.tensor_tensor(count[:, :, :], upto[:, :, :].rearrange("p e b -> p b e"), count[:, :, :], ALU.subtract))
            chain(dve.tensor_tensor(count[:, :, :], count[:, :, :], rank_sb[:, :, :], ALU.add))
            chain(dve.tensor_scalar(count[:, :, :], count[:, :, :], float(CAP), None, ALU.is_lt))
            chain(dve.tensor_tensor(count[:, :, :], count[:, :, :], hot[:, :, :, :].rearrange("p k t e -> p (k t) e"), ALU.mult))
            chain(dve.tensor_tensor(count[:, :, :], count[:, :, :],
                                    best[:, :, :].rearrange("p k t -> p (k t)").unsqueeze(2).broadcast_to([P, B, E1]),
                                    ALU.mult))
            chain(dve.tensor_tensor(share[:, :, :], count[:, 0:NT, :], count[:, NT:B, :], ALU.add))

        @block.scalar
        def _(act):
            act.wait_ge(dv_shift, 1)
            act.activation(logits[:, :], logits[:, :], ACT.Exp).then_inc(ac_exp, 1)

        @block.tensor
        def _(pe):
            pe.wait_ge(dv_hot, 1)
            for n, (b0, b1) in enumerate(banks):
                for out, left in ((rank[n], "before"), (total[n], "ones")):
                    pe.matmul(out[:, 0:(b1 - b0) * E1], consts[left][:, :], hot16[:, b0 * E1:b1 * E1], start=True,
                              stop=True).then_inc(pe_count, 1)


def experts1(nc, NT, yT, w1, w3, w2_dram, share, ident, x3, out):
    W = E1 * F1
    WC = W // P
    with ExitStack() as ctx:
        sb = lambda name, shape, dt=F32: ctx.enter_context(nc.sbuf_tensor("e1_" + name, shape, dt))
        ps = lambda name: ctx.enter_context(nc.psum_tensor("e1_" + name, [P, 512], F32))
        sem = lambda name: ctx.enter_context(nc.semaphore("e1_" + name))
        w2 = sb("w2", [P, WC, D])
        first = sb("first", [P, 2, W])
        inter = sb("inter", [P, 2, W])
        iT = sb("iT", [P, 2, W])
        x3t = sb("x3t", [P, 2, D])
        x4t = sb("x4t", [P, 2, D])
        up1 = [ps(f"up1{k}") for k in range(2)]
        up3 = [ps(f"up3{k}") for k in range(2)]
        turn = [ps(f"turn{k}") for k in range(2)]
        down = [ps(f"down{k}") for k in range(2)]
        w2_in = sem("w2_in")
        x3_in = [sem(f"x3_in{k}") for k in range(2)]
        x4_out = [sem(f"x4_out{k}") for k in range(2)]
        pe_up1, pe_up3, pe_turn, pe_down, ac_first, ac_silu, ac_iT, dv_ab, dv_share, dv_x4 = map(sem, (
            "pe_up1", "pe_up3", "pe_turn", "pe_down", "ac_first", "ac_silu", "ac_iT", "dv_ab", "dv_share", "dv_x4"))
        block = ctx.enter_context(nc.Block())

        def done(t, ago=0):
            return t + 3 - ago

        def walk(engine, step):
            step(0, 0, 0, True, False)
            with engine.Fori(0, NT // 2 - 1) as n:
                step(n * 2 + 1, n, 1, True, True)
                step(n * 2 + 2, n + 1, 0, True, True)
            step(NT - 1, NT // 2 - 1, 1, True, True)
            step(NT, NT // 2, 0, False, True)

        @block.sync
        def _(sp):
            sp.dma_start(w2[:, :, :], w2_dram.rearrange("p (c d) -> p c d", c=WC)).then_inc(w2_in, 16)
            for k in range(2):
                sp.sem_inc(x3_in[k], 16)
                sp.sem_inc(x4_out[k], 16)

            def step(t, n, k, up, rest):
                if up:
                    sp.wait_ge(dv_x4, done(t, 2))
                    sp.dma_start(x3t[:, k, :], x3[bass.ds(t * P, P), :]).then_inc(x3_in[k], 16)
                if rest:
                    sp.wait_ge(dv_x4, done(t, 1))
                    sp.dma_start(out[bass.ds((t - 1) * P, P), :], x4t[:, 1 - k, :]).then_inc(x4_out[1 - k], 16)

            walk(sp, step)
            for k in range(2):
                sp.wait_ge(x4_out[k], 16 * (NT // 2) + 16)

        @block.tensor
        def _(pe):
            for s in (pe_up1, pe_up3, pe_turn, pe_down):
                pe.sem_inc(s, 2)
            pe.wait_ge(w2_in, 16)
            trio = [(c, i, j) for c in range(DC) for i, j in ((0, 0), (0, 1), (1, 0))]

            def up_product(bank, t, w):
                for q, (c, i, j) in enumerate(trio):
                    m = pe.matmul(bank[:, 0:W], yT[i][:, c, bass.ds(t * P, P)], w[j][:, c * W:(c + 1) * W],
                                  start=(q == 0), stop=(q == len(trio) - 1))
                return m

            def step(t, n, k, up, rest):
                if up:
                    pe.wait_ge(ac_first, done(t, 2))
                    up_product(up1[k], t, w1).then_inc(pe_up1, 1)
                    pe.wait_ge(dv_ab, done(t, 2))
                    up_product(up3[k], t, w3).then_inc(pe_up3, 1)
                if rest:
                    pe.wait_ge(dv_share, done(t, 1))
                    pe.wait_ge(ac_iT, done(t, 3))
                    for c in range(WC):
                        i = pe.transpose(turn[1 - k][:, c * P:(c + 1) * P], inter[:, 1 - k, c * P:(c + 1) * P], ident[:, :])
                    i.then_inc(pe_turn, 1)
                    pe.wait_ge(ac_iT, done(t, 1))
                    pe.wait_ge(dv_x4, done(t, 3))
                    for c in range(WC):
                        i = pe.matmul(down[1 - k][:, 0:D], iT[:, 1 - k, c * P:(c + 1) * P], w2[:, c, :], start=(c == 0),
                                      stop=(c == WC - 1))
                    i.then_inc(pe_down, 1)

            walk(pe, step)

        @block.scalar
        def _(act):
            for s in (ac_first, ac_silu, ac_iT):
                act.sem_inc(s, 2)

            def step(t, n, k, up, rest):
                if up:
                    act.wait_ge(pe_up1, done(t))
                    act.wait_ge(dv_ab, done(t, 2))
                    act.activation(first[:, k, :], up1[k][:, 0:W], ACT.Copy).then_inc(ac_first, 1)
                if rest:
                    act.wait_ge(pe_turn, done(t, 1))
                    act.wait_ge(pe_down, done(t, 3))
                    act.activation(iT[:, 1 - k, :], turn[1 - k][:, 0:W], ACT.Copy).then_inc(ac_iT, 1)
                if up:
                    act.wait_ge(dv_ab, done(t))
                    act.activation(inter[:, k, :], inter[:, k, :], ACT.Silu, scale=1.0 / WSCALE**2).then_inc(ac_silu, 1)

            walk(act, step)

        @block.vector
        def _(dve):
            for s in (dv_ab, dv_share, dv_x4):
                dve.sem_inc(s, 2)

            def step(t, n, k, up, rest):
                if up:
                    dve.wait_ge(ac_first, done(t))
                    dve.wait_ge(pe_up3, done(t))
                    dve.wait_ge(pe_turn, done(t, 2))
                    dve.tensor_tensor(inter[:, k, :], first[:, k, :], up3[k][:, 0:W], ALU.mult).then_inc(dv_ab, 1)
                    dve.wait_ge(ac_silu, done(t))
                    i = inter[:, k, :].rearrange("p (e f) -> p e f", f=F1)
                    dve.tensor_tensor(i, i, share[:, bass.ds(t, 1), :].rearrange("p o e -> p e o")
                                      .broadcast_to([P, E1, F1]), ALU.mult).then_inc(dv_share, 1)
                if rest:
                    dve.wait_ge(pe_down, done(t, 1))
                    dve.wait_ge(x3_in[1 - k], (n + k) * 16 + 16)
                    dve.wait_ge(x4_out[1 - k], (n + k) * 16)
                    dve.tensor_tensor(x4t[:, 1 - k, :], down[1 - k][:, 0:D], x3t[:, 1 - k, :], ALU.add).then_inc(dv_x4, 1)

            walk(dve, step)


def program(nc, a, out, NT=32, stages=9):
    scratch = lambda name, rows: nc.dram_tensor(name, (rows, D), F32, kind="Internal").ap()
    J = (2 * NT * P + E0 * (P - 1)) // P
    J += J % 2
    x1 = out if stages == 1 else scratch("x1", NT * P)
    y1 = scratch("y1", NT * P)
    sorted0 = scratch("sorted0", J * P)
    rope_dram = nc.dram_tensor("rope_tables", (NT * P, 4 * HALF), F32, kind="Internal").ap()
    with ExitStack() as top:
        sb = lambda name, shape, dt=F32: top.enter_context(nc.sbuf_tensor(name, shape, dt))
        ident = sb("ident", [P, P])
        logits = sb("logits0", [P, NT * E0])
        dest = sb("dest0", [P, 2, NT], I32)
        weight = sb("weight0", [P, 2, NT])
        consts = {name: sb(name, list(a[name].shape), F16 if name in ("before", "ones") else F32)
                  for name in ("order", "count", "token", "pair", "before", "ones")}
        const_in = top.enter_context(nc.semaphore("const_in"))
        with nc.Block() as block:
            @block.sync
            def _(sp):
                sp.dma_start(ident[:, :], a["ident"]).then_inc(const_in, 16)
                for name, tile in consts.items():
                    sp.dma_start(tile[:, :], a[name]).then_inc(const_in, 16)
                sp.wait_ge(const_in, 16 * (1 + len(consts)))

        def pairs(stack, **sizes):
            return [tuple(stack.enter_context(nc.sbuf_tensor(f"{name}_{h}", [P, n], F16)) for h in ("hi", "lo"))
                    for name, n in sizes.items()]

        split_weights = WeightSplitter(nc, top)

        def split(*jobs):
            split_weights(*((a[name], *(w[:, :] for w in pair)) for name, pair in jobs))

        if True:
            with ExitStack() as st:
                wq, wk, wv = pairs(st, wq=DC * H0 * HD0, wk=DC * KV0 * HD0, wv=DC * KV0 * HD0)
                rope_tables(nc, NT, a["pos"], a["freq"], rope_dram)
                split(("wq0", wq), ("wk0", wk), ("wv0", wv))
                attention0(nc, NT, a["x"], a["ctxT"], rope_dram, a["qnw"], a["knw"], a["g_xattn"], wq, wk, wv,
                           a["wo0"], a["gate0"], ident, x1, y1, logits)
        if stages >= 2:
            with ExitStack() as st:
                expert = st.enter_context(nc.sbuf_tensor("expert", [P, J], I32))
                index = st.enter_context(nc.sbuf_tensor("index", [P, J], I32))
                w0, w1, wo = pairs(st, w0=E0 * DC * F0, w1=E0 * DC * F0, wo=E0 * FC * D)
                split(("e0_w0", w0), ("e0_w1", w1), ("e0_wo", wo))
                route0(nc, NT, J, logits, consts, dest, weight, expert, index)
                experts0(nc, NT, J, y1, w0, w1, wo, expert, index, ident, sorted0)
        if stages >= 3:
            CAP = int(np.ceil(NT * P / E1 * 1.25))
            tgates = sb("tgates", [P, 4])
            logits1 = sb("logits1", [P, NT * E1])
            share1 = sb("share1", [P, NT, E1])
            yT = [sb(f"yT{h}", [P, DC, NT * P], F16) for h in ("hi", "lo")]
            x3 = out if stages == 3 else scratch("x3", NT * P)
            with ExitStack() as st:
                wq1, wk1, wv1, router1 = pairs(st, wq1=DC * D, wk1=DC * D, wv1=DC * D, router1=DC * E1)
                split(("a1_wq", wq1), ("a1_wk", wk1), ("a1_wv", wv1), ("gate1", router1))
                attention1(nc, NT, a, consts, x1, sorted0, dest, weight, wq1, wk1, wv1, router1, ident, tgates, x3,
                           logits1, yT)
        if stages >= 4:
            route1(nc, NT, CAP, logits1, consts, tgates[:, 1:2], share1)
            with ExitStack() as st:
                w1, w3 = pairs(st, e1_w1=DC * E1 * F1, e1_w3=DC * E1 * F1)
                split(("e1_w1", w1), ("e1_w3", w3))
                experts1(nc, NT, yT, w1, w3, a["e1_w2"], share1, ident, x3, out)


def layout(i, NT=32):
    tok = lambda y: np.ascontiguousarray(np.asarray(y).reshape(-1, D)[:NT * P])
    chunks = lambda w: np.ascontiguousarray(w.reshape(-1, P, w.shape[1]).transpose(1, 0, 2).reshape(P, -1))
    rows = lambda w: chunks(np.asarray(w).T)
    columns = lambda y: np.ascontiguousarray(np.asarray(y).reshape(-1, P).T)
    experts = lambda w: np.ascontiguousarray(
        np.asarray(w).reshape(w.shape[0], -1, P, w.shape[2]).transpose(2, 0, 1, 3).reshape(P, -1))
    pos, itok = (np.asarray(i[k]).reshape(-1)[:NT * P].reshape(NT, P) for k in ("pos_BxS2", "itok_BxS_4096_4607"))
    inv = 1.0 / THETA ** (np.arange(0, HD0, 2, dtype=np.float32) / np.float32(HD0))
    c = np.asarray(i["ctx_2048"]).reshape(-1, D)[:NT * P].reshape(NT, P, DC, P)
    return {
        "x": tok(i["x"]),
        "ctxT": np.ascontiguousarray(c.transpose(3, 0, 2, 1).reshape(P, NT * D)),
        "pos": np.ascontiguousarray(np.stack([itok, pos], 1).transpose(2, 0, 1).reshape(P, NT * 2)),
        "freq": np.ascontiguousarray(np.broadcast_to(inv.astype(np.float32), (P, HALF))),
        "ident": np.eye(P, dtype=np.float32),
        "qnw": np.asarray(i["L0_xattn_q_norm_w"]), "knw": np.asarray(i["L0_xattn_k_norm_w"]),
        "g_xattn": np.asarray(i["g_xattn"]),
        "wq0": rows(i["L0_xattn_Wq"]), "wk0": rows(i["L0_xattn_Wk"]), "wv0": rows(i["L0_xattn_Wv"]),
        "order": np.ascontiguousarray(np.broadcast_to(np.arange(E1, 0, -1, dtype=np.float32), (P, E1))),
        "count": np.ascontiguousarray(np.broadcast_to(np.arange(P, dtype=np.float32), (P, P))),
        "token": np.ascontiguousarray(np.tile(np.arange(NT * P, dtype=np.float32).reshape(NT, P).T, (1, 2))),
        "before": np.triu(np.ones((P, P), np.float16), 1), "ones": np.ones((P, P), np.float16),
        "e0_w0": experts(i["L0_ffn_w0_kernel"]), "e0_w1": experts(i["L0_ffn_w1_kernel"]),
        "e0_wo": experts(i["L0_ffn_wo_kernel"]), "g_ffn": np.asarray(i["g_ffn"]),
        "pair": np.ascontiguousarray((np.arange(P)[:, None] % STRIP // HD1 == np.arange(2)).astype(np.float32)),
        "mask": np.asarray(i["mask_BxS2_ik0"])[:NT * NB],
        "a1_wq": rows(i["L1_xattn_Wq"]), "a1_wk": rows(i["L1_xattn_Wk"]), "a1_wv": rows(i["L1_xattn_Wv"]),
        "a1_wo": rows(i["L1_xattn_Wo"]), "a1_bq": columns(i["L1_xattn_bq"]), "a1_bk": columns(i["L1_xattn_bk"]),
        "a1_bv": np.asarray(i["L1_xattn_bv"]), "a1_bo": np.asarray(i["L1_xattn_bo"]),
        "a1_gamma": np.asarray(i["L1_xattn_ln_gamma"]), "a1_beta": np.asarray(i["L1_xattn_ln_beta"]),
        "a1_rs": np.asarray(i["L1_xattn_residual_scale"]).reshape(1),
        "gate1": rows(i["L1_ffn_gate_w"]), "e1_w1": rows(np.asarray(i["L1_ffn_w1"]).reshape(-1, D)),
        "e1_w3": rows(np.asarray(i["L1_ffn_w3"]).reshape(-1, D)),
        "e1_w2": chunks(np.asarray(i["L1_ffn_w2"]).transpose(0, 2, 1).reshape(-1, D)),
        "wo0": rows(i["L0_xattn_Wo"]), "gate0": chunks(np.asarray(i["L0_ffn_gate_kernel"])),
    }


def kernel(**inputs):
    import concourse.bacc as bacc
    from concourse.bass_utils import run_bass_kernel_spmd

    shape = np.asarray(inputs["x"]).shape
    arrays = {name: np.ascontiguousarray(y) for name, y in layout(inputs).items()}
    nc = bacc.Bacc("TRN2", target_bir_lowering=False, num_devices=1)
    a = {name: nc.dram_tensor(f"in_{name}", y.shape, mybir.dt.from_np(y.dtype), kind="ExternalInput").ap()
         for name, y in arrays.items()}
    out = nc.dram_tensor("out", (64 * S, D), F32, kind="ExternalOutput").ap()
    program(nc, a, out)
    result = run_bass_kernel_spmd(nc, [{f"in_{name}": y for name, y in arrays.items()}], core_ids=[0])
    return result.results[0]["out"].reshape(shape)
```

```python
from contextlib import ExitStack

import numpy as np
import concourse.bass as bass
from concourse import mybir

F32 = mybir.dt.float32
F16 = mybir.dt.float16
I32 = mybir.dt.int32
ALU = mybir.AluOpType
ACT = mybir.ActivationFunctionType
AX_X = mybir.AxisListType.X

P = 128
D = 256
DC = D // P
S = 64
NB = 2
H0, KV0, HD0 = 16, 4, 128
GROUP = H0 // KV0
E0, F0 = 8, 512
FC = F0 // P
E1, F1 = 12, 32
HALF = HD0 // 2
WSCALE = 64.0
EPS_LN = 1e-5
EPS_RMS = 1e-6
THETA = 10000.0
TWO_PI = 2.0 * np.pi
PI_A = 6.28125
PI_B = float(np.float32(np.round((TWO_PI - PI_A) * 2.0**21) / 2.0**21))
PI_C = float(TWO_PI - PI_A - PI_B)
ROUND = 1.5 * 2.0**23


def this(n, t, k):
    return n * t + n + k


def last(n, t, k):
    return n * t + k


def rope_tables(nc, NT, pos, freq_dram, rope_dram):
    W = NT * 2 * HALF
    with ExitStack() as ctx:
        sb = lambda name, shape, dt: ctx.enter_context(nc.sbuf_tensor(name, shape, dt))
        sem = lambda name: ctx.enter_context(nc.semaphore(name))
        pos_i = sb("pos_i", [P, NT * 2], I32)
        pos_f = sb("pos_f", [P, NT * 2, 1], F32)
        freq = sb("freq", [P, 1, HALF], F32)
        angle = sb("angle", [P, NT * 2, HALF], F32)
        turns = sb("turns", [P, NT * 2, HALF], F32)
        table = sb("table", [P, NT * 2, 2, HALF], F32)
        pos_in, freq_set, step, shifted, tables_made, stored = map(sem, (
            "pos_in", "freq_set", "rope_step", "rope_shifted", "tables_made", "rope_stored"))
        block = ctx.enter_context(nc.Block())

        @block.sync
        def _(sp):
            sp.dma_start(pos_i[:, :], pos).then_inc(pos_in, 16)
            sp.dma_start(freq[:, 0, :], freq_dram).then_inc(freq_set, 16)
            sp.wait_ge(tables_made, 2)
            sp.dma_start(rope_dram.rearrange("(t p) w -> p t w", p=P),
                         table[:, :, :, :].rearrange("p (t s) c d -> p t (s c d)", s=2)).then_inc(stored, 16)
            sp.wait_ge(stored, 16)

        @block.vector
        def _(dve):
            dve.wait_ge(pos_in, 16)
            dve.tensor_copy(pos_f[:, :, 0], pos_i[:, :]).then_inc(step, 1)
            dve.wait_ge(freq_set, 16)
            dve.wait_ge(step, 1)
            shape = [P, NT * 2, HALF]
            dve.tensor_tensor(angle[:, :, :], pos_f[:, :, :].broadcast_to(shape), freq[:, :, :].broadcast_to(shape),
                              ALU.mult).then_inc(step, 1)
            dve.wait_ge(step, 2)
            dve.tensor_scalar(turns[:, :, :], angle[:, :, :], 1.0 / TWO_PI, ROUND, ALU.mult, ALU.add).then_inc(step, 1)
            dve.wait_ge(step, 3)
            dve.tensor_scalar(turns[:, :, :], turns[:, :, :], -ROUND, None, ALU.add).then_inc(step, 1)
            for n, part in enumerate((PI_A, PI_B, PI_C)):
                dve.wait_ge(step, 4 + n)
                dve.scalar_tensor_tensor(out=angle[:, :, :], in0=turns[:, :, :], scalar=-part, in1=angle[:, :, :],
                                         op0=ALU.mult, op1=ALU.add).then_inc(step, 1)
            dve.wait_ge(step, 7)
            dve.tensor_scalar(angle[:, :, :], angle[:, :, :], -3.1415925, 3.1415925, ALU.max, ALU.min).then_inc(step, 1)
            dve.wait_ge(step, 8)
            dve.tensor_scalar(turns[:, :, :], angle[:, :, :], np.pi / 2, -TWO_PI, ALU.is_gt, ALU.mult).then_inc(step, 1)
            dve.wait_ge(step, 9)
            dve.scalar_tensor_tensor(out=turns[:, :, :], in0=angle[:, :, :], scalar=np.pi / 2, in1=turns[:, :, :],
                                     op0=ALU.add, op1=ALU.add).then_inc(step, 1)
            dve.wait_ge(step, 10)
            dve.tensor_scalar(turns[:, :, :], turns[:, :, :], -3.1415925, 3.1415925, ALU.max,
                              ALU.min).then_inc(shifted, 1)

        @block.scalar
        def _(act):
            act.wait_ge(shifted, 1)
            act.activation(table[:, :, 0, :], turns[:, :, :], ACT.Sin).then_inc(tables_made, 1)
            act.activation(table[:, :, 1, :], angle[:, :, :], ACT.Sin).then_inc(tables_made, 1)


class WeightSplitter:

    def __init__(self, nc, stack):
        self.nc, self.calls, self.before = nc, 0, 0
        sem = lambda name: stack.enter_context(nc.semaphore(name))
        self.w_in = [sem(f"w_in{j}") for j in range(2)]
        self.w_high, self.w_low = sem("w_high"), sem("w_low")

    def __call__(self, *jobs):
        nc, before = self.nc, self.before
        w_in, w_high, w_low = self.w_in, self.w_high, self.w_low
        pieces = []
        for src, high, low in jobs:
            n = src.shape[1]
            for c in range(0, n, 2048):
                pieces.append((src[:, c:min(n, c + 2048)], high[:, c:min(n, c + 2048)], low[:, c:min(n, c + 2048)]))
        with ExitStack() as ctx:
            stage = ctx.enter_context(nc.sbuf_tensor(f"w_stage{self.calls}", [P, 2, 2048], F32))
            block = ctx.enter_context(nc.Block())

            @block.sync
            def _(sp):
                for n, (src, _, _) in enumerate(pieces, before):
                    if n >= 2:
                        sp.wait_ge(w_low, n - 1)
                    sp.dma_start(stage[:, n % 2, 0:src.shape[1]], src).then_inc(w_in[n % 2], 16)

            @block.scalar
            def _(act):
                for n, (src, high, _) in enumerate(pieces, before):
                    act.wait_ge(w_in[n % 2], 16 * (n // 2 + 1))
                    act.activation(high, stage[:, n % 2, 0:src.shape[1]], ACT.Copy, scale=WSCALE).then_inc(w_high, 1)

            @block.vector
            def _(dve):
                for n, (src, high, low) in enumerate(pieces, before):
                    dve.wait_ge(w_high, n + 1)
                    dve.scalar_tensor_tensor(out=low, in0=stage[:, n % 2, 0:src.shape[1]], scalar=WSCALE, in1=high,
                                             op0=ALU.mult, op1=ALU.subtract).then_inc(w_low, 1)

        self.calls += 1
        self.before += len(pieces)


def attention0(nc, NT, x, ctxT, rope_dram, qnw, knw, g_xattn, wq, wk, wv, wo_dram, gate_dram, ident, X, y1, logits):
    USES = ("k0", "k1", "q0", "q1", "q2", "tk0", "q3", "tq0", "v0", "tq1", "v1", "tk1", "tq2", "tq3")
    USE = {name: n + 1 for n, name in enumerate(USES)}
    BANK = {name: n % 2 for n, name in enumerate(USES)}
    TURN = {name: n + 1 for n, name in enumerate(u for u in USES if u[0] == "t")}
    ROPED = ("k0", "k1", "q0", "q1", "q2", "q3")
    with ExitStack() as ctx:
        sb = lambda name, shape, dt=F32: ctx.enter_context(nc.sbuf_tensor(name, shape, dt))
        ps = lambda name, shape=[P, 512]: ctx.enter_context(nc.psum_tensor(name, shape, F32))
        sem = lambda name: ctx.enter_context(nc.semaphore("a0_" + name))

        wo = sb("wo0", [P, H0, D])
        gate = sb("gate0", [P, 2])
        tgate = sb("tgate0", [P, 1])
        half_neg = sb("half_neg0", [P, H0])
        qw = sb("qw0", [P, 2, HD0])
        kw = sb("kw0", [P, 2, HD0])
        xt = sb("xt0", [P, D])
        xres = sb("xres0", [P, D])
        xn = sb("xn0", [P, D])
        ctx32 = sb("ctx32", [P, DC, NB, S])
        raw = sb("raw0", [P, 3, 2, HALF])
        tab = sb("tab0", [P, 3, 2, 2, HALF])
        kv_hi = sb("kv_hi", [P, DC, 4, S], F16)
        kv_lo = sb("kv_lo", [P, DC, 4, S], F16)
        stats = sb("stats0", [P, 6])
        mv = sb("mv0", [P, 2])
        rstd = sb("rstd0", [P, 1])
        sq = sb("sq0", [P, 2, 512])
        ssk = sb("ssk", [P, NB * KV0])
        ssq = sb("ssq", [P, H0])
        rk = sb("rk", [P, NB * KV0])
        rq = sb("rq", [P, H0])
        rqT = sb("rqT", [P, NB, H0 // 2])
        k1 = sb("k1", [P, NB, KV0 * HD0])
        k2 = sb("k2", [P, NB, KV0 * HD0])
        q1 = sb("q1", [P, H0 * HD0])
        q2 = sb("q2", [P, H0 * HD0])
        qT = sb("qT0", [P, NB, H0, S])
        kT = sb("kT0", [P, NB, KV0, P])
        v = sb("v0", [P, NB, KV0 * HD0])
        E = sb("E0", [P, 2, 2, P])
        PT = sb("PT0", [P, 2, 2, P])
        mx = sb("mx0", [P, 2, 2])
        nb = sb("nb0", [P, 2, 2])
        es = sb("es0", [P, 2, 2])
        er = sb("er0", [P, 2, 2])
        attnT = sb("attnT0", [P, H0, NB, S])

        stats_y = sb("stats_y0", [P, 6])
        mv_y = sb("mv_y0", [P, 2])
        rstd_y = sb("rstd_y0", [P, 1])
        yn = sb("yn0", [P, D])
        ynT = sb("ynT0", [P, D])
        router = sb("router0", [P, DC, E0])
        eps_q = sb("eps_q", [P, H0])
        eps_ln = sb("eps_ln0", [P, 1])

        proj = [ps("proj0"), ps("proj1")]
        turnA = ps("turnA")
        score = [ps("score0"), ps("score1")]
        turnB = [ps("turnB0"), ps("turnB1")]
        outp = ps("outp0")

        x_in, ctx_in, raw_in, xres_in, y1_out, const_in = map(sem, (
            "x_in", "ctx_in", "raw_in", "xres_in", "y1_out", "const_in"))
        pe_xT = sem("pe_xT")
        pe_proj = sem("pe_proj")
        pe_rq = sem("pe_rq")
        pe_score = sem("pe_score")
        pe_PT = sem("pe_PT")
        pe_out = sem("pe_out")
        pe_yT = sem("pe_yT")
        pe_gate = sem("pe_gate")
        dv_y = sem("dv_y")
        dv_gate = sem("dv_gate")
        dv_ln = sem("dv_ln")
        dv_stats = sem("dv_stats")
        dv_xlo = sem("dv_xlo")
        dv_rope = sem("dv_rope")
        dv_ss = sem("dv_ss")
        dv_max = sem("dv_max")
        dv_norm = sem("dv_norm")
        dv_x1 = sem("dv_x1")
        ac_xhi = sem("ac_xhi")
        ac_sq = sem("ac_sq")
        ac_v = sem("ac_v")
        ac_turn = sem("ac_turn")
        ac_rq = sem("ac_rq")
        ac_exp = sem("ac_exp")
        ac_PT = sem("ac_PT")
        ac_out = sem("ac_out")
        ac_yT = sem("ac_yT")
        po_y = sem("po_y")
        po_rstd = sem("po_rstd")
        po_clo = sem("po_clo")
        po_tab = sem("po_tab")
        po_add = sem("po_add")
        po_r = sem("po_r")
        po_const = sem("po_const")
        dv_const = sem("dv_const")
        dv_turn = sem("dv_turn")
        ac_const = sem("ac_const")
        block = ctx.enter_context(nc.Block())

        @block.sync
        def _(sp):
            for dst, src in ((wo[:, :, :], wo_dram.rearrange("p (h d) -> p h d", h=H0)),
                             (router[:, :, :], gate_dram.rearrange("p (c e) -> p c e", c=DC)),
                             (gate[:, :], g_xattn.partition_broadcast(P)),
                             (qw[:, 0, :], qnw.partition_broadcast(P)), (kw[:, 0, :], knw.partition_broadcast(P)),
                             (qw[:, 1, 0:HALF], qnw[HALF:].partition_broadcast(P)),
                             (qw[:, 1, HALF:], qnw[0:HALF].partition_broadcast(P)),
                             (kw[:, 1, 0:HALF], knw[HALF:].partition_broadcast(P)),
                             (kw[:, 1, HALF:], knw[0:HALF].partition_broadcast(P))):
                sp.dma_start(dst, src).then_inc(const_in, 16)
            for s in (x_in, ctx_in, raw_in, xres_in, y1_out):
                sp.sem_inc(s, 16)

            def load(t):
                sp.wait_ge(dv_ln, last(2, t, 2))
                sp.dma_start(xt[:, :], x[bass.ds(t * P, P), :]).then_inc(x_in, 16)
                sp.wait_ge(po_clo, last(1, t, 1))
                sp.dma_start(ctx32[:, :, :, :], ctxT[:, bass.ds(t * D, D)]
                             .rearrange("p (c b s) -> p c b s", c=DC, b=NB)).then_inc(ctx_in, 16)
                sp.wait_ge(po_tab, last(6, t, 6))
                r = rope_dram[bass.ds(t * P, P), :].rearrange("(b s) (o a d) -> b s o a d", b=NB, o=2, a=2)
                for h in range(NB):
                    sp.dma_start(raw[h * S:(h + 1) * S, 0, :, :], r[h, :, 0, :, :]).then_inc(raw_in, 16)
                    context, own = (slice(0, S), slice(S, P))[::1 - 2 * h]
                    sp.dma_start(raw[context, 1 + h, :, :], r[h, :, 1, :, :]).then_inc(raw_in, 16)
                    sp.dma_start(raw[own, 1 + h, :, :], r[h, :, 0, :, :]).then_inc(raw_in, 16)

            def load_res(p):
                sp.wait_ge(dv_x1, last(1, p, 1))
                sp.dma_start(xres[:, :], x[bass.ds(p * P, P), :]).then_inc(xres_in, 16)

            def store(c):
                sp.wait_ge(dv_y, this(2, c, 2))
                sp.dma_start(y1[bass.ds(c * P, P), :], yn[:, :]).then_inc(y1_out, 16)

            load(0)
            load_res(0)
            load(1)
            load(2)
            with sp.Fori(0, NT - 3) as c:
                store(c)
                load_res(c + 1)
                load(c + 3)
            for c in range(NT - 3, NT):
                store(c)
                if c + 1 < NT:
                    load_res(c + 1)
            sp.wait_ge(y1_out, 16 * (NT + 1))

        @block.gpsimd
        def _(pool):
            pool.memset(half_neg[:, :], -0.5).then_inc(po_const, 1)
            pool.memset(eps_q[:, :], EPS_RMS * WSCALE**2 * HD0).then_inc(po_const, 1)
            pool.memset(eps_ln[:, :], EPS_LN).then_inc(po_const, 1)
            for s, n in ((po_y, 2), (po_rstd, 2), (po_clo, 1), (po_tab, 6), (po_add, 8), (po_r, 6)):
                pool.sem_inc(s, n)
            pool.wait_ge(po_const, 3)

            def part_a(t):
                pool.wait_ge(dv_ln, this(2, t, 1))
                pool.tensor_tensor(rstd[:, :], mv[:, 1:2], eps_ln[:, :], ALU.add).then_inc(po_rstd, 1)
                pool.wait_ge(po_rstd, this(2, t, 1))
                pool.tensor_tensor(rstd[:, :], rstd[:, :], half_neg[:, 0:1], ALU.pow).then_inc(po_rstd, 1)

            def part_a2(t):
                pool.wait_ge(ac_xhi, this(2, t, 1))
                pool.wait_ge(ctx_in, this(16, t, 16))
                pool.tensor_tensor(kv_lo[:, :, 0::3, :], ctx32[:, :, :, :], kv_hi[:, :, 0::3, :],
                                   ALU.subtract).then_inc(po_clo, 1)
                pool.wait_ge(raw_in, 96 * t + 16 + 96)
                pool.wait_ge(dv_rope, last(6, t, 6))
                for n in range(3):
                    w = qw if n == 0 else kw
                    pool.tensor_tensor(tab[:, n, 0, :, :], raw[:, n, 0:1, :].broadcast_to([P, 2, HALF]),
                                       w[:, 0, :].rearrange("p (a d) -> p a d", a=2), ALU.mult).then_inc(po_tab, 1)
                    pool.tensor_tensor(tab[:, n, 1, :, :], raw[:, n, 1:2, :].broadcast_to([P, 2, HALF]),
                                       w[:, 1, :].rearrange("p (a d) -> p a d", a=2), ALU.mult).then_inc(po_tab, 1)

            def part_a3(t):
                for b in range(NB):
                    pool.wait_ge(dv_rope, this(6, t, b + 1))
                    pool.tensor_tensor(k1[:, b, :], k1[:, b, :], k2[:, b, :], ALU.add).then_inc(po_add, 1)
                    pool.wait_ge(dv_ss, this(6, t, b + 1))
                    part = slice(b * KV0, (b + 1) * KV0)
                    pool.tensor_tensor(rk[:, part], ssk[:, part], eps_q[:, 0:KV0], ALU.add).then_inc(po_r, 1)
                    pool.wait_ge(po_r, this(6, t, 2 * b + 1))
                    pool.tensor_tensor(rk[:, part], rk[:, part], half_neg[:, 0:KV0], ALU.pow).then_inc(po_r, 1)
                    pool.wait_ge(po_r, this(6, t, 2 * b + 2))
                    pool.wait_ge(po_add, this(8, t, 2 * b + 1))
                    kb = k1[:, b, :].rearrange("p (h d) -> p h d", h=KV0)
                    r = rk[:, part].unsqueeze(2).broadcast_to([P, KV0, HD0])
                    pool.tensor_tensor(kb, kb, r, ALU.mult).then_inc(po_add, 1)
                for j in range(4):
                    pool.wait_ge(dv_rope, this(6, t, 3 + j))
                    part = slice(512 * j, 512 * (j + 1))
                    pool.tensor_tensor(q1[:, part], q1[:, part], q2[:, part], ALU.add).then_inc(po_add, 1)
                pool.wait_ge(dv_ss, this(6, t, 6))
                pool.tensor_tensor(rq[:, :], ssq[:, :], eps_q[:, :], ALU.add).then_inc(po_r, 1)
                pool.wait_ge(po_r, this(6, t, 5))
                pool.tensor_tensor(rq[:, :], rq[:, :], half_neg[:, :], ALU.pow).then_inc(po_r, 1)

            def part_c(p):
                pool.wait_ge(dv_y, this(2, p, 1))
                pool.tensor_tensor(rstd_y[:, :], mv_y[:, 1:2], eps_ln[:, :], ALU.add).then_inc(po_y, 1)
                pool.wait_ge(po_y, this(2, p, 1))
                pool.tensor_tensor(rstd_y[:, :], rstd_y[:, :], half_neg[:, 0:1], ALU.pow).then_inc(po_y, 1)

            pool.wait_ge(const_in, 16 * 9)
            for w in (qw, kw):
                pool.tensor_scalar(w[:, 1, 0:HALF], w[:, 1, 0:HALF], -1.0, None, ALU.mult).then_inc(po_const, 1)
            pool.wait_ge(po_const, 5)
            def iteration(t, p, c):
                if t is not None:
                    part_a(t)
                    part_a2(t)
                if c is not None:
                    part_c(c)
                if t is not None:
                    part_a3(t)

            iteration(0, None, None)
            iteration(1, None, None)
            with pool.Fori(0, NT - 2) as c:
                iteration(c + 2, None, c)
            iteration(None, None, NT - 2)
            iteration(None, None, NT - 1)

        @block.tensor
        def _(pe):
            for s, n in ((pe_xT, 1), (pe_proj, 14), (pe_rq, 1), (pe_score, 8), (pe_PT, 8), (pe_out, 9), (pe_yT, 1), (pe_gate, 1)):
                pe.sem_inc(s, n)
            pe.wait_ge(const_in, 16 * 9)

            def x_turn(t):
                pe.wait_ge(dv_ln, this(2, t, 2))
                pe.wait_ge(ac_rq, last(1, t, 1))
                for c in range(DC):
                    i = pe.transpose(turnA[:, c * P:(c + 1) * P], xn[:, c * P:(c + 1) * P], ident[:, :])
                i.then_inc(pe_xT, 1)

            def mm3(out, left, right):
                steps = [(c, a, b) for c in range(DC) for a, b in ((0, 0), (0, 1), (1, 0))]
                for n, (c, a, b) in enumerate(steps):
                    i = pe.matmul(out, left(c, a), right(c, b), start=(n == 0), stop=(n == len(steps) - 1))
                return i

            kv = (kv_hi, kv_lo)

            def wait_bank(t, name):
                n = USES.index(name) - 2
                before = USES[n]
                if n < 0:
                    pe.wait_ge(ac_turn, last(6, t, TURN[before]))
                elif before in ROPED:
                    pe.wait_ge(dv_rope, this(6, t, ROPED.index(before) + 1))
                    pe.wait_ge(ac_sq, this(6, t, ROPED.index(before) + 1))
                elif before[0] == "v":
                    pe.wait_ge(ac_v, this(2, t, int(before[1]) + 1))
                else:
                    pe.wait_ge(ac_turn, this(6, t, TURN[before]))

            def project(t, name):
                if name == "k0":
                    pe.wait_ge(po_clo, this(1, t, 1))
                    pe.wait_ge(dv_xlo, this(1, t, 1))
                    pe.wait_ge(ac_xhi, this(2, t, 2))
                wait_bank(t, name)
                kind, n = name[0], int(name[1])
                tokens = slice(1, 3) if kind == "q" else slice(2 * n, 2 * n + 2)
                w = {"q": wq, "k": wk, "v": wv}[kind]
                at = lambda c: c * 2048 + n * 512 if kind == "q" else c * 512
                mm3(proj[BANK[name]][:, :], lambda c, a: kv[a][:, c, tokens, :],
                    lambda c, a: w[a][:, at(c):at(c) + 512]).then_inc(pe_proj, 1)

            def turn(t, name):
                n = int(name[2])
                pe.wait_ge(po_add, this(8, t, 2 * n + 2 if name[1] == "k" else 5 + n))
                wait_bank(t, name)
                for g in range(4):
                    y = k1[:, n, g * HD0:(g + 1) * HD0] if name[1] == "k" else q1[:, (4 * n + g) * HD0:(4 * n + g + 1) * HD0]
                    i = pe.transpose(proj[BANK[name]][:, g * P:(g + 1) * P], y, ident[:, :])
                i.then_inc(pe_proj, 1)

            def move_rq(t, c):
                pe.wait_ge(po_r, this(6, t, 6))
                if c is not None:
                    pe.wait_ge(dv_gate, this(1, c, 1))
                pe.wait_ge(dv_xlo, this(1, t, 1))
                pe.wait_ge(ac_xhi, this(2, t, 2))
                r = rq[:, :].rearrange("p (m j) -> p j m", j=2)
                for j in range(2):
                    for b in range(NB):
                        i = pe.matmul(turnA[j * S:(j + 1) * S, b * 8:(b + 1) * 8], ident[:, b * S:(b + 1) * S],
                                      r[:, j, :], start=True, stop=True)
                i.then_inc(pe_rq, 1)

            def scores(p, u):
                b, g = divmod(u, KV0)
                if u < 4:
                    pe.wait_ge(ac_turn, this(6, p, TURN[f"tq{g}"]))
                pe.wait_ge(ac_exp, this(8, p, u - 1) if u >= 2 else last(8, p, 7 + u))
                for m in range(2):
                    h = GROUP * g + 2 * m
                    i = pe.matmul(score[u % 2][:, m * P:(m + 1) * P], qT[:, b, h:h + 2, :], kT[:, b, g, :],
                                  start=True, stop=True)
                i.then_inc(pe_score, 1)

            def turn_P(p, u):
                pe.wait_ge(dv_norm, this(16, p, 2 * u + 2))
                pe.wait_ge(ac_PT, this(8, p, u - 1) if u >= 2 else last(8, p, 7 + u))
                for m in range(2):
                    i = pe.transpose(turnB[u % 2][:, m * P:(m + 1) * P], E[:, u % 2, m, :], ident[:, :])
                i.then_inc(pe_PT, 1)

            def weigh_v(p, u, c):
                b, g = divmod(u, KV0)
                pe.wait_ge(ac_PT, this(8, p, u + 1))
                if u == 0:
                    if c is not None:
                        pe.wait_ge(dv_x1, this(1, c, 1))
                    pe.wait_ge(ac_v, this(2, p, 2))
                else:
                    pe.wait_ge(ac_out, this(8, p, u))
                pe.matmul(outp[:, 0:256], v[:, b, g * HD0:(g + 1) * HD0], PT[:, u % 2, :, :], start=True,
                          stop=True).then_inc(pe_out, 1)

            def out_projection(p, heads):
                pe.wait_ge(ac_out, this(8, p, 8))
                for h in heads:
                    i = pe.matmul(outp[:, 0:D], attnT[:, h, :, :], wo[:, h, :], start=(h == 0), stop=(h == H0 - 1))
                if h == H0 - 1:
                    i.then_inc(pe_out, 1)

            def y_turn(c, t):
                pe.wait_ge(dv_y, this(2, c, 2))
                if t is not None:
                    pe.wait_ge(dv_xlo, this(1, t, 1))
                for k in range(DC):
                    i = pe.transpose(turnA[:, k * P:(k + 1) * P], yn[:, k * P:(k + 1) * P], ident[:, :])
                i.then_inc(pe_yT, 1)

            def route(c):
                pe.wait_ge(ac_yT, this(1, c, 1))
                for k in range(DC):
                    i = pe.matmul(turnA[:, 0:E0], ynT[:, k * P:(k + 1) * P], router[:, k, :], start=(k == 0),
                                  stop=(k == DC - 1))
                i.then_inc(pe_gate, 1)

            def iteration(t, p, c):
                if p is not None:
                    scores(p, 0)
                    scores(p, 1)
                if c is not None:
                    out_projection(c, range(H0 // 2))
                if t is not None:
                    x_turn(t)
                if c is not None:
                    out_projection(c, range(H0 // 2, H0))
                for u, (block, turned) in enumerate((
                        ("k0", None), ("k1", None), ("q0", None), ("q1", None), ("q2", "tk0"), ("q3", "tq0"),
                        ("v0", "tq1"), ("v1", "tk1"))):
                    if p is not None:
                        turn_P(p, u)
                        if u + 2 < 8:
                            scores(p, u + 2)
                    if t is not None:
                        project(t, block)
                    if p is not None:
                        weigh_v(p, u, c)
                    if t is not None and turned:
                        turn(t, turned)
                    if c is not None and u == 3:
                        y_turn(c, t)
                    if c is not None and u == 5:
                        route(c)
                if t is not None:
                    move_rq(t, c)
                    turn(t, "tq2")
                    turn(t, "tq3")

            iteration(0, None, None)
            iteration(1, 0, None)
            with pe.Fori(0, NT - 2) as c:
                iteration(c + 2, c + 1, c)
            iteration(None, NT - 1, NT - 2)
            iteration(None, None, NT - 1)

        @block.vector
        def _(dve):
            for s, n in ((dv_ln, 2), (dv_xlo, 1), (dv_rope, 6), (dv_ss, 6), (dv_max, 16), (dv_norm, 16), (dv_x1, 1), (dv_y, 2), (dv_gate, 1)):
                dve.sem_inc(s, n)

            def layernorm(t):
                dve.sem_clear(dv_stats)
                dve.wait_ge(x_in, this(16, t, 16))
                dve.bn_stats(stats[:, :], xt[:, :]).then_inc(dv_stats, 1)
                dve.wait_ge(dv_stats, 1)
                dve.bn_aggr(mv[:, :], stats[:, :]).then_inc(dv_ln, 1)
                dve.wait_ge(po_rstd, this(2, t, 2))
                dve.wait_ge(pe_xT, last(1, t, 1))
                dve.tensor_scalar(xn[:, :], xt[:, :], mv[:, 0:1], rstd[:, 0:1], ALU.subtract,
                                  ALU.mult).then_inc(dv_ln, 1)

            def low_x(t):
                dve.wait_ge(ac_xhi, this(2, t, 2))
                dve.tensor_tensor(kv_lo[:, :, 1:3, :], turnA[:, 0:D].rearrange("p (c b s) -> p c b s", c=DC, b=NB),
                                  kv_hi[:, :, 1:3, :], ALU.subtract).then_inc(dv_xlo, 1)

            def rope(t, n):
                dve.wait_ge(pe_proj, this(14, t, USE[ROPED[n]]))
                if n == 0:
                    dve.wait_ge(po_tab, this(6, t, 6))
                    dve.wait_ge(pe_proj, last(14, t, 14))
                which = 0 if n >= 2 else 1 + n
                if n < 2:
                    o1, o2 = k1[:, n, :], k2[:, n, :]
                else:
                    part = slice(512 * (n - 2), 512 * (n - 1))
                    o1, o2 = q1[:, part], q2[:, part]
                y = proj[BANK[ROPED[n]]][:, :].rearrange("p (h a d) -> p h a d", a=2, d=HALF)
                shape = [P, 4, 2, HALF]
                cos, sin = (tab[:, which, s:s + 1, :, :].broadcast_to(shape) for s in range(2))
                dve.tensor_tensor(o1.rearrange("p (h a d) -> p h a d", a=2, d=HALF), y, cos, ALU.mult)
                dve.tensor_tensor(o2.rearrange("p (h a d) -> p h a d", a=2, d=HALF), y[:, :, ::-1, :], sin,
                                  ALU.mult).then_inc(dv_rope, 1)

            def sum_squares(t, n):
                ss = ssk[:, n * KV0:(n + 1) * KV0] if n < 2 else ssq[:, 4 * (n - 2):4 * (n - 1)]
                dve.wait_ge(ac_sq, this(6, t, n + 1))
                if n == 2:
                    dve.wait_ge(po_r, last(6, t, 6))
                dve.tensor_reduce(ss, sq[:, n % 2, :].rearrange("p (h d) -> p h d", h=4), AX_X,
                                  ALU.add).then_inc(dv_ss, 1)

            def maximum(p, u):
                b, g = divmod(u, KV0)
                dve.wait_ge(pe_score, this(8, p, u + 1))
                dve.tensor_reduce(mx[:, u % 2, :], score[u % 2][:, 0:256].rearrange("p (m k) -> p m k", m=2), AX_X,
                                  ALU.max).then_inc(dv_max, 1)
                dve.wait_ge(dv_max, this(16, p, 2 * u + 1))
                if u == 0:
                    dve.wait_ge(ac_rq, this(1, p, 1))
                dve.wait_ge(ac_exp, this(8, p, u - 1) if u >= 2 else last(8, p, 7 + u))
                dve.scalar_tensor_tensor(out=nb[:, u % 2, :], in0=mx[:, u % 2, :], scalar=-1.0,
                                         in1=rqT[:, b, 2 * g:2 * g + 2], op0=ALU.mult,
                                         op1=ALU.mult).then_inc(dv_max, 1)

            def normalize(p, u):
                dve.wait_ge(ac_exp, this(8, p, u + 1))
                dve.reciprocal(er[:, u % 2, :], es[:, u % 2, :]).then_inc(dv_norm, 1)
                dve.wait_ge(dv_norm, this(16, p, 2 * u + 1))
                dve.tensor_tensor(E[:, u % 2, :, :], E[:, u % 2, :, :],
                                  er[:, u % 2, :].unsqueeze(2).broadcast_to([P, 2, P]), ALU.mult).then_inc(dv_norm, 1)

            def residual(p):
                dve.wait_ge(pe_out, this(9, p, 9))
                dve.wait_ge(xres_in, this(16, p, 16))
                x1 = X[:, bass.ds(p, 1), :].rearrange("p o d -> p (o d)")
                dve.scalar_tensor_tensor(out=x1, in0=outp[:, 0:D], scalar=tgate[:, 0:1], in1=xres[:, :],
                                         op0=ALU.mult, op1=ALU.add).then_inc(dv_x1, 1)
                dve.sem_clear(dv_stats)
                dve.wait_ge(dv_x1, this(1, p, 1))
                dve.sem_inc(dv_turn, 1)
                dve.bn_stats(stats_y[:, :], x1).then_inc(dv_stats, 1)
                dve.wait_ge(dv_stats, 1)
                dve.bn_aggr(mv_y[:, :], stats_y[:, :]).then_inc(dv_y, 1)

            def standard_y(p):
                dve.wait_ge(po_y, this(2, p, 2))
                dve.wait_ge(pe_yT, last(1, p, 1))
                dve.wait_ge(y1_out, last(16, p, 16))
                dve.tensor_scalar(yn[:, :], X[:, bass.ds(p, 1), :].rearrange("p o d -> p (o d)"), mv_y[:, 0:1], rstd_y[:, 0:1], ALU.subtract,
                                  ALU.mult).then_inc(dv_y, 1)

            def keep_logits(c):
                dve.wait_ge(pe_gate, this(1, c, 1))
                dve.tensor_scalar(logits[:, bass.ds(c * E0, E0)], turnA[:, 0:E0], 1.0, None,
                                  ALU.mult).then_inc(dv_gate, 1)

            def iteration(t, p, c):
                if t is not None:
                    layernorm(t)
                if p is not None:
                    maximum(p, 0)
                    maximum(p, 1)
                if t is not None:
                    low_x(t)
                if p is not None:
                    normalize(p, 0)
                if c is not None:
                    residual(c)
                for u in range(8):
                    if p is not None and u + 2 < 8:
                        maximum(p, u + 2)
                    if p is not None and u + 1 < 8:
                        normalize(p, u + 1)
                    if t is not None and 1 <= u < 7:
                        sum_squares(t, u - 1)
                    if t is not None and u < 6:
                        rope(t, u)
                    if c is not None and u == 0:
                        standard_y(c)
                if c is not None:
                    keep_logits(c)

            dve.wait_ge(ac_const, 1)
            iteration(0, None, None)
            iteration(1, 0, None)
            with dve.Fori(0, NT - 2) as c:
                iteration(c + 2, c + 1, c)
            iteration(None, NT - 1, NT - 2)
            iteration(None, None, NT - 1)

        @block.scalar
        def _(act):
            for s, n in ((ac_xhi, 2), (ac_sq, 6), (ac_v, 2), (ac_turn, 6), (ac_rq, 1), (ac_exp, 8), (ac_PT, 8),
                         (ac_out, 8), (ac_yT, 1)):
                act.sem_inc(s, n)
            act.wait_ge(const_in, 16 * 9)
            act.activation(tgate[:, :], gate[:, 0:1], ACT.Tanh).then_inc(ac_const, 1)

            def high_context(t):
                act.wait_ge(ctx_in, this(16, t, 16))
                act.wait_ge(pe_proj, last(14, t, USE["v1"]))
                act.activation(kv_hi[:, :, 0::3, :], ctx32[:, :, :, :], ACT.Copy).then_inc(ac_xhi, 1)

            def high_x(t):
                act.wait_ge(pe_xT, this(1, t, 1))
                act.activation(kv_hi[:, :, 1:3, :], turnA[:, 0:D].rearrange("p (c b s) -> p c b s", c=DC, b=NB),
                               ACT.Copy).then_inc(ac_xhi, 1)

            def squares(t, n):
                act.wait_ge(pe_proj, this(14, t, USE[ROPED[n]]))
                act.wait_ge(dv_rope, this(6, t, n + 1))
                act.wait_ge(dv_ss, this(6, t, n - 1) if n >= 2 else last(6, t, 5 + n))
                act.activation(sq[:, n % 2, :], proj[BANK[ROPED[n]]][:, :], ACT.Square).then_inc(ac_sq, 1)

            def values(t, b):
                act.wait_ge(pe_proj, this(14, t, USE[f"v{b}"]))
                act.activation(v[:, b, :], proj[BANK[f"v{b}"]][:, :], ACT.Copy, scale=1.0 / WSCALE).then_inc(ac_v, 1)

            def turned(t, name):
                n, y = int(name[2]), proj[BANK[name]]
                act.wait_ge(pe_proj, this(14, t, USE[name]))
                if name[1] == "k":
                    act.activation(kT[:, n, :, :], y[:, :].rearrange("p (g k) -> p g k", g=KV0),
                                   ACT.Copy).then_inc(ac_turn, 1)
                else:
                    act.activation(qT[:, :, 4 * n:4 * n + 4, :].rearrange("p b h s -> p h b s"),
                                   y[:, :].rearrange("p (h b s) -> p h b s", h=4, b=NB), ACT.Copy).then_inc(ac_turn, 1)

            def moved_rq(t):
                act.wait_ge(pe_rq, this(1, t, 1))
                act.activation(rqT[:, :, :], turnA[:, 0:16].rearrange("p (b m) -> p b m", b=NB),
                               ACT.Copy, scale=HD0**0.5).then_inc(ac_rq, 1)

            def exponentials(p, u):
                b, g = divmod(u, KV0)
                act.wait_ge(dv_max, this(16, p, 2 * u + 2))
                act.wait_ge(pe_PT, this(8, p, u - 1) if u >= 2 else last(8, p, 7 + u))
                for m in range(2):
                    i = act.activation(E[:, u % 2, m, :], score[u % 2][:, m * P:(m + 1) * P], ACT.Exp,
                                       bias=nb[:, u % 2, m:m + 1], scale=rqT[:, b, 2 * g + m:2 * g + m + 1],
                                       accum_out=es[:, u % 2, m:m + 1])
                i.then_inc(ac_exp, 1)

            def turned_P(p, u):
                act.wait_ge(pe_PT, this(8, p, u + 1))
                act.wait_ge(pe_out, this(9, p, u - 1) if u >= 2 else last(9, p, 7 + u))
                act.activation(PT[:, u % 2, :, :], turnB[u % 2][:, 0:256].rearrange("p (m q) -> p m q", m=2),
                               ACT.Copy).then_inc(ac_PT, 1)

            def turned_out(p, u):
                b, g = divmod(u, KV0)
                act.wait_ge(pe_out, this(9, p, u + 1))
                act.activation(attnT[:, GROUP * g:GROUP * (g + 1), b, :],
                               outp[:, 0:256].rearrange("p (h s) -> p h s", h=GROUP), ACT.Copy).then_inc(ac_out, 1)

            def turned_y(c):
                act.wait_ge(pe_yT, this(1, c, 1))
                act.wait_ge(pe_gate, last(1, c, 1))
                act.activation(ynT[:, :], turnA[:, 0:D], ACT.Copy).then_inc(ac_yT, 1)

            def iteration(t, p, c):
                if t is not None:
                    high_context(t)
                if p is not None:
                    exponentials(p, 0)
                    exponentials(p, 1)
                if t is not None:
                    high_x(t)
                for u in range(8):
                    if p is not None:
                        turned_P(p, u)
                        if u + 2 < 8:
                            exponentials(p, u + 2)
                        turned_out(p, u)
                    if t is not None and u < 6:
                        squares(t, u)
                    if t is not None and u >= 6:
                        values(t, u - 6)
                    if t is not None and u >= 4:
                        turned(t, ("tk0", "tq0", "tq1", "tk1")[u - 4])
                    if c is not None and u == 3:
                        turned_y(c)
                if t is not None:
                    moved_rq(t)
                    turned(t, "tq2")
                    turned(t, "tq3")

            iteration(0, None, None)
            iteration(1, 0, None)
            with act.Fori(0, NT - 2) as c:
                iteration(c + 2, c + 1, c)
            iteration(None, NT - 1, NT - 2)
            iteration(None, None, NT - 1)


class Chain:

    def __init__(self, engine, semaphore):
        self.engine, self.semaphore, self.steps = engine, semaphore, 0

    def __call__(self, instruction):
        self.steps += 1
        instruction.then_inc(self.semaphore, 1)
        self.engine.wait_ge(self.semaphore, self.steps)


def top2(dve, chain, values, order, hot, best, t, m):
    shape = list(values.shape)
    wide = lambda y: y.unsqueeze(2).broadcast_to(shape)
    for slot in range(2):
        chain(dve.tensor_reduce(best[:, slot, :], values, AX_X, ALU.max))
        chain(dve.tensor_tensor(t, values, wide(best[:, slot, :]), ALU.is_equal))
        chain(dve.tensor_tensor(t, t, order, ALU.mult))
        chain(dve.tensor_reduce(m, t, AX_X, ALU.max))
        chain(dve.tensor_tensor(hot[:, slot, :, :], t, wide(m), ALU.is_equal))
        if slot == 0:
            chain(dve.scalar_tensor_tensor(out=values, in0=hot[:, 0, :, :], scalar=-1e30, in1=values, op0=ALU.mult,
                                           op1=ALU.add))


def route0(nc, NT, J, logits, consts, dest, weight, expert, index):
    B = 2 * NT
    with ExitStack() as ctx:
        sb = lambda name, shape, dt=F32: ctx.enter_context(nc.sbuf_tensor(name, shape, dt))
        sem = lambda name: ctx.enter_context(nc.semaphore("r0_" + name))
        hot = sb("r0_hot", [P, 2, NT, E0])
        hot16 = sb("r0_hot16", [P, B * E0], F16)
        best = sb("r0_best", [P, 2, NT])
        t = sb("r0_t", [P, NT, E0])
        m = sb("r0_m", [P, NT])
        diff = sb("r0_diff", [P, NT])
        zero = sb("r0_zero", [P, B])
        upto = sb("r0_upto", [P, E0, B])
        row = sb("r0_row", [P, B, E0])
        tiles = sb("r0_tiles", [P, E0])
        end = sb("r0_end", [P, E0])
        base = sb("r0_base", [P, E0])
        behind = sb("r0_behind", [P, J, E0])
        expf = sb("r0_expf", [P, J])
        rowf = sb("r0_rowf", [P, B])
        tile_of = sb("r0_tile_of", [P, B])
        place_of = sb("r0_place_of", [P, B])
        here = sb("r0_here", [P, 2, 4, P])
        token = sb("r0_token", [P, 2, 4, J])
        rank = ctx.enter_context(nc.psum_tensor("r0_rank", [P, B * E0], F32))
        total = ctx.enter_context(nc.psum_tensor("r0_total", [P, B * E0], F32))
        table = ctx.enter_context(nc.psum_tensor("r0_table", [P, 512], F32))
        dv_step, dv_hot, dv_diff, ac_exp, pe_count, dv_dest, dv_pick, pe_pick = map(sem, (
            "dv_step", "dv_hot", "dv_diff", "ac_exp", "pe_count", "dv_dest", "dv_pick", "pe_pick"))
        block = ctx.enter_context(nc.Block())
        order = consts["order"][:, 0:E0].unsqueeze(1).broadcast_to([P, NT, E0])

        @block.vector
        def _(dve):
            chain = Chain(dve, dv_step)
            values = logits[:, :].rearrange("p (t e) -> p t e", e=E0)
            top2(dve, chain, values, order, hot, best, t[:, :, :], m[:, :])
            dve.tensor_copy(hot16[:, :], hot[:, :, :, :].rearrange("p k t e -> p (k t e)")).then_inc(dv_hot, 1)
            dve.tensor_tensor(diff[:, :], best[:, 1, :], best[:, 0, :], ALU.subtract).then_inc(dv_diff, 1)
            dve.wait_ge(ac_exp, 1)
            chain(dve.tensor_scalar(m[:, :], diff[:, :], 1.0, None, ALU.add))
            chain(dve.reciprocal(weight[:, 0, :], m[:, :]))
            chain(dve.tensor_tensor(weight[:, 1, :], weight[:, 0, :], diff[:, :], ALU.mult))
            chain(dve.memset(zero[:, :], 0.0))
            dve.wait_ge(pe_count, 2)
            counts = total[:, :].rearrange("p (b e) -> p e b", e=E0)
            for e in range(E0):
                i = dve.tensor_tensor_scan(upto[:, e, :], counts[:, e, :], zero[:, :], 0.0, ALU.add, ALU.add)
            chain(i)
            chain(dve.tensor_scalar(tiles[:, :], upto[:, :, B - 1], 1.0 / P, (P - 1) / P - 0.5 + 0.5 / P, ALU.mult,
                                    ALU.add))
            chain(dve.tensor_scalar(tiles[:, :], tiles[:, :], ROUND, -ROUND, ALU.add, ALU.add))
            chain(dve.tensor_tensor_scan(end[:, :], tiles[:, :], zero[:, 0:E0], 0.0, ALU.add, ALU.add))
            chain(dve.tensor_tensor(base[:, :], end[:, :], tiles[:, :], ALU.subtract))
            chain(dve.tensor_scalar(base[:, :], base[:, :], float(P), None, ALU.mult))
            chain(dve.tensor_tensor(row[:, :, :], upto[:, :, :].rearrange("p e b -> p b e"),
                                    total[:, :].rearrange("p (b e) -> p b e", e=E0), ALU.subtract))
            chain(dve.tensor_tensor(row[:, :, :], row[:, :, :], rank[:, :].rearrange("p (b e) -> p b e", e=E0), ALU.add))
            chain(dve.tensor_tensor(row[:, :, :], row[:, :, :], base[:, :].unsqueeze(1).broadcast_to([P, B, E0]),
                                    ALU.add))
            chain(dve.tensor_tensor(row[:, :, :], row[:, :, :], hot[:, :, :, :].rearrange("p k t e -> p (k t) e"),
                                    ALU.mult))
            chain(dve.tensor_reduce(rowf[:, :], row[:, :, :], AX_X, ALU.add))
            chain(dve.tensor_copy(dest[:, :, :].rearrange("p k t -> p (k t)"), rowf[:, :]))
            chain(dve.tensor_tensor(behind[:, :, :], end[:, :].unsqueeze(1).broadcast_to([P, J, E0]),
                                    consts["count"][:, 0:J].unsqueeze(2).broadcast_to([P, J, E0]), ALU.is_le))
            chain(dve.tensor_reduce(expf[:, :], behind[:, :, :], AX_X, ALU.add))
            chain(dve.tensor_scalar(expf[:, :], expf[:, :], E0 - 1.0, None, ALU.min))
            chain(dve.tensor_copy(expert[:, :], expf[:, :]))
            chain(dve.tensor_scalar(tile_of[:, :], rowf[:, :], 1.0 / P, -0.5 + 0.5 / P, ALU.mult, ALU.add))
            chain(dve.tensor_scalar(tile_of[:, :], tile_of[:, :], ROUND, -ROUND, ALU.add, ALU.add))
            chain(dve.scalar_tensor_tensor(out=place_of[:, :], in0=tile_of[:, :], scalar=-float(P), in1=rowf[:, :],
                                           op0=ALU.mult, op1=ALU.add))
            dve.sem_inc(dv_pick, 2)
            dve.sem_inc(dv_dest, 1)
            with dve.Fori(0, B // 8) as r2:
                for k in range(2):
                    r = r2 * 2 + k
                    part = bass.ds(r * 4, 4)
                    dve.wait_ge(pe_pick, r2 * 2 + 1 + k)
                    dve.tensor_tensor(here[:, k, :, :], consts["count"][:, 0:P].unsqueeze(1).broadcast_to([P, 4, P]),
                                      place_of[:, part].unsqueeze(2).broadcast_to([P, 4, P]),
                                      ALU.is_equal).then_inc(dv_pick, 1)
                    dve.tensor_tensor(token[:, k, :, :], consts["count"][:, 0:J].unsqueeze(1).broadcast_to([P, 4, J]),
                                      tile_of[:, part].unsqueeze(2).broadcast_to([P, 4, J]),
                                      ALU.is_equal).then_inc(dv_dest, 1)
                    dve.wait_ge(dv_dest, r2 * 2 + 2 + k)
                    dve.tensor_tensor(token[:, k, :, :], token[:, k, :, :],
                                      consts["token"][:, part].unsqueeze(2).broadcast_to([P, 4, J]),
                                      ALU.mult).then_inc(dv_pick, 1)
            dve.wait_ge(pe_pick, B // 4 + 2)
            chain(dve.tensor_copy(index[:, :], table[:, 0:J]))

        @block.scalar
        def _(act):
            act.wait_ge(dv_diff, 1)
            act.activation(diff[:, :], diff[:, :], ACT.Exp).then_inc(ac_exp, 1)

        @block.tensor
        def _(pe):
            pe.wait_ge(dv_hot, 1)
            pe.matmul(rank[:, :], consts["before"][:, :], hot16[:, :], start=True, stop=True).then_inc(pe_count, 1)
            pe.matmul(total[:, :], consts["ones"][:, :], hot16[:, :], start=True, stop=True).then_inc(pe_count, 1)
            pe.sem_inc(pe_pick, 2)

            def pick(r2, k, first, final):
                pe.wait_ge(dv_pick, (r2 * 2 + k) * 2 + 4)
                for q in range(4):
                    i = pe.matmul(table[:, 0:J], here[:, k, q, :], token[:, k, q, :], start=first and q == 0,
                                  stop=final and q == 3)
                i.then_inc(pe_pick, 1)

            pick(0, 0, True, False)
            pick(0, 1, False, B // 8 == 1)
            if B // 8 > 2:
                with pe.Fori(1, B // 8 - 1) as r2:
                    pick(r2, 0, False, False)
                    pick(r2, 1, False, False)
            if B // 8 > 1:
                pick(B // 8 - 1, 0, False, False)
                pick(B // 8 - 1, 1, False, True)


def experts0(nc, NT, J, y1, w0, w1, wo, expert, index, ident, out):
    with ExitStack() as ctx:
        sb = lambda name, shape, dt=F32: ctx.enter_context(nc.sbuf_tensor(name, shape, dt))
        ps = lambda name: ctx.enter_context(nc.psum_tensor(name, [P, 512], F32))
        sem = lambda name: ctx.enter_context(nc.semaphore("e0_" + name))
        now = sb("e0_now", [P, 2], I32)
        rows = sb("e0_rows", [P, 2, D])
        xT = [sb(f"e0_xT{h}", [P, 2, D], F16) for h in ("hi", "lo")]
        silu = sb("e0_silu", [P, 2, F0])
        inter = sb("e0_inter", [P, 2, F0])
        iT = [sb(f"e0_iT{h}", [P, 2, F0], F16) for h in ("hi", "lo")]
        result = sb("e0_result", [P, 2, D])
        turn_x = ps("e0_turn_x")
        up0 = [ps(f"e0_up0{k}") for k in range(2)]
        up1 = [ps(f"e0_up1{k}") for k in range(2)]
        turn_i = [ps(f"e0_turn_i{k}") for k in range(2)]
        down = ps("e0_down")
        rows_in = [sem(f"rows_in{k}") for k in range(2)]
        rows_out = [sem(f"rows_out{k}") for k in range(2)]
        po_turn = sem("po_turn")
        dv_now = sem("dv_now")
        pe_x = sem("pe_x")
        ac_x = sem("ac_x")
        dv_x = sem("dv_x")
        pe_up0 = sem("pe_up0")
        pe_up1 = sem("pe_up1")
        ac_silu = sem("ac_silu")
        dv_inter = sem("dv_inter")
        pe_i = sem("pe_i")
        ac_i = sem("ac_i")
        dv_i = sem("dv_i")
        pe_down = sem("pe_down")
        dv_down = sem("dv_down")
        block = ctx.enter_context(nc.Block())
        def done(t, ago=0):
            return t + 3 - ago

        def landed(n):
            return n * 16 + 32

        def walk(engine, step):
            step(0, 0, 0, True, False, True)
            with engine.Fori(0, J // 2 - 1) as n:
                step(n * 2 + 1, n, 1, True, True, True)
                step(n * 2 + 2, n + 1, 0, True, True, True)
            step(J - 1, J // 2 - 1, 1, True, True, False)
            step(J, J // 2, 0, False, True, False)

        @block.gpsimd
        def _(pool):
            with pool.Fori(0, J // 2) as n:
                for k in range(2):
                    pool.wait_ge(dv_now, done(n * 2 + k))
                    pool.wait_ge(pe_x, done(n * 2 + k, 2))
                    pool.sem_inc(po_turn, 1)
                    pool.indirect_dma_start(rows[:, k, :], None, y1,
                                            bass.IndirectOffsetOnAxis(ap=now[:, k:k + 1], axis=0)
                                            ).then_inc(rows_in[k], 16)

        @block.sync
        def _(sp):
            for k in range(2):
                sp.sem_inc(rows_out[k], 16)
            with sp.Fori(0, J // 2) as n:
                for k in range(2):
                    sp.wait_ge(dv_down, done(n * 2 + k))
                    sp.dma_start(out[bass.ds((n * 2 + k) * P, P), :], result[:, k, :]).then_inc(rows_out[k], 16)
            for k in range(2):
                sp.wait_ge(rows_out[k], 16 * (J // 2) + 16)

        @block.tensor
        def _(pe):
            for s in (pe_x, pe_up0, pe_up1, pe_i, pe_down):
                pe.sem_inc(s, 2)

            def turn_rows(t, n, k):
                pe.wait_ge(rows_in[k], n * 16 + 16)
                pe.wait_ge(ac_x, done(t, 1))
                pe.wait_ge(dv_x, done(t, 1))
                for c in range(DC):
                    i = pe.transpose(turn_x[:, c * P:(c + 1) * P], rows[:, k, c * P:(c + 1) * P], ident[:, :])
                i.then_inc(pe_x, 1)

            def product(bank, k, left, right, chunks, width, e):
                trio = [(c, a, b) for c in range(chunks) for a, b in ((0, 0), (0, 1), (1, 0))]
                for q, (c, a, b) in enumerate(trio):
                    i = pe.matmul(bank[:, 0:width], left[a][:, k, c * P:(c + 1) * P],
                                  right[b][:, bass.ds(e * (chunks * width) + c * width, width)], start=(q == 0),
                                  stop=(q == len(trio) - 1))
                return i

            def step(t, n, k, up, rest, more):
                if up:
                    e = pe.value_load(expert[0:1, bass.ds(t, 1)], min_val=0, max_val=E0 - 1)
                    pe.wait_ge(ac_x, done(t))
                    pe.wait_ge(dv_x, done(t))
                    pe.wait_ge(ac_silu, done(t, 2))
                    product(up0[k], k, xT, w0, DC, F0, e).then_inc(pe_up0, 1)
                if rest:
                    pe.wait_ge(dv_inter, done(t, 1))
                    pe.wait_ge(ac_i, done(t, 3))
                    pe.wait_ge(dv_i, done(t, 3))
                    for c in range(FC):
                        i = pe.transpose(turn_i[1 - k][:, c * P:(c + 1) * P], inter[:, 1 - k, c * P:(c + 1) * P],
                                         ident[:, :])
                    i.then_inc(pe_i, 1)
                if up:
                    pe.wait_ge(dv_inter, done(t, 2))
                    product(up1[k], k, xT, w1, DC, F0, e).then_inc(pe_up1, 1)
                if more:
                    turn_rows(t + 1, n + k, 1 - k)
                if rest:
                    e = pe.value_load(expert[0:1, bass.ds(t - 1, 1)], min_val=0, max_val=E0 - 1)
                    pe.wait_ge(ac_i, done(t, 1))
                    pe.wait_ge(dv_i, done(t, 1))
                    pe.wait_ge(dv_down, done(t, 2))
                    product(down, 1 - k, iT, wo, FC, D, e).then_inc(pe_down, 1)

            turn_rows(0, 0, 0)
            walk(pe, step)

        @block.scalar
        def _(act):
            for s in (ac_x, ac_silu, ac_i):
                act.sem_inc(s, 2)

            def high_x(t, k):
                act.wait_ge(pe_x, done(t))
                act.wait_ge(pe_up1, done(t, 2))
                act.activation(xT[0][:, k, :], turn_x[:, 0:D], ACT.Copy).then_inc(ac_x, 1)

            def step(t, n, k, up, rest, more):
                if up:
                    act.wait_ge(pe_up0, done(t))
                    act.wait_ge(dv_inter, done(t, 2))
                    act.activation(silu[:, k, :], up0[k][:, :], ACT.Silu, scale=1.0 / WSCALE).then_inc(ac_silu, 1)
                if rest:
                    act.wait_ge(pe_i, done(t, 1))
                    act.wait_ge(pe_down, done(t, 3))
                    act.activation(iT[0][:, 1 - k, :], turn_i[1 - k][:, :], ACT.Copy).then_inc(ac_i, 1)
                if more:
                    high_x(t + 1, 1 - k)

            high_x(0, 0)
            walk(act, step)

        @block.vector
        def _(dve):
            for s in (dv_now, dv_x, dv_inter, dv_i, dv_down):
                dve.sem_inc(s, 2)

            def fetch(t, n, k):
                if not (isinstance(t, int) and t < 2):
                    dve.wait_ge(rows_in[k], n * 16)
                dve.tensor_scalar(now[:, k:k + 1], index[:, bass.ds(t, 1)], 0.0, None, ALU.add).then_inc(dv_now, 1)

            def low_x(t, k):
                dve.wait_ge(ac_x, done(t))
                dve.tensor_tensor(xT[1][:, k, :], turn_x[:, 0:D], xT[0][:, k, :], ALU.subtract).then_inc(dv_x, 1)

            def step(t, n, k, up, rest, more, fetches=True):
                if rest:
                    dve.wait_ge(ac_i, done(t, 1))
                    dve.tensor_tensor(iT[1][:, 1 - k, :], turn_i[1 - k][:, :], iT[0][:, 1 - k, :],
                                      ALU.subtract).then_inc(dv_i, 1)
                if up:
                    dve.wait_ge(ac_silu, done(t))
                    dve.wait_ge(pe_up1, done(t))
                    dve.wait_ge(pe_i, done(t, 2))
                    dve.tensor_tensor(inter[:, k, :], silu[:, k, :], up1[k][:, :], ALU.mult).then_inc(dv_inter, 1)
                if more:
                    low_x(t + 1, 1 - k)
                if more and fetches:
                    fetch(t + 2, n + 1, k)
                if rest:
                    dve.wait_ge(pe_down, done(t, 1))
                    dve.wait_ge(rows_out[1 - k], landed(n + k) - 32)
                    dve.tensor_scalar(result[:, 1 - k, :], down[:, 0:D], 1.0 / WSCALE**2, None,
                                      ALU.mult).then_inc(dv_down, 1)

            fetch(0, 0, 0)
            fetch(1, 0, 1)
            low_x(0, 0)
            step(0, 0, 0, True, False, True)
            with dve.Fori(0, J // 2 - 2) as n:
                step(n * 2 + 1, n, 1, True, True, True)
                step(n * 2 + 2, n + 1, 0, True, True, True)
            step(J - 3, J // 2 - 2, 1, True, True, True)
            step(J - 2, J // 2 - 1, 0, True, True, True, fetches=False)
            step(J - 1, J // 2 - 1, 1, True, True, False)
            step(J, J // 2, 0, False, True, False)



H1, HD1 = 16, 16
STRIP = 32
STRIPS = P // STRIP
LIMIT = 50.0
SCALE1 = HD1**-0.5


def attention1(nc, NT, a, consts, X, sorted0, dest, weight, wq, wk, wv, router, ident, tgates, logits, yT):
    with ExitStack() as ctx:
        sb = lambda name, shape, dt=F32: ctx.enter_context(nc.sbuf_tensor("a1_" + name, shape, dt))
        ps = lambda name: ctx.enter_context(nc.psum_tensor("a1_" + name, [P, 512], F32))
        sem = lambda name: ctx.enter_context(nc.semaphore("a1_" + name))
        wo = sb("wo", [P, DC, D])
        bq = sb("bq", [P, DC])
        bk = sb("bk", [P, DC])
        bv = sb("bv", [P, D])
        bo = sb("bo", [P, D])
        gamma = sb("gamma", [P, D])
        beta = sb("beta", [P, D])
        rs = sb("rs", [P, 1])
        gates = sb("gates", [P, 4])
        half_neg = sb("half_neg", [P, 1])
        eps = sb("eps", [P, 1])
        mask_i = sb("mask_i", [P, NT, S], I32)
        bound = sb("bound", [P, NT, S])
        share = sb("share", [P, 2, NT])
        now = sb("now", [P, 2], I32)
        rows = sb("rows", [P, 2, D])
        xn = sb("xn", [P, D])
        stats = sb("stats", [P, 6])
        mv = sb("mv", [P, 3, 2])
        rstd = sb("rstd", [P, 3])
        xT = [sb(f"xT{h}", [P, DC, P], F16) for h in ("hi", "lo")]
        ctx32 = sb("ctx32", [P, DC, NB, 2, S])
        cT = [sb(f"cT{h}", [P, DC, NB, 2, S], F16) for h in ("hi", "lo")]
        qT = sb("qT", [P, DC, P])
        kT = sb("kT", [P, DC, P])
        kz = sb("kz", [P, DC, NB, 2, S])
        vz = sb("vz", [P, NB, D])
        E = sb("E", [P, STRIPS, DC, 2, S])
        sums = sb("sums", [P, H1])
        PT = sb("PT", [P, STRIPS, DC, P])
        cxT = sb("cxT", [P, DC, P])
        delta = sb("delta", [P, D])
        yn = sb("yn", [P, D])
        score = [ps(f"score{r}") for r in range(STRIPS)]
        turn = ps("turn")
        proj = ps("proj")
        turnP = ps("turnP")
        outp = ps("outp")

        ctx_in, const_in = map(sem, ("ctx_in", "const_in"))
        rows_in = [sem(f"rows_in{k}") for k in range(2)]
        v_const, a_const, a_turn, v_turn, p_const, p_turn, v_stats = map(sem, (
            "v_const", "a_const", "a_turn", "v_turn", "p_const", "p_turn", "v_stats"))
        e_x, e_qk, e_v, e_sc, e_PT, e_cx, e_d, e_y, e_log = map(sem, (
            "e_x",
            "e_qk",
            "e_v",
            "e_sc",
            "e_PT",
            "e_cx",
            "e_d",
            "e_y",
            "e_log"))
        v_now, v_x2, v_ln, v_xlo, v_cap, v_sum, v_norm, v_v, v_d, v_y, v_ylo, v_log = map(sem, (
            "v_now",
            "v_x2",
            "v_ln",
            "v_xlo",
            "v_cap",
            "v_sum",
            "v_norm",
            "v_v",
            "v_d",
            "v_y",
            "v_ylo",
            "v_log"))
        a_chi, a_xhi, a_qk, a_exp, a_PT, a_cx, a_yhi = map(sem, (
            "a_chi",
            "a_xhi",
            "a_qk",
            "a_exp",
            "a_PT",
            "a_cx",
            "a_yhi"))
        p_clo, p_rstd, p_rstd_d, p_rstd_y, p_kz, p_beta, p_x3 = map(sem, (
            "p_clo",
            "p_rstd",
            "p_rstd_d",
            "p_rstd_y",
            "p_kz",
            "p_beta",
            "p_x3"))
        block = ctx.enter_context(nc.Block())

        def row(t):
            return X[:, bass.ds(t, 1), :].rearrange("p o d -> p (o d)")

        def walk(engine, iteration):
            iteration(0, None, None, None, 2)
            iteration(1, 0, None, None, 2)
            iteration(2, 1, 0, None, 2)
            with engine.Fori(0, NT - 5) as c:
                iteration(c + 3, c + 2, c + 1, c, 2)
            iteration(NT - 2, NT - 3, NT - 4, NT - 5, 1)
            iteration(NT - 1, NT - 2, NT - 3, NT - 4, 0)
            iteration(None, NT - 1, NT - 2, NT - 3, 0)
            iteration(None, None, NT - 1, NT - 2, 0)
            iteration(None, None, None, NT - 1, 0)

        loads = [(wo[:, :, :], a["a1_wo"].rearrange("p (c d) -> p c d", c=DC)), (bq[:, :], a["a1_bq"]),
                 (bk[:, :], a["a1_bk"])]
        loads += [(dst[:, :], a[name].partition_broadcast(P)) for dst, name in (
            (bv, "a1_bv"), (bo, "a1_bo"), (gamma, "a1_gamma"), (beta, "a1_beta"), (rs, "a1_rs"))]
        loads += [(gates[:, 0:2], a["g_ffn"].partition_broadcast(P)), (gates[:, 2:4], a["g_xattn"].partition_broadcast(P))]
        loads += [(mask_i[b * S:(b + 1) * S, :, :],
                   a["mask"].rearrange("(t b) k -> b t k", b=NB)[b].partition_broadcast(S)) for b in range(NB)]
        LOADED = 16 * len(loads)

        @block.sync
        def _(sp):
            for dst, src in loads:
                sp.dma_start(dst, src).then_inc(const_in, 16)
            sp.sem_inc(ctx_in, 32)

            def load_context(n):
                sp.wait_ge(p_clo, last(1, n, 1))
                for k in range(2):
                    sp.dma_start(ctx32[:, :, :, k, :], a["ctxT"][:, bass.ds(n * D, D)]
                                 .rearrange("p (c b s) -> p c b s", c=DC, b=NB)).then_inc(ctx_in, 16)

            with sp.Fori(0, NT) as n:
                load_context(n)

        @block.gpsimd
        def _(pool):
            pool.memset(half_neg[:, :], -0.5).then_inc(p_const, 1)
            pool.memset(eps[:, :], EPS_LN).then_inc(p_const, 1)
            pool.memset(vz[:, :, :], 0.0).then_inc(p_const, 1)
            for s, n in ((p_clo, 1), (p_rstd, 2), (p_rstd_d, 2), (p_rstd_y, 2), (p_kz, 1), (p_beta, 1), (p_x3, 2)):
                pool.sem_inc(s, n)
            pool.wait_ge(p_const, 3)
            pool.wait_ge(v_const, 1)

            def power(n, s, t):
                pool.tensor_tensor(rstd[:, n:n + 1], mv[:, n, 1:2], eps[:, :], ALU.add).then_inc(s, 1)
                pool.wait_ge(s, this(2, t, 1))
                pool.tensor_tensor(rstd[:, n:n + 1], rstd[:, n:n + 1], half_neg[:, :], ALU.pow).then_inc(s, 1)

            def gather(n):
                pool.wait_ge(v_now, this(1, n, 1))
                pool.wait_ge(v_x2, last(2, n, 2))
                pool.sem_inc(p_turn, 1)
                for k in range(2):
                    pool.indirect_dma_start(rows[:, k, :], None, sorted0,
                                            bass.IndirectOffsetOnAxis(ap=now[:, k:k + 1], axis=0)
                                            ).then_inc(rows_in[k], 16)

            def iteration(n, t, p, c, ahead):
                if c is not None:
                    pool.wait_ge(v_d, this(3, c, 2))
                    power(1, p_rstd_d, c)
                    pool.wait_ge(v_d, this(3, c, 3))
                    pool.tensor_tensor(delta[:, :], delta[:, :], gamma[:, :], ALU.mult).then_inc(p_x3, 1)
                    pool.wait_ge(p_x3, this(2, c, 1))
                    pool.tensor_tensor(row(c), row(c), delta[:, :], ALU.add).then_inc(p_x3, 1)
                if t is not None:
                    pool.wait_ge(a_qk, this(1, t, 1))
                    if p is not None:
                        pool.wait_ge(e_sc, this(2, p, 2))
                    for h in range(DC):
                        pair = consts["pair"][:, :].unsqueeze(2).broadcast_to([P, 2, S])
                        for b in range(NB):
                            i = pool.tensor_tensor(kz[:, h, b, :, :], kT[:, h:h + 1, b * S:(b + 1) * S]
                                                   .broadcast_to([P, 2, S]), pair, ALU.mult)
                    i.then_inc(p_kz, 1)
                if c is not None:
                    pool.wait_ge(v_y, this(2, c, 1))
                    power(2, p_rstd_y, c)
                if n is not None:
                    pool.wait_ge(v_ln, this(2, n, 2))
                    pool.tensor_tensor(row(n), row(n), beta[:, :], ALU.add).then_inc(p_beta, 1)
                    pool.wait_ge(a_chi, this(1, n, 1))
                    pool.wait_ge(ctx_in, this(32, n, 32))
                    pool.tensor_tensor(cT[1][:, :, :, :, :], ctx32[:, :, :, :, :], cT[0][:, :, :, :, :],
                                       ALU.subtract).then_inc(p_clo, 1)
                if ahead >= 2:
                    gather(n + 2)
                if ahead >= 1:
                    pool.wait_ge(v_ln, this(2, n + 1, 1))
                    power(0, p_rstd, n + 1)

            gather(0)
            gather(1)
            pool.wait_ge(v_ln, this(2, 0, 1))
            power(0, p_rstd, 0)
            walk(pool, iteration)

        @block.tensor
        def _(pe):
            for s, n in ((e_x, 1), (e_qk, 1), (e_v, 1), (e_sc, 2), (e_PT, 2), (e_cx, 1), (e_d, 1), (e_y, 1), (e_log, 1)):
                pe.sem_inc(s, n)
            pe.wait_ge(const_in, LOADED)
            trio = [(c, i, j) for c in range(DC) for i, j in ((0, 0), (0, 1), (1, 0))]

            def mm3(out, left, right):
                for n, (c, i, j) in enumerate(trio):
                    m = pe.matmul(out, left(c, i), right(c, j), start=(n == 0), stop=(n == len(trio) - 1))
                return m

            def turn_x(n, c):
                pe.wait_ge(v_ln, this(2, n, 2))
                pe.wait_ge(v_xlo, last(1, n, 1))
                if c is not None:
                    pe.wait_ge(v_log, last(1, c, 1))
                for c in range(DC):
                    i = pe.transpose(turn[:, c * P:(c + 1) * P], xn[:, c * P:(c + 1) * P], ident[:, :])
                i.then_inc(e_x, 1)

            def scores(p, half):
                if half == 0:
                    pe.wait_ge(p_kz, this(1, p, 1))
                    pe.wait_ge(a_qk, this(1, p, 1))
                pe.wait_ge(v_cap, last(2, p, half + 1))
                for r in (2 * half, 2 * half + 1):
                    strip = slice(r * STRIP, (r + 1) * STRIP)
                    for b in range(NB):
                        for h in range(DC):
                            i = pe.matmul(score[r][b * S:(b + 1) * S, h * P:(h + 1) * P],
                                          qT[strip, h, b * S:(b + 1) * S], kz[strip, h, b, :, :], start=True, stop=True)
                i.then_inc(e_sc, 1)

            def query_key(t):
                pe.wait_ge(v_xlo, this(1, t, 1))
                pe.wait_ge(p_clo, this(1, t, 1))
                pe.wait_ge(v_v, last(1, t, 1))
                for h in range(DC):
                    part = lambda c: slice(c * D + h * P, c * D + (h + 1) * P)
                    mm3(proj[:, h * P:(h + 1) * P], lambda c, i: wq[i][:, part(c)], lambda c, j: xT[j][:, c, :])
                    i = mm3(proj[:, D + h * P:D + (h + 1) * P], lambda c, i: wk[i][:, part(c)],
                            lambda c, j: cT[j][:, c, :, 0, :])
                i.then_inc(e_qk, 1)

            def value(t):
                pe.wait_ge(a_qk, this(1, t, 1))
                for b in range(NB):
                    i = mm3(proj[:, b * D:(b + 1) * D], lambda c, i: cT[i][:, c, b, :, :],
                            lambda c, j: wv[j][:, c * D:(c + 1) * D])
                i.then_inc(e_v, 1)

            def turn_P(p, half):
                pe.wait_ge(v_norm, this(2, p, half + 1))
                pe.wait_ge(a_PT, last(2, p, 2) if half == 0 else this(2, p, 1))
                for n in range(4):
                    r, h = 2 * half + n // 2, n % 2
                    i = pe.transpose(turnP[:, n * P:(n + 1) * P], E[:, r, h, :, :], ident[:, :])
                i.then_inc(e_PT, 1)

            def weigh(p, half):
                pe.wait_ge(a_PT, this(2, p, half + 1))
                if half == 0:
                    pe.wait_ge(v_d, last(3, p, 1))
                    pe.wait_ge(v_v, this(1, p, 1))
                for r in (2 * half, 2 * half + 1):
                    strip = slice(r * STRIP, (r + 1) * STRIP)
                    for h in range(DC):
                        for b in range(NB):
                            i = pe.matmul(outp[strip, h * P + b * S:h * P + (b + 1) * S],
                                          vz[:, b, h * P + r * STRIP:h * P + (r + 1) * STRIP],
                                          PT[:, r, h, b * S:(b + 1) * S], start=True, stop=True)
                if half == 1:
                    i.then_inc(e_cx, 1)

            def result(p):
                pe.wait_ge(a_cx, this(1, p, 1))
                for h in range(DC):
                    i = pe.matmul(outp[:, 0:D], cxT[:, h, :], wo[:, h, :], start=(h == 0), stop=(h == DC - 1))
                i.then_inc(e_d, 1)

            def turn_y(c, n):
                pe.wait_ge(v_y, this(2, c, 2))
                pe.wait_ge(v_log, last(1, c, 1))
                if n is not None:
                    pe.wait_ge(v_xlo, this(1, n, 1))
                for k in range(DC):
                    i = pe.transpose(turn[:, k * P:(k + 1) * P], yn[:, k * P:(k + 1) * P], ident[:, :])
                i.then_inc(e_y, 1)

            def route(c):
                pe.wait_ge(v_ylo, this(1, c, 1))
                for n, (k, i, j) in enumerate(trio):
                    m = pe.matmul(turn[:, 0:E1], yT[i][:, k, bass.ds(c * P, P)], router[j][:, k * E1:(k + 1) * E1],
                                  start=(n == 0), stop=(n == len(trio) - 1))
                m.then_inc(e_log, 1)

            def iteration(n, t, p, c, ahead):
                if p is not None:
                    scores(p, 0)
                    scores(p, 1)
                if t is not None:
                    query_key(t)
                if p is not None:
                    turn_P(p, 0)
                if n is not None:
                    turn_x(n, c)
                if t is not None:
                    value(t)
                if p is not None:
                    weigh(p, 0)
                    turn_P(p, 1)
                    weigh(p, 1)
                if c is not None:
                    turn_y(c, n)
                if p is not None:
                    result(p)
                if c is not None:
                    route(c)

            walk(pe, iteration)

        @block.vector
        def _(dve):
            chain = Chain(dve, v_const)
            for s, n in ((v_now, 1), (v_x2, 2), (v_ln, 2), (v_xlo, 1), (v_cap, 2), (v_sum, 6), (v_norm, 2), (v_v, 1),
                         (v_d, 3), (v_y, 2), (v_ylo, 1), (v_log, 1)):
                dve.sem_inc(s, n)
            dve.wait_ge(const_in, LOADED)
            dve.wait_ge(a_const, 1)
            chain(dve.tensor_scalar(beta[:, :], beta[:, :], tgates[:, 3:4], None, ALU.mult))
            chain(dve.tensor_scalar(gamma[:, :], gamma[:, :], tgates[:, 3:4], None, ALU.mult))
            chain(dve.tensor_scalar(rs[:, :], rs[:, :], 0.0, 0.3, ALU.max, ALU.min))
            chain(dve.tensor_scalar(bo[:, :], bo[:, :], rs[:, 0:1], None, ALU.mult))
            chain(dve.tensor_scalar(share[:, :, :], weight[:, :, :], tgates[:, 0:1], None, ALU.mult))
            chain(dve.tensor_scalar(bound[:, :, :], mask_i[:, :, :], 0.5, 2 * LIMIT / SCALE1, ALU.is_gt, ALU.mult))
            chain(dve.tensor_scalar(bound[:, :, :], bound[:, :, :], -LIMIT / SCALE1, None, ALU.add))

            def fetch(t):
                if not (isinstance(t, int) and t == 0):
                    for k in range(2):
                        dve.wait_ge(rows_in[k], t * 16)
                dve.tensor_scalar(now[:, :].unsqueeze(2), dest[:, :, bass.ds(t, 1)], 0.0, None,
                                  ALU.add).then_inc(v_now, 1)

            def sum_x2(t):
                dve.wait_ge(rows_in[0], t * 16 + 16)
                dve.scalar_tensor_tensor(out=row(t), in0=rows[:, 0, :], scalar=share[:, 0, bass.ds(t, 1)],
                                         in1=row(t), op0=ALU.mult, op1=ALU.add).then_inc(v_x2, 1)
                dve.wait_ge(rows_in[1], t * 16 + 16)
                dve.wait_ge(v_x2, this(2, t, 1))
                dve.scalar_tensor_tensor(out=row(t), in0=rows[:, 1, :], scalar=share[:, 1, bass.ds(t, 1)],
                                         in1=row(t), op0=ALU.mult, op1=ALU.add).then_inc(v_x2, 1)

            def moments(n, source, before, value, s):
                dve.sem_clear(v_stats)
                dve.wait_ge(before, value)
                dve.sem_inc(v_turn, 1)
                dve.bn_stats(stats[:, :], source).then_inc(v_stats, 1)
                dve.wait_ge(v_stats, 1)
                dve.bn_aggr(mv[:, n, :], stats[:, :]).then_inc(s, 1)

            def standard(n, out, source, s):
                dve.tensor_scalar(out, source, mv[:, n, 0:1], rstd[:, n:n + 1], ALU.subtract, ALU.mult).then_inc(s, 1)

            def cap(p, half):
                dve.wait_ge(e_sc, this(2, p, half + 1))
                dve.wait_ge(e_PT, last(2, p, half + 1))
                for r in (2 * half, 2 * half + 1):
                    i = dve.scalar_tensor_tensor(
                        out=E[:, r, :, :, :].rearrange("p h j k -> p (h j) k"),
                        in0=score[r][:, 0:D].rearrange("p (n k) -> p n k", k=S), scalar=-LIMIT / SCALE1,
                        in1=bound[:, bass.ds(p, 1), :].broadcast_to([P, 4, S]), op0=ALU.max, op1=ALU.min)
                i.then_inc(v_cap, 1)

            def normalize(p, half):
                dve.wait_ge(a_exp, this(2, p, half + 1))
                e = E[:, 2 * half:2 * half + 2, :, :, :].rearrange("p r h j k -> p (r h j) k")
                s = sums[:, 8 * half:8 * half + 8]
                dve.tensor_reduce(s, e, AX_X, ALU.add).then_inc(v_sum, 1)
                dve.wait_ge(v_sum, this(6, p, 3 * half + 1))
                dve.scalar_tensor_tensor(out=s, in0=s, scalar=1e-8, in1=s, op0=ALU.mult, op1=ALU.add).then_inc(v_sum, 1)
                dve.wait_ge(v_sum, this(6, p, 3 * half + 2))
                dve.reciprocal(s, s).then_inc(v_sum, 1)
                dve.wait_ge(v_sum, this(6, p, 3 * half + 3))
                dve.tensor_tensor(e, e, s.unsqueeze(2).broadcast_to([P, 8, S]), ALU.mult).then_inc(v_norm, 1)

            def keep_value(t):
                dve.wait_ge(e_v, this(1, t, 1))
                dve.wait_ge(e_cx, last(1, t, 1))
                for b in range(NB):
                    for j in range(2):
                        half = slice(j * S, (j + 1) * S)
                        view = lambda y: y.rearrange("p (m j d) -> p m j d", j=2, d=HD1)[:, :, j, :]
                        i = dve.scalar_tensor_tensor(out=view(vz[half, b, :]), in0=view(proj[half, b * D:(b + 1) * D]),
                                                     scalar=1.0 / WSCALE, in1=view(bv[half, :]), op0=ALU.mult,
                                                     op1=ALU.add)
                i.then_inc(v_v, 1)

            def result(c):
                dve.wait_ge(e_d, this(1, c, 1))
                dve.wait_ge(p_x3, last(2, c, 2))
                dve.scalar_tensor_tensor(out=delta[:, :], in0=outp[:, 0:D], scalar=rs[:, 0:1], in1=bo[:, :],
                                         op0=ALU.mult, op1=ALU.add).then_inc(v_d, 1)
                moments(1, delta[:, :], v_d, this(3, c, 1), v_d)

            def iteration(n, t, p, c, ahead):
                if p is not None:
                    cap(p, 0)
                if c is not None:
                    result(c)
                if p is not None:
                    cap(p, 1)
                    normalize(p, 0)
                if c is not None:
                    dve.wait_ge(p_rstd_d, this(2, c, 2))
                    standard(1, delta[:, :], delta[:, :], v_d)
                if n is not None:
                    dve.wait_ge(p_rstd, this(2, n, 2))
                    dve.wait_ge(e_x, last(1, n, 1))
                    standard(0, xn[:, :], row(n), v_ln)
                if p is not None:
                    normalize(p, 1)
                if n is not None:
                    dve.wait_ge(a_xhi, this(1, n, 1))
                    dve.tensor_tensor(xT[1][:, :, :], turn[:, 0:D].rearrange("p (c k) -> p c k", c=DC), xT[0][:, :, :],
                                      ALU.subtract).then_inc(v_xlo, 1)
                if c is not None:
                    moments(2, row(c), p_x3, this(2, c, 2), v_y)
                if ahead >= 1:
                    sum_x2(n + 1)
                if ahead >= 2:
                    fetch(n + 2)
                if c is not None:
                    dve.wait_ge(p_rstd_y, this(2, c, 2))
                    dve.wait_ge(e_y, last(1, c, 1))
                    standard(2, yn[:, :], row(c), v_y)
                if ahead >= 1:
                    moments(0, row(n + 1), v_x2, this(2, n + 1, 2), v_ln)
                if c is not None:
                    dve.wait_ge(a_yhi, this(1, c, 1))
                    dve.tensor_tensor(yT[1][:, :, bass.ds(c * P, P)], turn[:, 0:D].rearrange("p (c k) -> p c k", c=DC),
                                      yT[0][:, :, bass.ds(c * P, P)], ALU.subtract).then_inc(v_ylo, 1)
                if t is not None:
                    keep_value(t)
                if c is not None:
                    dve.wait_ge(e_log, this(1, c, 1))
                    dve.tensor_scalar(logits[:, bass.ds(c * E1, E1)], turn[:, 0:E1], 1.0 / WSCALE, None,
                                      ALU.mult).then_inc(v_log, 1)

            fetch(0)
            sum_x2(0)
            fetch(1)
            moments(0, row(0), v_x2, this(2, 0, 2), v_ln)
            walk(dve, iteration)

        @block.scalar
        def _(act):
            for s, n in ((a_chi, 1), (a_xhi, 1), (a_qk, 1), (a_exp, 2), (a_PT, 2), (a_cx, 1), (a_yhi, 1)):
                act.sem_inc(s, n)
            act.wait_ge(const_in, LOADED)
            act.activation(tgates[:, :], gates[:, :], ACT.Tanh).then_inc(a_const, 1)

            def high_context(n):
                act.wait_ge(ctx_in, this(32, n, 32))
                act.wait_ge(e_v, last(1, n, 1))
                act.activation(cT[0][:, :, :, :, :], ctx32[:, :, :, :, :], ACT.Copy).then_inc(a_chi, 1)

            def exponentials(p, half):
                act.wait_ge(v_cap, this(2, p, half + 1))
                e = E[:, 2 * half:2 * half + 2, :, :, :]
                act.activation(e, e, ACT.Exp, scale=SCALE1).then_inc(a_exp, 1)

            def turned_P(p, half):
                act.wait_ge(e_PT, this(2, p, half + 1))
                act.wait_ge(e_cx, last(1, p, 1))
                act.activation(PT[:, 2 * half:2 * half + 2, :, :].rearrange("p r h q -> p (r h) q"),
                               turnP[:, :].rearrange("p (n q) -> p n q", q=P), ACT.Copy).then_inc(a_PT, 1)

            def iteration(n, t, p, c, ahead):
                if p is not None:
                    exponentials(p, 0)
                    exponentials(p, 1)
                if t is not None:
                    act.wait_ge(e_qk, this(1, t, 1))
                    if p is not None:
                        act.wait_ge(e_sc, this(2, p, 2))
                    act.wait_ge(p_kz, last(1, t, 1))
                    for h in range(DC):
                        act.activation(qT[:, h, :], proj[:, h * P:(h + 1) * P], ACT.Identity, bias=bq[:, h:h + 1],
                                       scale=1.0 / WSCALE)
                        i = act.activation(kT[:, h, :], proj[:, D + h * P:D + (h + 1) * P], ACT.Identity,
                                           bias=bk[:, h:h + 1], scale=1.0 / WSCALE)
                    i.then_inc(a_qk, 1)
                if p is not None:
                    turned_P(p, 0)
                if n is not None:
                    act.wait_ge(e_x, this(1, n, 1))
                    act.wait_ge(e_qk, last(1, n, 1))
                    act.activation(xT[0][:, :, :], turn[:, 0:D].rearrange("p (c k) -> p c k", c=DC),
                                   ACT.Copy).then_inc(a_xhi, 1)
                    high_context(n)
                if p is not None:
                    turned_P(p, 1)
                if p is not None:
                    act.wait_ge(e_cx, this(1, p, 1))
                    act.activation(cxT[:, :, :], outp[:, 0:D].rearrange("p (h q) -> p h q", h=DC),
                                   ACT.Copy).then_inc(a_cx, 1)
                if c is not None:
                    act.wait_ge(e_y, this(1, c, 1))
                    act.sem_inc(a_turn, 1)
                    act.activation(yT[0][:, :, bass.ds(c * P, P)], turn[:, 0:D].rearrange("p (c k) -> p c k", c=DC),
                                   ACT.Copy).then_inc(a_yhi, 1)

            walk(act, iteration)


def route1(nc, NT, CAP, logits, consts, tgate, share):
    B = 2 * NT
    BANK = 512 // E1
    banks = [(b, min(B, b + BANK)) for b in range(0, B, BANK)]
    with ExitStack() as ctx:
        sb = lambda name, shape, dt=F32: ctx.enter_context(nc.sbuf_tensor("r1_" + name, shape, dt))
        sem = lambda name: ctx.enter_context(nc.semaphore("r1_" + name))
        hot = sb("hot", [P, 2, NT, E1])
        hot16 = sb("hot16", [P, B * E1], F16)
        best = sb("best", [P, 2, NT])
        t = sb("t", [P, NT, E1])
        m = sb("m", [P, NT])
        zero = sb("zero", [P, B])
        count = sb("count", [P, B, E1])
        rank_sb = sb("rank_sb", [P, B, E1])
        upto = sb("upto", [P, E1, B])
        rank = [ctx.enter_context(nc.psum_tensor(f"r1_rank{n}", [P, 512], F32)) for n in range(len(banks))]
        total = [ctx.enter_context(nc.psum_tensor(f"r1_total{n}", [P, 512], F32)) for n in range(len(banks))]
        dv_step, dv_shift, ac_exp, dv_hot, pe_count = map(sem, ("dv_step", "dv_shift", "ac_exp", "dv_hot", "pe_count"))
        block = ctx.enter_context(nc.Block())

        @block.vector
        def _(dve):
            chain = Chain(dve, dv_step)
            values = logits[:, :].rearrange("p (t e) -> p t e", e=E1)
            wide = lambda y: y.unsqueeze(2).broadcast_to([P, NT, E1])
            chain(dve.tensor_reduce(m[:, :], values, AX_X, ALU.max))
            dve.tensor_tensor(values, values, wide(m[:, :]), ALU.subtract).then_inc(dv_shift, 1)
            dve.wait_ge(ac_exp, 1)
            chain(dve.tensor_reduce(m[:, :], values, AX_X, ALU.add))
            chain(dve.reciprocal(m[:, :], m[:, :]))
            chain(dve.tensor_tensor(values, values, wide(m[:, :]), ALU.mult))
            order = consts["order"][:, :].unsqueeze(1).broadcast_to([P, NT, E1])
            top2(dve, chain, values, order, hot, best, t[:, :, :], m[:, :])
            dve.tensor_copy(hot16[:, :], hot[:, :, :, :].rearrange("p k t e -> p (k t e)")).then_inc(dv_hot, 1)
            chain(dve.tensor_tensor(m[:, :], best[:, 0, :], best[:, 1, :], ALU.add))
            chain(dve.reciprocal(m[:, :], m[:, :]))
            chain(dve.tensor_scalar(m[:, :], m[:, :], tgate, None, ALU.mult))
            chain(dve.tensor_tensor(best[:, :, :], best[:, :, :], m[:, :].unsqueeze(1).broadcast_to([P, 2, NT]), ALU.mult))
            chain(dve.memset(zero[:, :], 0.0))
            dve.wait_ge(pe_count, 2 * len(banks))
            for n, (b0, b1) in enumerate(banks):
                dve.tensor_copy(rank_sb[:, b0:b1, :].rearrange("p b e -> p (b e)"), rank[n][:, 0:(b1 - b0) * E1])
                i = dve.tensor_copy(count[:, b0:b1, :].rearrange("p b e -> p (b e)"), total[n][:, 0:(b1 - b0) * E1])
            chain(i)
            for e in range(E1):
                i = dve.tensor_tensor_scan(upto[:, e, :], count[:, :, e], zero[:, :], 0.0, ALU.add, ALU.add)
            chain(i)
            chain(dve.tensor_tensor(count[:, :, :], upto[:, :, :].rearrange("p e b -> p b e"), count[:, :, :], ALU.subtract))
            chain(dve.tensor_tensor(count[:, :, :], count[:, :, :], rank_sb[:, :, :], ALU.add))
            chain(dve.tensor_scalar(count[:, :, :], count[:, :, :], float(CAP), None, ALU.is_lt))
            chain(dve.tensor_tensor(count[:, :, :], count[:, :, :], hot[:, :, :, :].rearrange("p k t e -> p (k t) e"), ALU.mult))
            chain(dve.tensor_tensor(count[:, :, :], count[:, :, :],
                                    best[:, :, :].rearrange("p k t -> p (k t)").unsqueeze(2).broadcast_to([P, B, E1]),
                                    ALU.mult))
            chain(dve.tensor_tensor(share[:, :, :], count[:, 0:NT, :], count[:, NT:B, :], ALU.add))

        @block.scalar
        def _(act):
            act.wait_ge(dv_shift, 1)
            act.activation(logits[:, :], logits[:, :], ACT.Exp).then_inc(ac_exp, 1)

        @block.tensor
        def _(pe):
            pe.wait_ge(dv_hot, 1)
            for n, (b0, b1) in enumerate(banks):
                for out, left in ((rank[n], "before"), (total[n], "ones")):
                    pe.matmul(out[:, 0:(b1 - b0) * E1], consts[left][:, :], hot16[:, b0 * E1:b1 * E1], start=True,
                              stop=True).then_inc(pe_count, 1)


def experts1(nc, NT, yT, w1, w3, w2_dram, share, ident, X, out):
    W = E1 * F1
    WC = W // P
    with ExitStack() as ctx:
        sb = lambda name, shape, dt=F32: ctx.enter_context(nc.sbuf_tensor("e1_" + name, shape, dt))
        ps = lambda name: ctx.enter_context(nc.psum_tensor("e1_" + name, [P, 512], F32))
        sem = lambda name: ctx.enter_context(nc.semaphore("e1_" + name))
        w2 = sb("w2", [P, WC, D])
        first = sb("first", [P, 2, W])
        inter = sb("inter", [P, 2, W])
        iT = sb("iT", [P, 2, W])
        up1 = [ps(f"up1{k}") for k in range(2)]
        up3 = [ps(f"up3{k}") for k in range(2)]
        turn = [ps(f"turn{k}") for k in range(2)]
        down = [ps(f"down{k}") for k in range(2)]
        w2_in = sem("w2_in")
        x4_out = sem("x4_out")
        pe_up1, pe_up3, pe_turn, pe_down, ac_first, ac_silu, ac_iT, dv_ab, dv_share, dv_x4 = map(sem, (
            "pe_up1", "pe_up3", "pe_turn", "pe_down", "ac_first", "ac_silu", "ac_iT", "dv_ab", "dv_share", "dv_x4"))
        block = ctx.enter_context(nc.Block())

        def done(t, ago=0):
            return t + 3 - ago

        def row(t):
            return X[:, bass.ds(t, 1), :].rearrange("p o d -> p (o d)")

        def walk(engine, step):
            step(0, 0, 0, True, False)
            with engine.Fori(0, NT // 2 - 1) as n:
                step(n * 2 + 1, n, 1, True, True)
                step(n * 2 + 2, n + 1, 0, True, True)
            step(NT - 1, NT // 2 - 1, 1, True, True)
            step(NT, NT // 2, 0, False, True)

        @block.sync
        def _(sp):
            sp.dma_start(w2[:, :, :], w2_dram.rearrange("p (c d) -> p c d", c=WC)).then_inc(w2_in, 16)
            with sp.Fori(0, NT) as t:
                sp.wait_ge(dv_x4, t + 3)
                sp.dma_start(out[bass.ds(t * P, P), :], row(t)).then_inc(x4_out, 16)
            sp.wait_ge(x4_out, 16 * NT)

        @block.tensor
        def _(pe):
            for s in (pe_up1, pe_up3, pe_turn, pe_down):
                pe.sem_inc(s, 2)
            pe.wait_ge(w2_in, 16)
            trio = [(c, i, j) for c in range(DC) for i, j in ((0, 0), (0, 1), (1, 0))]

            def up_product(bank, t, w):
                for q, (c, i, j) in enumerate(trio):
                    m = pe.matmul(bank[:, 0:W], yT[i][:, c, bass.ds(t * P, P)], w[j][:, c * W:(c + 1) * W],
                                  start=(q == 0), stop=(q == len(trio) - 1))
                return m

            def step(t, n, k, up, rest):
                if up:
                    pe.wait_ge(ac_first, done(t, 2))
                    up_product(up1[k], t, w1).then_inc(pe_up1, 1)
                    pe.wait_ge(dv_ab, done(t, 2))
                    up_product(up3[k], t, w3).then_inc(pe_up3, 1)
                if rest:
                    pe.wait_ge(dv_share, done(t, 1))
                    pe.wait_ge(ac_iT, done(t, 3))
                    for c in range(WC):
                        i = pe.transpose(turn[1 - k][:, c * P:(c + 1) * P], inter[:, 1 - k, c * P:(c + 1) * P], ident[:, :])
                    i.then_inc(pe_turn, 1)
                    pe.wait_ge(ac_iT, done(t, 1))
                    pe.wait_ge(dv_x4, done(t, 3))
                    for c in range(WC):
                        i = pe.matmul(down[1 - k][:, 0:D], iT[:, 1 - k, c * P:(c + 1) * P], w2[:, c, :], start=(c == 0),
                                      stop=(c == WC - 1))
                    i.then_inc(pe_down, 1)

            walk(pe, step)

        @block.scalar
        def _(act):
            for s in (ac_first, ac_silu, ac_iT):
                act.sem_inc(s, 2)

            def step(t, n, k, up, rest):
                if up:
                    act.wait_ge(pe_up1, done(t))
                    act.wait_ge(dv_ab, done(t, 2))
                    act.activation(first[:, k, :], up1[k][:, 0:W], ACT.Copy).then_inc(ac_first, 1)
                if rest:
                    act.wait_ge(pe_turn, done(t, 1))
                    act.wait_ge(pe_down, done(t, 3))
                    act.activation(iT[:, 1 - k, :], turn[1 - k][:, 0:W], ACT.Copy).then_inc(ac_iT, 1)
                if up:
                    act.wait_ge(dv_ab, done(t))
                    act.activation(inter[:, k, :], inter[:, k, :], ACT.Silu, scale=1.0 / WSCALE**2).then_inc(ac_silu, 1)

            walk(act, step)

        @block.vector
        def _(dve):
            for s in (dv_ab, dv_share, dv_x4):
                dve.sem_inc(s, 2)

            def step(t, n, k, up, rest):
                if up:
                    dve.wait_ge(ac_first, done(t))
                    dve.wait_ge(pe_up3, done(t))
                    dve.wait_ge(pe_turn, done(t, 2))
                    dve.tensor_tensor(inter[:, k, :], first[:, k, :], up3[k][:, 0:W], ALU.mult).then_inc(dv_ab, 1)
                    dve.wait_ge(ac_silu, done(t))
                    i = inter[:, k, :].rearrange("p (e f) -> p e f", f=F1)
                    dve.tensor_tensor(i, i, share[:, bass.ds(t, 1), :].rearrange("p o e -> p e o")
                                      .broadcast_to([P, E1, F1]), ALU.mult).then_inc(dv_share, 1)
                if rest:
                    dve.wait_ge(pe_down, done(t, 1))
                    dve.tensor_tensor(row(t - 1), down[1 - k][:, 0:D], row(t - 1), ALU.add).then_inc(dv_x4, 1)

            walk(dve, step)


def program(nc, a, out, NT=32):
    scratch = lambda name, rows: nc.dram_tensor(name, (rows, D), F32, kind="Internal").ap()
    J = (2 * NT * P + E0 * (P - 1)) // P
    J += J % 2
    y1 = scratch("y1", NT * P)
    sorted0 = scratch("sorted0", J * P)
    rope_dram = nc.dram_tensor("rope_tables", (NT * P, 4 * HALF), F32, kind="Internal").ap()
    with ExitStack() as top:
        sb = lambda name, shape, dt=F32: top.enter_context(nc.sbuf_tensor(name, shape, dt))
        X = sb("X", [P, NT, D])
        ident = sb("ident", [P, P])
        logits = sb("logits0", [P, NT * E0])
        dest = sb("dest0", [P, 2, NT], I32)
        weight = sb("weight0", [P, 2, NT])
        consts = {name: sb(name, list(a[name].shape), F16 if name in ("before", "ones") else F32)
                  for name in ("order", "count", "token", "pair", "before", "ones")}
        const_in = top.enter_context(nc.semaphore("const_in"))
        with nc.Block() as block:
            @block.sync
            def _(sp):
                sp.dma_start(ident[:, :], a["ident"]).then_inc(const_in, 16)
                for name, tile in consts.items():
                    sp.dma_start(tile[:, :], a[name]).then_inc(const_in, 16)
                sp.wait_ge(const_in, 16 * (1 + len(consts)))

        def pairs(stack, **sizes):
            return [tuple(stack.enter_context(nc.sbuf_tensor(f"{name}_{h}", [P, n], F16)) for h in ("hi", "lo"))
                    for name, n in sizes.items()]

        split_weights = WeightSplitter(nc, top)

        def split(*jobs):
            split_weights(*((a[name], *(w[:, :] for w in pair)) for name, pair in jobs))

        with ExitStack() as st:
            wq, wk, wv = pairs(st, wq=DC * H0 * HD0, wk=DC * KV0 * HD0, wv=DC * KV0 * HD0)
            rope_tables(nc, NT, a["pos"], a["freq"], rope_dram)
            split(("wq0", wq), ("wk0", wk), ("wv0", wv))
            attention0(nc, NT, a["x"], a["ctxT"], rope_dram, a["qnw"], a["knw"], a["g_xattn"], wq, wk, wv,
                       a["wo0"], a["gate0"], ident, X, y1, logits)
        with ExitStack() as st:
            expert = st.enter_context(nc.sbuf_tensor("expert", [P, J], I32))
            index = st.enter_context(nc.sbuf_tensor("index", [P, J], I32))
            w0, w1, wo = pairs(st, w0=E0 * DC * F0, w1=E0 * DC * F0, wo=E0 * FC * D)
            split(("e0_w0", w0), ("e0_w1", w1), ("e0_wo", wo))
            route0(nc, NT, J, logits, consts, dest, weight, expert, index)
            experts0(nc, NT, J, y1, w0, w1, wo, expert, index, ident, sorted0)
        CAP = int(np.ceil(NT * P / E1 * 1.25))
        tgates = sb("tgates", [P, 4])
        logits1 = sb("logits1", [P, NT * E1])
        share1 = sb("share1", [P, NT, E1])
        yT = [sb(f"yT{h}", [P, DC, NT * P], F16) for h in ("hi", "lo")]
        with ExitStack() as st:
            wq1, wk1, wv1, router1 = pairs(st, wq1=DC * D, wk1=DC * D, wv1=DC * D, router1=DC * E1)
            split(("a1_wq", wq1), ("a1_wk", wk1), ("a1_wv", wv1), ("gate1", router1))
            attention1(nc, NT, a, consts, X, sorted0, dest, weight, wq1, wk1, wv1, router1, ident, tgates,
                       logits1, yT)
        route1(nc, NT, CAP, logits1, consts, tgates[:, 1:2], share1)
        with ExitStack() as st:
            w1, w3 = pairs(st, e1_w1=DC * E1 * F1, e1_w3=DC * E1 * F1)
            split(("e1_w1", w1), ("e1_w3", w3))
            experts1(nc, NT, yT, w1, w3, a["e1_w2"], share1, ident, X, out)


def layout(i, NT=32):
    tok = lambda y: np.ascontiguousarray(np.asarray(y).reshape(-1, D)[:NT * P])
    chunks = lambda w: np.ascontiguousarray(w.reshape(-1, P, w.shape[1]).transpose(1, 0, 2).reshape(P, -1))
    rows = lambda w: chunks(np.asarray(w).T)
    columns = lambda y: np.ascontiguousarray(np.asarray(y).reshape(-1, P).T)
    experts = lambda w: np.ascontiguousarray(
        np.asarray(w).reshape(w.shape[0], -1, P, w.shape[2]).transpose(2, 0, 1, 3).reshape(P, -1))
    pos, itok = (np.asarray(i[k]).reshape(-1)[:NT * P].reshape(NT, P) for k in ("pos_BxS2", "itok_BxS_4096_4607"))
    inv = 1.0 / THETA ** (np.arange(0, HD0, 2, dtype=np.float32) / np.float32(HD0))
    c = np.asarray(i["ctx_2048"]).reshape(-1, D)[:NT * P].reshape(NT, P, DC, P)
    return {
        "x": tok(i["x"]),
        "ctxT": np.ascontiguousarray(c.transpose(3, 0, 2, 1).reshape(P, NT * D)),
        "pos": np.ascontiguousarray(np.stack([itok, pos], 1).transpose(2, 0, 1).reshape(P, NT * 2)),
        "freq": np.ascontiguousarray(np.broadcast_to(inv.astype(np.float32), (P, HALF))),
        "ident": np.eye(P, dtype=np.float32),
        "qnw": np.asarray(i["L0_xattn_q_norm_w"]), "knw": np.asarray(i["L0_xattn_k_norm_w"]),
        "g_xattn": np.asarray(i["g_xattn"]),
        "wq0": rows(i["L0_xattn_Wq"]), "wk0": rows(i["L0_xattn_Wk"]), "wv0": rows(i["L0_xattn_Wv"]),
        "order": np.ascontiguousarray(np.broadcast_to(np.arange(E1, 0, -1, dtype=np.float32), (P, E1))),
        "count": np.ascontiguousarray(np.broadcast_to(np.arange(P, dtype=np.float32), (P, P))),
        "token": np.ascontiguousarray(np.tile(np.arange(NT * P, dtype=np.float32).reshape(NT, P).T, (1, 2))),
        "before": np.triu(np.ones((P, P), np.float16), 1), "ones": np.ones((P, P), np.float16),
        "e0_w0": experts(i["L0_ffn_w0_kernel"]), "e0_w1": experts(i["L0_ffn_w1_kernel"]),
        "e0_wo": experts(i["L0_ffn_wo_kernel"]), "g_ffn": np.asarray(i["g_ffn"]),
        "pair": np.ascontiguousarray((np.arange(P)[:, None] % STRIP // HD1 == np.arange(2)).astype(np.float32)),
        "mask": np.asarray(i["mask_BxS2_ik0"])[:NT * NB],
        "a1_wq": rows(i["L1_xattn_Wq"]), "a1_wk": rows(i["L1_xattn_Wk"]), "a1_wv": rows(i["L1_xattn_Wv"]),
        "a1_wo": rows(i["L1_xattn_Wo"]), "a1_bq": columns(i["L1_xattn_bq"]), "a1_bk": columns(i["L1_xattn_bk"]),
        "a1_bv": np.asarray(i["L1_xattn_bv"]), "a1_bo": np.asarray(i["L1_xattn_bo"]),
        "a1_gamma": np.asarray(i["L1_xattn_ln_gamma"]), "a1_beta": np.asarray(i["L1_xattn_ln_beta"]),
        "a1_rs": np.asarray(i["L1_xattn_residual_scale"]).reshape(1),
        "gate1": rows(i["L1_ffn_gate_w"]), "e1_w1": rows(np.asarray(i["L1_ffn_w1"]).reshape(-1, D)),
        "e1_w3": rows(np.asarray(i["L1_ffn_w3"]).reshape(-1, D)),
        "e1_w2": chunks(np.asarray(i["L1_ffn_w2"]).transpose(0, 2, 1).reshape(-1, D)),
        "wo0": rows(i["L0_xattn_Wo"]), "gate0": chunks(np.asarray(i["L0_ffn_gate_kernel"])),
    }


def kernel(**inputs):
    import concourse.bacc as bacc
    from concourse.bass_utils import run_bass_kernel_spmd

    shape = np.asarray(inputs["x"]).shape
    arrays = {name: np.ascontiguousarray(y) for name, y in layout(inputs).items()}
    nc = bacc.Bacc("TRN2", target_bir_lowering=False, num_devices=1)
    a = {name: nc.dram_tensor(f"in_{name}", y.shape, mybir.dt.from_np(y.dtype), kind="ExternalInput").ap()
         for name, y in arrays.items()}
    out = nc.dram_tensor("out", (64 * S, D), F32, kind="ExternalOutput").ap()
    program(nc, a, out)
    result = run_bass_kernel_spmd(nc, [{f"in_{name}": y for name, y in arrays.items()}], core_ids=[0])
    return result.results[0]["out"].reshape(shape)
```

```python
from contextlib import ExitStack

import numpy as np
import concourse.bass as bass
from concourse import mybir

F32 = mybir.dt.float32
F16 = mybir.dt.float16
I32 = mybir.dt.int32
ALU = mybir.AluOpType
ACT = mybir.ActivationFunctionType
AX_X = mybir.AxisListType.X

P = 128
D = 256
DC = D // P
S = 64
NB = 2
H0, KV0, HD0 = 16, 4, 128
GROUP = H0 // KV0
E0, F0 = 8, 512
FC = F0 // P
E1, F1 = 12, 32
HALF = HD0 // 2
WSCALE = 64.0
EPS_LN = 1e-5
EPS_RMS = 1e-6
THETA = 10000.0
TWO_PI = 2.0 * np.pi
PI_A = 6.28125
PI_B = float(np.float32(np.round((TWO_PI - PI_A) * 2.0**21) / 2.0**21))
PI_C = float(TWO_PI - PI_A - PI_B)
ROUND = 1.5 * 2.0**23


def this(n, t, k):
    return n * t + n + k


def last(n, t, k):
    return n * t + k


def rope_tables(nc, NT, pos, freq_dram, rope_dram, weights, constants, const_in):
    parts = [slice(n, min(2 * NT, n + 16)) for n in range(0, 2 * NT, 16)]
    with ExitStack() as ctx:
        sb = lambda name, shape, dt: ctx.enter_context(nc.sbuf_tensor(name, shape, dt))
        sem = lambda name: ctx.enter_context(nc.semaphore(name))
        pos_i = sb("pos_i", [P, NT * 2], I32)
        pos_f = sb("pos_f", [P, NT * 2, 1], F32)
        freq = sb("freq", [P, 1, HALF], F32)
        angle = sb("angle", [P, NT * 2, HALF], F32)
        turns = sb("turns", [P, NT * 2, HALF], F32)
        table = sb("table", [P, NT * 2, 2, HALF], F32)
        pos_in, freq_set, step, shifted, tables_made, stored = map(sem, (
            "pos_in", "freq_set", "rope_step", "rope_shifted", "tables_made", "rope_stored"))
        split = WeightSplit(nc, ctx, "split_a", weights)
        block = ctx.enter_context(nc.Block())

        @block.sync
        def _(sp):
            sp.dma_start(pos_i[:, :], pos).then_inc(pos_in, 16)
            sp.dma_start(freq[:, 0, :], freq_dram).then_inc(freq_set, 16)
            split.load(sp)
            for tile, src in constants:
                sp.dma_start(tile[:, :], src).then_inc(const_in, 16)
            for n, part in enumerate(parts):
                sp.wait_ge(tables_made, 2 * n + 2)
                sp.dma_start(rope_dram.rearrange("(t p) w -> p t w", p=P)[:, part.start // 2:part.stop // 2, :],
                             table[:, part, :, :].rearrange("p (t s) c d -> p t (s c d)", s=2)).then_inc(stored, 16)
            sp.wait_ge(const_in, 16 * len(constants))
            sp.wait_ge(stored, 16 * len(parts))

        @block.vector
        def _(dve):
            dve.wait_ge(pos_in, 16)
            dve.tensor_copy(pos_f[:, :, 0], pos_i[:, :]).then_inc(step, 1)
            dve.wait_ge(freq_set, 16)
            dve.wait_ge(step, 1)
            steps = 1

            def chain(instruction):
                nonlocal steps
                steps += 1
                instruction.then_inc(step, 1)
                dve.wait_ge(step, steps)

            for part in parts:
                shape = [P, part.stop - part.start, HALF]
                y, r = angle[:, part, :], turns[:, part, :]
                chain(dve.tensor_tensor(y, pos_f[:, part, :].broadcast_to(shape), freq[:, :, :].broadcast_to(shape),
                                        ALU.mult))
                chain(dve.tensor_scalar(r, y, 1.0 / TWO_PI, ROUND, ALU.mult, ALU.add))
                chain(dve.tensor_scalar(r, r, -ROUND, None, ALU.add))
                for pi in (PI_A, PI_B, PI_C):
                    chain(dve.scalar_tensor_tensor(out=y, in0=r, scalar=-pi, in1=y, op0=ALU.mult, op1=ALU.add))
                chain(dve.tensor_scalar(y, y, -3.1415925, 3.1415925, ALU.max, ALU.min))
                chain(dve.tensor_scalar(r, y, np.pi / 2, -TWO_PI, ALU.is_gt, ALU.mult))
                chain(dve.scalar_tensor_tensor(out=r, in0=y, scalar=np.pi / 2, in1=r, op0=ALU.add, op1=ALU.add))
                dve.tensor_scalar(r, r, -3.1415925, 3.1415925, ALU.max, ALU.min).then_inc(shifted, 1)

        @block.gpsimd
        def _(pool):
            split.low(pool)

        @block.scalar
        def _(act):
            share = -(-len(split.pieces) // len(parts))
            for n, part in enumerate(parts):
                split.high(act, n * share, (n + 1) * share)
                act.wait_ge(shifted, n + 1)
                act.activation(table[:, part, 0, :], turns[:, part, :], ACT.Sin).then_inc(tables_made, 1)
                act.activation(table[:, part, 1, :], angle[:, part, :], ACT.Sin).then_inc(tables_made, 1)


class WeightSplit:
    PIECE, SLOTS = 1024, 5

    def __init__(self, nc, stack, tag, jobs):
        sem = lambda name: stack.enter_context(nc.semaphore(f"{tag}_{name}"))
        self.stage = stack.enter_context(nc.sbuf_tensor(f"{tag}_stage", [P, self.SLOTS, self.PIECE], F32))
        self.loaded = [sem(f"loaded{k}") for k in range(self.SLOTS)]
        self.high_made, self.low_made = sem("high_made"), sem("low_made")
        self.pieces = []
        for src, high, low in jobs:
            for c in range(0, src.shape[1], self.PIECE):
                part = slice(c, min(src.shape[1], c + self.PIECE))
                self.pieces.append((src[:, part], high[:, part], low[:, part]))

    def slot(self, n):
        return self.stage[:, n % self.SLOTS, 0:self.pieces[n][0].shape[1]]

    def load(self, sp):
        for n, (src, _, _) in enumerate(self.pieces):
            if n >= self.SLOTS:
                sp.wait_ge(self.low_made, n - self.SLOTS + 1)
            sp.dma_start(self.slot(n), src).then_inc(self.loaded[n % self.SLOTS], 16)

    def high(self, act, first=0, end=None):
        for n, (_, high, _) in list(enumerate(self.pieces))[first:end]:
            act.wait_ge(self.loaded[n % self.SLOTS], 16 * (n // self.SLOTS + 1))
            act.activation(high, self.slot(n), ACT.Copy, scale=WSCALE)
            act.activation(self.slot(n), self.slot(n), ACT.Copy, scale=WSCALE).then_inc(self.high_made, 1)

    def low(self, pool):
        for n, (_, high, low) in enumerate(self.pieces):
            pool.wait_ge(self.high_made, n + 1)
            pool.tensor_tensor(low, self.slot(n), high, ALU.subtract).then_inc(self.low_made, 1)


def attention0(nc, NT, x, ctxT, rope_dram, qnw, knw, g_xattn, wq, wk, wv, wo, gate_dram, ident, X, y1, logits):
    USES = ("k0", "k1", "q0", "q1", "q2", "tk0", "q3", "tq0", "v0", "tq1", "v1", "tk1", "tq2", "tq3")
    USE = {name: n + 1 for n, name in enumerate(USES)}
    BANK = dict(k0=0, k1=1, q0=0, q1=1, q2=0, q3=1, v0=0, v1=1, tq2=0, tq3=1, tk0=2, tq0=2, tq1=2, tk1=2)
    TURN = {name: n + 1 for n, name in enumerate(u for u in USES if u[0] == "t")}
    ROPED = ("k0", "k1", "q0", "q1", "q2", "q3")
    with ExitStack() as ctx:
        sb = lambda name, shape, dt=F32: ctx.enter_context(nc.sbuf_tensor(name, shape, dt))
        ps = lambda name, shape=[P, 512]: ctx.enter_context(nc.psum_tensor(name, shape, F32))
        sem = lambda name: ctx.enter_context(nc.semaphore("a0_" + name))

        gate = sb("gate0", [P, 2])
        tgate = sb("tgate0", [P, 1])
        half_neg = sb("half_neg0", [P, H0])
        qw = sb("qw0", [P, 2, HD0])
        kw = sb("kw0", [P, 2, HD0])
        xt = sb("xt0", [P, D])
        xres = sb("xres0", [P, D])
        xn = sb("xn0", [P, D])
        ctx32 = sb("ctx32", [P, DC, NB, S])
        raw = sb("raw0", [P, 3, 2, HALF])
        tab = sb("tab0", [P, 3, 2, 2, HALF])
        kv_hi = sb("kv_hi", [P, DC, 4, S], F16)
        kv_lo = sb("kv_lo", [P, DC, 4, S], F16)
        stats = sb("stats0", [P, 6])
        mv = sb("mv0", [P, 2])
        rstd = sb("rstd0", [P, 1])
        sq = sb("sq0", [P, 6, 512])
        ssk = sb("ssk", [P, NB * KV0])
        ssq = sb("ssq", [P, H0])
        rk = sb("rk", [P, NB * KV0])
        rq = sb("rq", [P, H0])
        rqT = sb("rqT", [P, NB, H0 // 2])
        k1 = sb("k1", [P, NB, KV0 * HD0])
        k2 = sb("k2", [P, NB, KV0 * HD0])
        q1 = sb("q1", [P, H0 * HD0])
        q2 = sb("q2", [P, H0 * HD0])
        qT = sb("qT0", [P, NB, H0, S])
        kT = sb("kT0", [P, NB, KV0, P])
        v = sb("v0", [P, NB, KV0 * HD0])
        E = sb("E0", [P, 2, 2, P])
        PT = sb("PT0", [P, 2, 2, P])
        mx = sb("mx0", [P, 2, 2])
        nb = sb("nb0", [P, 2, 2])
        es = sb("es0", [P, 2, 2])
        er = sb("er0", [P, 2, 2])
        attn32 = sb("attn32_0", [P, 4, GROUP, S])
        attnT = [sb(f"attnT0_{h}", [P, H0, NB, S], F16) for h in ("hi", "lo")]

        stats_y = sb("stats_y0", [P, 6])
        mv_y = sb("mv_y0", [P, 2])
        rstd_y = sb("rstd_y0", [P, 1])
        yn = sb("yn0", [P, D])
        ynT = sb("ynT0", [P, D])
        router = sb("router0", [P, DC, E0])
        eps_q = sb("eps_q", [P, H0])
        eps_ln = sb("eps_ln0", [P, 1])

        proj = [ps("proj0"), ps("proj1")]
        turnA = ps("turnA")
        bank = proj + [turnA]
        score = [ps("score0"), ps("score1")]
        turnB = [ps("turnB0"), ps("turnB1")]
        outp = ps("outp0")

        x_in, ctx_in, raw_in, xres_in, y1_out, const_in = map(sem, (
            "x_in", "ctx_in", "raw_in", "xres_in", "y1_out", "const_in"))
        pe_xT = sem("pe_xT")
        pe_proj = sem("pe_proj")
        pe_rq = sem("pe_rq")
        pe_score = sem("pe_score")
        pe_PT = sem("pe_PT")
        pe_out = sem("pe_out")
        pe_yT = sem("pe_yT")
        pe_gate = sem("pe_gate")
        dv_y = sem("dv_y")
        dv_gate = sem("dv_gate")
        dv_ln = sem("dv_ln")
        dv_stats = sem("dv_stats")
        dv_xlo = sem("dv_xlo")
        dv_rope = sem("dv_rope")
        dv_ss = sem("dv_ss")
        dv_max = sem("dv_max")
        dv_norm = sem("dv_norm")
        dv_x1 = sem("dv_x1")
        ac_xhi = sem("ac_xhi")
        ac_sq = sem("ac_sq")
        ac_v = sem("ac_v")
        ac_turn = sem("ac_turn")
        ac_rq = sem("ac_rq")
        ac_exp = sem("ac_exp")
        ac_PT = sem("ac_PT")
        ac_out = sem("ac_out")
        ac_yT = sem("ac_yT")
        po_y = sem("po_y")
        po_rstd = sem("po_rstd")
        po_clo = sem("po_clo")
        po_tab = sem("po_tab")
        po_add = sem("po_add")
        po_r = sem("po_r")
        po_lo = sem("po_lo")
        po_const = sem("po_const")
        dv_const = sem("dv_const")
        dv_turn = sem("dv_turn")
        ac_const = sem("ac_const")
        block = ctx.enter_context(nc.Block())

        @block.sync
        def _(sp):
            for dst, src in ((router[:, :, :], gate_dram.rearrange("p (c e) -> p c e", c=DC)),
                             (gate[:, :], g_xattn.partition_broadcast(P)),
                             (qw[:, 0, :], qnw.partition_broadcast(P)), (kw[:, 0, :], knw.partition_broadcast(P)),
                             (qw[:, 1, 0:HALF], qnw[HALF:].partition_broadcast(P)),
                             (qw[:, 1, HALF:], qnw[0:HALF].partition_broadcast(P)),
                             (kw[:, 1, 0:HALF], knw[HALF:].partition_broadcast(P)),
                             (kw[:, 1, HALF:], knw[0:HALF].partition_broadcast(P))):
                sp.dma_start(dst, src).then_inc(const_in, 16)
            for s in (x_in, ctx_in, raw_in, xres_in, y1_out):
                sp.sem_inc(s, 16)

            def load(t):
                sp.wait_ge(dv_ln, last(2, t, 2))
                sp.dma_start(xt[:, :], x[bass.ds(t * P, P), :]).then_inc(x_in, 16)
                sp.wait_ge(po_clo, last(1, t, 1))
                sp.dma_start(ctx32[:, :, :, :], ctxT[:, bass.ds(t * D, D)]
                             .rearrange("p (c b s) -> p c b s", c=DC, b=NB)).then_inc(ctx_in, 16)
                sp.wait_ge(po_tab, last(6, t, 6))
                r = rope_dram[bass.ds(t * P, P), :].rearrange("(b s) (o a d) -> b s o a d", b=NB, o=2, a=2)
                for h in range(NB):
                    sp.dma_start(raw[h * S:(h + 1) * S, 0, :, :], r[h, :, 0, :, :]).then_inc(raw_in, 16)
                    context, own = (slice(0, S), slice(S, P))[::1 - 2 * h]
                    sp.dma_start(raw[context, 1 + h, :, :], r[h, :, 1, :, :]).then_inc(raw_in, 16)
                    sp.dma_start(raw[own, 1 + h, :, :], r[h, :, 0, :, :]).then_inc(raw_in, 16)

            def load_res(p):
                sp.wait_ge(dv_x1, last(1, p, 1))
                sp.dma_start(xres[:, :], x[bass.ds(p * P, P), :]).then_inc(xres_in, 16)

            def store(c):
                sp.wait_ge(dv_y, this(2, c, 2))
                sp.dma_start(y1[bass.ds(c * P, P), :], yn[:, :]).then_inc(y1_out, 16)

            load(0)
            load_res(0)
            load(1)
            load(2)
            with sp.Fori(0, NT - 3) as c:
                store(c)
                load_res(c + 1)
                load(c + 3)
            for c in range(NT - 3, NT):
                store(c)
                if c + 1 < NT:
                    load_res(c + 1)
            sp.wait_ge(y1_out, 16 * (NT + 1))

        @block.gpsimd
        def _(pool):
            pool.memset(half_neg[:, :], -0.5).then_inc(po_const, 1)
            pool.memset(eps_q[:, :], EPS_RMS * WSCALE**2 * HD0).then_inc(po_const, 1)
            pool.memset(eps_ln[:, :], EPS_LN).then_inc(po_const, 1)
            for s, n in ((po_y, 2), (po_rstd, 2), (po_clo, 1), (po_tab, 6), (po_add, 8), (po_r, 8), (po_lo, 8)):
                pool.sem_inc(s, n)
            pool.wait_ge(po_const, 3)

            def part_a(t):
                pool.wait_ge(dv_ln, this(2, t, 1))
                pool.tensor_tensor(rstd[:, :], mv[:, 1:2], eps_ln[:, :], ALU.add).then_inc(po_rstd, 1)
                pool.wait_ge(po_rstd, this(2, t, 1))
                pool.tensor_tensor(rstd[:, :], rstd[:, :], half_neg[:, 0:1], ALU.pow).then_inc(po_rstd, 1)

            def part_a2(t):
                pool.wait_ge(ac_xhi, this(2, t, 1))
                pool.wait_ge(ctx_in, this(16, t, 16))
                pool.tensor_tensor(kv_lo[:, :, 0::3, :], ctx32[:, :, :, :], kv_hi[:, :, 0::3, :],
                                   ALU.subtract).then_inc(po_clo, 1)
                pool.wait_ge(raw_in, 96 * t + 16 + 96)
                pool.wait_ge(dv_rope, last(6, t, 6))
                for n in range(3):
                    w = qw if n == 0 else kw
                    pool.tensor_tensor(tab[:, n, 0, :, :], raw[:, n, 0:1, :].broadcast_to([P, 2, HALF]),
                                       w[:, 0, :].rearrange("p (a d) -> p a d", a=2), ALU.mult).then_inc(po_tab, 1)
                    pool.tensor_tensor(tab[:, n, 1, :, :], raw[:, n, 1:2, :].broadcast_to([P, 2, HALF]),
                                       w[:, 1, :].rearrange("p (a d) -> p a d", a=2), ALU.mult).then_inc(po_tab, 1)

            def finish_k(t, b):
                pool.wait_ge(dv_rope, this(6, t, b + 1))
                pool.tensor_tensor(k1[:, b, :], k1[:, b, :], k2[:, b, :], ALU.add).then_inc(po_add, 1)
                pool.wait_ge(ac_sq, this(6, t, b + 1))
                part = slice(b * KV0, (b + 1) * KV0)
                pool.tensor_tensor(rk[:, part], ssk[:, part], eps_q[:, 0:KV0], ALU.add).then_inc(po_r, 1)
                pool.wait_ge(po_r, this(8, t, 2 * b + 1))
                pool.tensor_tensor(rk[:, part], rk[:, part], half_neg[:, 0:KV0], ALU.pow).then_inc(po_r, 1)
                pool.wait_ge(po_r, this(8, t, 2 * b + 2))
                pool.wait_ge(po_add, this(8, t, 2 * b + 1))
                kb = k1[:, b, :].rearrange("p (h d) -> p h d", h=KV0)
                r = rk[:, part].unsqueeze(2).broadcast_to([P, KV0, HD0])
                pool.tensor_tensor(kb, kb, r, ALU.mult).then_inc(po_add, 1)

            def add_q(t, j):
                pool.wait_ge(dv_rope, this(6, t, 3 + j))
                part = slice(512 * j, 512 * (j + 1))
                pool.tensor_tensor(q1[:, part], q1[:, part], q2[:, part], ALU.add).then_inc(po_add, 1)

            def rms_q(t, half):
                part = slice(8 * half, 8 * (half + 1))
                pool.wait_ge(dv_ss, this(2, t, 1 + half))
                if half == 0:
                    pool.wait_ge(pe_rq, last(1, t, 1))
                pool.tensor_tensor(rq[:, part], ssq[:, part], eps_q[:, part], ALU.add).then_inc(po_r, 1)
                pool.wait_ge(po_r, this(8, t, 5 + 2 * half))
                pool.tensor_tensor(rq[:, part], rq[:, part], half_neg[:, part], ALU.pow).then_inc(po_r, 1)

            def low_out(p, u):
                b, g = divmod(u, KV0)
                part = slice(GROUP * g, GROUP * (g + 1))
                pool.wait_ge(ac_out, this(8, p, u + 1))
                pool.tensor_tensor(attnT[1][:, part, b, :], attn32[:, u % 4, :, :], attnT[0][:, part, b, :],
                                   ALU.subtract).then_inc(po_lo, 1)

            def part_c(p):
                pool.wait_ge(dv_y, this(2, p, 1))
                pool.tensor_tensor(rstd_y[:, :], mv_y[:, 1:2], eps_ln[:, :], ALU.add).then_inc(po_y, 1)
                pool.wait_ge(po_y, this(2, p, 1))
                pool.tensor_tensor(rstd_y[:, :], rstd_y[:, :], half_neg[:, 0:1], ALU.pow).then_inc(po_y, 1)

            pool.wait_ge(const_in, 16 * 8)
            for w in (qw, kw):
                pool.tensor_scalar(w[:, 1, 0:HALF], w[:, 1, 0:HALF], -1.0, None, ALU.mult).then_inc(po_const, 1)
            pool.wait_ge(po_const, 5)
            def iteration(t, p, c):
                if t is not None:
                    part_a(t)
                    part_a2(t)
                if c is not None:
                    part_c(c)
                for u in range(8):
                    if t is not None and u < 2:
                        finish_k(t, u)
                    if t is not None and 2 <= u < 6:
                        add_q(t, u - 2)
                    if t is not None and u in (4, 6):
                        rms_q(t, (u - 4) // 2)
                    if p is not None and u >= 1:
                        low_out(p, u - 1)
                if p is not None:
                    low_out(p, 7)

            iteration(0, None, None)
            iteration(1, 0, None)
            with pool.Fori(0, NT - 2) as c:
                iteration(c + 2, c + 1, c)
            iteration(None, NT - 1, NT - 2)
            iteration(None, None, NT - 1)

        @block.tensor
        def _(pe):
            for s, n in ((pe_xT, 1), (pe_proj, 14), (pe_rq, 1), (pe_score, 8), (pe_PT, 8), (pe_out, 9), (pe_yT, 1), (pe_gate, 1)):
                pe.sem_inc(s, n)
            pe.wait_ge(const_in, 16 * 8)

            def x_turn(t):
                pe.wait_ge(dv_ln, this(2, t, 2))
                pe.wait_ge(ac_rq, last(1, t, 1))
                for c in range(DC):
                    i = pe.transpose(turnA[:, c * P:(c + 1) * P], xn[:, c * P:(c + 1) * P], ident[:, :])
                i.then_inc(pe_xT, 1)

            def mm3(out, left, right):
                steps = [(c, a, b) for c in range(DC) for a, b in ((0, 0), (0, 1), (1, 0))]
                for n, (c, a, b) in enumerate(steps):
                    i = pe.matmul(out, left(c, a), right(c, b), start=(n == 0), stop=(n == len(steps) - 1))
                return i

            kv = (kv_hi, kv_lo)

            def wait_bank(t, name, c):
                uses = [u for u in USES if BANK[u] == BANK[name]]
                n = uses.index(name)
                before = uses[n - 1]
                if n == 0 and name == "tk0":
                    pe.wait_ge(dv_xlo, this(1, t, 1))
                    if c is not None:
                        pe.wait_ge(dv_gate, this(1, c, 1))
                elif n == 0:
                    pe.wait_ge(ac_turn, last(6, t, TURN[before]))
                elif before in ROPED:
                    pe.wait_ge(dv_rope, this(6, t, ROPED.index(before) + 1))
                    pe.wait_ge(ac_sq, this(6, t, ROPED.index(before) + 1))
                elif before[0] == "v":
                    pe.wait_ge(ac_v, this(2, t, int(before[1]) + 1))
                else:
                    pe.wait_ge(ac_turn, this(6, t, TURN[before]))

            def project(t, name, c=None):
                if name == "k0":
                    pe.wait_ge(po_clo, this(1, t, 1))
                    pe.wait_ge(dv_xlo, this(1, t, 1))
                    pe.wait_ge(ac_xhi, this(2, t, 2))
                wait_bank(t, name, c)
                kind, n = name[0], int(name[1])
                tokens = slice(1, 3) if kind == "q" else slice(2 * n, 2 * n + 2)
                w = {"q": wq, "k": wk, "v": wv}[kind]
                at = lambda c: c * 2048 + n * 512 if kind == "q" else c * 512
                mm3(bank[BANK[name]][:, :], lambda c, a: kv[a][:, c, tokens, :],
                    lambda c, a: w[a][:, at(c):at(c) + 512]).then_inc(pe_proj, 1)

            def turn(t, name, c=None):
                n = int(name[2])
                pe.wait_ge(po_add, this(8, t, 2 * n + 2 if name[1] == "k" else 5 + n))
                wait_bank(t, name, c)
                for g in range(4):
                    y = k1[:, n, g * HD0:(g + 1) * HD0] if name[1] == "k" else q1[:, (4 * n + g) * HD0:(4 * n + g + 1) * HD0]
                    i = pe.transpose(bank[BANK[name]][:, g * P:(g + 1) * P], y, ident[:, :])
                i.then_inc(pe_proj, 1)

            def move_rq(t):
                pe.wait_ge(po_r, this(8, t, 8))
                pe.wait_ge(ac_turn, this(6, t, TURN["tk1"]))
                r = rq[:, :].rearrange("p (m j) -> p j m", j=2)
                for j in range(2):
                    for b in range(NB):
                        i = pe.matmul(turnA[j * S:(j + 1) * S, b * 8:(b + 1) * 8], ident[:, b * S:(b + 1) * S],
                                      r[:, j, :], start=True, stop=True)
                i.then_inc(pe_rq, 1)

            def scores(p, u):
                b, g = divmod(u, KV0)
                if u < 4:
                    pe.wait_ge(ac_turn, this(6, p, TURN[f"tq{g}"]))
                pe.wait_ge(ac_exp, this(8, p, u - 1) if u >= 2 else last(8, p, 7 + u))
                for m in range(2):
                    h = GROUP * g + 2 * m
                    i = pe.matmul(score[u % 2][:, m * P:(m + 1) * P], qT[:, b, h:h + 2, :], kT[:, b, g, :],
                                  start=True, stop=True)
                i.then_inc(pe_score, 1)

            def turn_P(p, u):
                pe.wait_ge(dv_norm, this(16, p, 2 * u + 2))
                pe.wait_ge(ac_PT, this(8, p, u - 1) if u >= 2 else last(8, p, 7 + u))
                for m in range(2):
                    i = pe.transpose(turnB[u % 2][:, m * P:(m + 1) * P], E[:, u % 2, m, :], ident[:, :])
                i.then_inc(pe_PT, 1)

            def weigh_v(p, u, c):
                b, g = divmod(u, KV0)
                pe.wait_ge(ac_PT, this(8, p, u + 1))
                if u == 0:
                    if c is not None:
                        pe.wait_ge(dv_x1, this(1, c, 1))
                    pe.wait_ge(ac_v, this(2, p, 2))
                else:
                    pe.wait_ge(ac_out, this(8, p, u))
                pe.matmul(outp[:, 0:256], v[:, b, g * HD0:(g + 1) * HD0], PT[:, u % 2, :, :], start=True,
                          stop=True).then_inc(pe_out, 1)

            def out_projection(p, heads):
                pe.wait_ge(ac_out, this(8, p, 8))
                pe.wait_ge(po_lo, this(8, p, 6 if heads[-1] < 2 * GROUP else 8))
                for h in heads:
                    for a, b in ((0, 0), (0, 1), (1, 0)):
                        i = pe.matmul(outp[:, 0:D], attnT[a][:, h, :, :], wo[b][:, h * D:(h + 1) * D],
                                      start=(h == 0 and a == b), stop=(h == H0 - 1 and a == 1))
                if h == H0 - 1:
                    i.then_inc(pe_out, 1)

            def y_turn(c, t):
                pe.wait_ge(dv_y, this(2, c, 2))
                if t is not None:
                    pe.wait_ge(dv_xlo, this(1, t, 1))
                for k in range(DC):
                    i = pe.transpose(turnA[:, k * P:(k + 1) * P], yn[:, k * P:(k + 1) * P], ident[:, :])
                i.then_inc(pe_yT, 1)

            def route(c):
                pe.wait_ge(ac_yT, this(1, c, 1))
                for k in range(DC):
                    i = pe.matmul(turnA[:, 0:E0], ynT[:, k * P:(k + 1) * P], router[:, k, :], start=(k == 0),
                                  stop=(k == DC - 1))
                i.then_inc(pe_gate, 1)

            def iteration(t, p, c):
                if c is not None:
                    out_projection(c, range(H0 // 2))
                if t is not None:
                    x_turn(t)
                if c is not None:
                    out_projection(c, range(H0 // 2, H0))
                for u, (block, turned) in enumerate((
                        ("k0", None), ("k1", None), ("q0", None), ("q1", None), ("q2", "tk0"), ("q3", "tq0"),
                        ("v0", "tq1"), ("v1", "tk1"))):
                    if p is not None:
                        turn_P(p, u)
                        if u + 2 < 8:
                            scores(p, u + 2)
                    if t is not None:
                        project(t, block)
                    if p is not None:
                        weigh_v(p, u, c)
                    if t is not None and turned:
                        turn(t, turned, c)
                    if c is not None and u == 1:
                        y_turn(c, t)
                    if c is not None and u == 2:
                        route(c)
                if t is not None:
                    turn(t, "tq2")
                    scores(t, 0)
                    turn(t, "tq3")
                    move_rq(t)
                    scores(t, 1)

            iteration(0, None, None)
            iteration(1, 0, None)
            with pe.Fori(0, (NT - 2) // 2) as half:
                for k in range(2):
                    c = half * 2 + k
                    iteration(c + 2, c + 1, c)
            iteration(None, NT - 1, NT - 2)
            iteration(None, None, NT - 1)

        @block.vector
        def _(dve):
            for s, n in ((dv_ln, 2), (dv_xlo, 1), (dv_rope, 6), (dv_ss, 2), (dv_max, 16), (dv_norm, 16), (dv_x1, 1), (dv_y, 2), (dv_gate, 1)):
                dve.sem_inc(s, n)

            def statistics(t):
                dve.sem_clear(dv_stats)
                dve.wait_ge(x_in, this(16, t, 16))
                dve.bn_stats(stats[:, :], xt[:, :]).then_inc(dv_stats, 1)
                dve.wait_ge(dv_stats, 1)
                dve.bn_aggr(mv[:, :], stats[:, :]).then_inc(dv_ln, 1)

            def standard_x(t):
                dve.wait_ge(po_rstd, this(2, t, 2))
                dve.wait_ge(pe_xT, last(1, t, 1))
                dve.tensor_scalar(xn[:, :], xt[:, :], mv[:, 0:1], rstd[:, 0:1], ALU.subtract,
                                  ALU.mult).then_inc(dv_ln, 1)

            def low_x(t):
                dve.wait_ge(ac_xhi, this(2, t, 2))
                dve.tensor_tensor(kv_lo[:, :, 1:3, :], turnA[:, 0:D].rearrange("p (c b s) -> p c b s", c=DC, b=NB),
                                  kv_hi[:, :, 1:3, :], ALU.subtract).then_inc(dv_xlo, 1)

            def rope(t, n):
                dve.wait_ge(pe_proj, this(14, t, USE[ROPED[n]]))
                if n == 0:
                    dve.wait_ge(po_tab, this(6, t, 6))
                    dve.wait_ge(pe_proj, last(14, t, 14))
                which = 0 if n >= 2 else 1 + n
                if n < 2:
                    o1, o2 = k1[:, n, :], k2[:, n, :]
                else:
                    part = slice(512 * (n - 2), 512 * (n - 1))
                    o1, o2 = q1[:, part], q2[:, part]
                y = bank[BANK[ROPED[n]]][:, :].rearrange("p (h a d) -> p h a d", a=2, d=HALF)
                shape = [P, 4, 2, HALF]
                cos, sin = (tab[:, which, s:s + 1, :, :].broadcast_to(shape) for s in range(2))
                dve.tensor_tensor(o1.rearrange("p (h a d) -> p h a d", a=2, d=HALF), y, cos, ALU.mult)
                dve.tensor_tensor(o2.rearrange("p (h a d) -> p h a d", a=2, d=HALF), y[:, :, ::-1, :], sin,
                                  ALU.mult).then_inc(dv_rope, 1)

            def sum_squares(t, n):
                dve.wait_ge(ac_sq, this(6, t, 2 * n))
                if n == 2:
                    dve.wait_ge(po_r, last(8, t, 8))
                dve.tensor_reduce(ssq[:, 8 * (n - 2):8 * (n - 1)],
                                  sq[:, 2 * n - 2:2 * n, :].rearrange("p n (h d) -> p (n h) d", h=4), AX_X,
                                  ALU.add).then_inc(dv_ss, 1)

            def maximum(p, u):
                b, g = divmod(u, KV0)
                dve.wait_ge(pe_score, this(8, p, u + 1))
                dve.tensor_reduce(mx[:, u % 2, :], score[u % 2][:, 0:256].rearrange("p (m k) -> p m k", m=2), AX_X,
                                  ALU.max).then_inc(dv_max, 1)
                dve.wait_ge(dv_max, this(16, p, 2 * u + 1))
                if u == 0:
                    dve.wait_ge(ac_rq, this(1, p, 1))
                dve.wait_ge(ac_exp, this(8, p, u - 1) if u >= 2 else last(8, p, 7 + u))
                dve.scalar_tensor_tensor(out=nb[:, u % 2, :], in0=mx[:, u % 2, :], scalar=-1.0,
                                         in1=rqT[:, b, 2 * g:2 * g + 2], op0=ALU.mult,
                                         op1=ALU.mult).then_inc(dv_max, 1)

            def normalize(p, u):
                dve.wait_ge(ac_exp, this(8, p, u + 1))
                dve.reciprocal(er[:, u % 2, :], es[:, u % 2, :]).then_inc(dv_norm, 1)
                dve.wait_ge(dv_norm, this(16, p, 2 * u + 1))
                dve.tensor_tensor(E[:, u % 2, :, :], E[:, u % 2, :, :],
                                  er[:, u % 2, :].unsqueeze(2).broadcast_to([P, 2, P]), ALU.mult).then_inc(dv_norm, 1)

            def residual(p):
                dve.wait_ge(pe_out, this(9, p, 9))
                dve.wait_ge(xres_in, this(16, p, 16))
                x1 = X[:, bass.ds(p, 1), :].rearrange("p o d -> p (o d)")
                dve.scalar_tensor_tensor(out=x1, in0=outp[:, 0:D], scalar=tgate[:, 0:1], in1=xres[:, :],
                                         op0=ALU.mult, op1=ALU.add).then_inc(dv_x1, 1)
                dve.sem_clear(dv_stats)
                dve.wait_ge(dv_x1, this(1, p, 1))
                dve.sem_inc(dv_turn, 1)
                dve.bn_stats(stats_y[:, :], x1).then_inc(dv_stats, 1)
                dve.wait_ge(dv_stats, 1)
                dve.bn_aggr(mv_y[:, :], stats_y[:, :]).then_inc(dv_y, 1)

            def standard_y(p):
                dve.wait_ge(po_y, this(2, p, 2))
                dve.wait_ge(pe_yT, last(1, p, 1))
                dve.wait_ge(y1_out, last(16, p, 16))
                dve.tensor_scalar(yn[:, :], X[:, bass.ds(p, 1), :].rearrange("p o d -> p (o d)"), mv_y[:, 0:1], rstd_y[:, 0:1], ALU.subtract,
                                  ALU.mult).then_inc(dv_y, 1)

            def keep_logits(c):
                dve.wait_ge(pe_gate, this(1, c, 1))
                dve.tensor_scalar(logits[:, bass.ds(c * E0, E0)], turnA[:, 0:E0], 1.0, None,
                                  ALU.mult).then_inc(dv_gate, 1)

            def iteration(t, p, c):
                if t is not None:
                    statistics(t)
                if p is not None:
                    maximum(p, 0)
                    maximum(p, 1)
                if t is not None:
                    standard_x(t)
                if p is not None:
                    normalize(p, 0)
                if t is not None:
                    low_x(t)
                if p is not None:
                    normalize(p, 1)
                if c is not None:
                    residual(c)
                for u in range(8):
                    if t is not None and u == 5:
                        sum_squares(t, 2)
                    if p is not None and u + 2 < 8:
                        maximum(p, u + 2)
                    if p is not None and 2 <= u + 1 < 8:
                        normalize(p, u + 1)
                    if t is not None and u == 6:
                        sum_squares(t, 3)
                    if t is not None and u < 6:
                        rope(t, u)
                    if c is not None and u == 0:
                        standard_y(c)
                    if c is not None and u == 3:
                        keep_logits(c)

            dve.wait_ge(ac_const, 2)
            iteration(0, None, None)
            iteration(1, 0, None)
            with dve.Fori(0, NT - 2) as c:
                iteration(c + 2, c + 1, c)
            iteration(None, NT - 1, NT - 2)
            iteration(None, None, NT - 1)

        @block.scalar
        def _(act):
            for s, n in ((ac_xhi, 2), (ac_sq, 6), (ac_v, 2), (ac_turn, 6), (ac_rq, 1), (ac_exp, 8), (ac_PT, 8),
                         (ac_out, 8), (ac_yT, 1)):
                act.sem_inc(s, n)
            act.wait_ge(const_in, 16 * 8)
            act.activation(tgate[:, :], gate[:, 0:1], ACT.Tanh).then_inc(ac_const, 1)
            act.wait_ge(ac_const, 1)
            act.activation(tgate[:, :], tgate[:, :], ACT.Copy, scale=1.0 / WSCALE).then_inc(ac_const, 1)

            def high_context(t):
                act.wait_ge(ctx_in, this(16, t, 16))
                act.wait_ge(pe_proj, last(14, t, USE["v1"]))
                act.activation(kv_hi[:, :, 0::3, :], ctx32[:, :, :, :], ACT.Copy).then_inc(ac_xhi, 1)

            def high_x(t):
                act.wait_ge(pe_xT, this(1, t, 1))
                act.activation(kv_hi[:, :, 1:3, :], turnA[:, 0:D].rearrange("p (c b s) -> p c b s", c=DC, b=NB),
                               ACT.Copy).then_inc(ac_xhi, 1)

            def squares(t, n):
                act.wait_ge(pe_proj, this(14, t, USE[ROPED[n]]))
                act.wait_ge(dv_rope, this(6, t, n + 1))
                if n < 2:
                    act.wait_ge(po_r, last(8, t, 2 * n + 1))
                    for h in range(KV0):
                        part = slice(h * HD0, (h + 1) * HD0)
                        i = act.activation(sq[:, n, part], bank[BANK[ROPED[n]]][:, part], ACT.Square,
                                           accum_out=ssk[:, n * KV0 + h:n * KV0 + h + 1])
                    i.then_inc(ac_sq, 1)
                    return
                act.wait_ge(dv_ss, last(2, t, n // 2))
                act.activation(sq[:, n, :], bank[BANK[ROPED[n]]][:, :], ACT.Square).then_inc(ac_sq, 1)

            def values(t, b):
                act.wait_ge(pe_proj, this(14, t, USE[f"v{b}"]))
                act.activation(v[:, b, :], bank[BANK[f"v{b}"]][:, :], ACT.Copy, scale=1.0 / WSCALE).then_inc(ac_v, 1)

            def turned(t, name):
                n, y = int(name[2]), bank[BANK[name]]
                act.wait_ge(pe_proj, this(14, t, USE[name]))
                if name[1] == "k":
                    act.activation(kT[:, n, :, :], y[:, :].rearrange("p (g k) -> p g k", g=KV0),
                                   ACT.Copy).then_inc(ac_turn, 1)
                else:
                    act.activation(qT[:, :, 4 * n:4 * n + 4, :].rearrange("p b h s -> p h b s"),
                                   y[:, :].rearrange("p (h b s) -> p h b s", h=4, b=NB), ACT.Copy).then_inc(ac_turn, 1)

            def moved_rq(t):
                act.wait_ge(pe_rq, this(1, t, 1))
                act.activation(rqT[:, :, :], turnA[:, 0:16].rearrange("p (b m) -> p b m", b=NB),
                               ACT.Copy, scale=HD0**0.5).then_inc(ac_rq, 1)

            def exponentials(p, u):
                b, g = divmod(u, KV0)
                act.wait_ge(dv_max, this(16, p, 2 * u + 2))
                act.wait_ge(pe_PT, this(8, p, u - 1) if u >= 2 else last(8, p, 7 + u))
                for m in range(2):
                    i = act.activation(E[:, u % 2, m, :], score[u % 2][:, m * P:(m + 1) * P], ACT.Exp,
                                       bias=nb[:, u % 2, m:m + 1], scale=rqT[:, b, 2 * g + m:2 * g + m + 1],
                                       accum_out=es[:, u % 2, m:m + 1])
                i.then_inc(ac_exp, 1)

            def turned_P(p, u):
                act.wait_ge(pe_PT, this(8, p, u + 1))
                act.wait_ge(pe_out, this(9, p, u - 1) if u >= 2 else last(9, p, 7 + u))
                act.activation(PT[:, u % 2, :, :], turnB[u % 2][:, 0:256].rearrange("p (m q) -> p m q", m=2),
                               ACT.Copy).then_inc(ac_PT, 1)

            def turned_out(p, u):
                b, g = divmod(u, KV0)
                act.wait_ge(pe_out, this(9, p, u + 1))
                act.wait_ge(po_lo, this(8, p, u - 3) if u >= 4 else last(8, p, 5 + u))
                y = outp[:, 0:256].rearrange("p (h s) -> p h s", h=GROUP)
                act.activation(attnT[0][:, GROUP * g:GROUP * (g + 1), b, :], y, ACT.Copy)
                act.activation(attn32[:, u % 4, :, :], y, ACT.Copy).then_inc(ac_out, 1)

            def turned_y(c):
                act.wait_ge(pe_yT, this(1, c, 1))
                act.wait_ge(pe_gate, last(1, c, 1))
                act.activation(ynT[:, :], turnA[:, 0:D], ACT.Copy).then_inc(ac_yT, 1)

            def iteration(t, p, c):
                if t is not None:
                    high_context(t)
                if p is not None:
                    exponentials(p, 0)
                    exponentials(p, 1)
                if t is not None:
                    high_x(t)
                for u in range(8):
                    if p is not None:
                        turned_P(p, u)
                    if t is not None and 1 <= u < 7:
                        squares(t, u - 1)
                    if p is not None:
                        if u + 2 < 8:
                            exponentials(p, u + 2)
                        turned_out(p, u)
                    if t is not None and u >= 6:
                        values(t, u - 6)
                    if t is not None and u >= 4:
                        turned(t, ("tk0", "tq0", "tq1", "tk1")[u - 4])
                    if c is not None and u == 1:
                        turned_y(c)
                if t is not None:
                    turned(t, "tq2")
                    turned(t, "tq3")
                    moved_rq(t)

            iteration(0, None, None)
            iteration(1, 0, None)
            with act.Fori(0, NT - 2) as c:
                iteration(c + 2, c + 1, c)
            iteration(None, NT - 1, NT - 2)
            iteration(None, None, NT - 1)


class Chain:

    def __init__(self, engine, semaphore):
        self.engine, self.semaphore, self.steps = engine, semaphore, 0

    def __call__(self, instruction):
        self.steps += 1
        instruction.then_inc(self.semaphore, 1)
        self.engine.wait_ge(self.semaphore, self.steps)


def top2(dve, chain, values, order, hot, best, t, m):
    shape = list(values.shape)
    wide = lambda y: y.unsqueeze(2).broadcast_to(shape)
    for slot in range(2):
        chain(dve.tensor_reduce(best[:, slot, :], values, AX_X, ALU.max))
        chain(dve.tensor_tensor(t, values, wide(best[:, slot, :]), ALU.is_equal))
        chain(dve.tensor_tensor(t, t, order, ALU.mult))
        chain(dve.tensor_reduce(m, t, AX_X, ALU.max))
        chain(dve.tensor_tensor(hot[:, slot, :, :], t, wide(m), ALU.is_equal))
        if slot == 0:
            chain(dve.scalar_tensor_tensor(out=values, in0=hot[:, 0, :, :], scalar=-1e30, in1=values, op0=ALU.mult,
                                           op1=ALU.add))


def route0(nc, NT, J, logits, consts, dest, weight, expert, index, weights):
    B = 2 * NT
    with ExitStack() as ctx:
        sb = lambda name, shape, dt=F32: ctx.enter_context(nc.sbuf_tensor(name, shape, dt))
        sem = lambda name: ctx.enter_context(nc.semaphore("r0_" + name))
        hot = sb("r0_hot", [P, 2, NT, E0])
        hot16 = sb("r0_hot16", [P, B * E0], F16)
        best = sb("r0_best", [P, 2, NT])
        t = sb("r0_t", [P, NT, E0])
        m = sb("r0_m", [P, NT])
        diff = sb("r0_diff", [P, NT])
        zero = sb("r0_zero", [P, B])
        upto = sb("r0_upto", [P, E0, B])
        row = sb("r0_row", [P, B, E0])
        tiles = sb("r0_tiles", [P, E0])
        end = sb("r0_end", [P, E0])
        base = sb("r0_base", [P, E0])
        behind = sb("r0_behind", [P, J, E0])
        expf = sb("r0_expf", [P, J])
        rowf = sb("r0_rowf", [P, B])
        tile_of = sb("r0_tile_of", [P, B])
        place_of = sb("r0_place_of", [P, B])
        here = sb("r0_here", [P, 2, 4, P])
        token = sb("r0_token", [P, 2, 4, J])
        rank = ctx.enter_context(nc.psum_tensor("r0_rank", [P, B * E0], F32))
        total = ctx.enter_context(nc.psum_tensor("r0_total", [P, B * E0], F32))
        table = ctx.enter_context(nc.psum_tensor("r0_table", [P, 512], F32))
        dv_step, dv_hot, dv_diff, ac_exp, pe_count, dv_dest, dv_pick, pe_pick = map(sem, (
            "dv_step", "dv_hot", "dv_diff", "ac_exp", "pe_count", "dv_dest", "dv_pick", "pe_pick"))
        split = WeightSplit(nc, ctx, "split_b", weights)
        block = ctx.enter_context(nc.Block())
        order = consts["order"][:, 0:E0].unsqueeze(1).broadcast_to([P, NT, E0])

        @block.vector
        def _(dve):
            chain = Chain(dve, dv_step)
            values = logits[:, :].rearrange("p (t e) -> p t e", e=E0)
            top2(dve, chain, values, order, hot, best, t[:, :, :], m[:, :])
            dve.tensor_copy(hot16[:, :], hot[:, :, :, :].rearrange("p k t e -> p (k t e)")).then_inc(dv_hot, 1)
            dve.tensor_tensor(diff[:, :], best[:, 1, :], best[:, 0, :], ALU.subtract).then_inc(dv_diff, 1)
            dve.wait_ge(ac_exp, 1)
            chain(dve.tensor_scalar(m[:, :], diff[:, :], 1.0, None, ALU.add))
            chain(dve.reciprocal(weight[:, 0, :], m[:, :]))
            chain(dve.tensor_tensor(weight[:, 1, :], weight[:, 0, :], diff[:, :], ALU.mult))
            chain(dve.memset(zero[:, :], 0.0))
            dve.wait_ge(pe_count, 2)
            counts = total[:, :].rearrange("p (b e) -> p e b", e=E0)
            for e in range(E0):
                i = dve.tensor_tensor_scan(upto[:, e, :], counts[:, e, :], zero[:, :], 0.0, ALU.add, ALU.add)
            chain(i)
            chain(dve.tensor_scalar(tiles[:, :], upto[:, :, B - 1], 1.0 / P, (P - 1) / P - 0.5 + 0.5 / P, ALU.mult,
                                    ALU.add))
            chain(dve.tensor_scalar(tiles[:, :], tiles[:, :], ROUND, -ROUND, ALU.add, ALU.add))
            chain(dve.tensor_tensor_scan(end[:, :], tiles[:, :], zero[:, 0:E0], 0.0, ALU.add, ALU.add))
            chain(dve.tensor_tensor(base[:, :], end[:, :], tiles[:, :], ALU.subtract))
            chain(dve.tensor_scalar(base[:, :], base[:, :], float(P), None, ALU.mult))
            chain(dve.tensor_tensor(row[:, :, :], upto[:, :, :].rearrange("p e b -> p b e"),
                                    total[:, :].rearrange("p (b e) -> p b e", e=E0), ALU.subtract))
            chain(dve.tensor_tensor(row[:, :, :], row[:, :, :], rank[:, :].rearrange("p (b e) -> p b e", e=E0), ALU.add))
            chain(dve.tensor_tensor(row[:, :, :], row[:, :, :], base[:, :].unsqueeze(1).broadcast_to([P, B, E0]),
                                    ALU.add))
            chain(dve.tensor_tensor(row[:, :, :], row[:, :, :], hot[:, :, :, :].rearrange("p k t e -> p (k t) e"),
                                    ALU.mult))
            chain(dve.tensor_reduce(rowf[:, :], row[:, :, :], AX_X, ALU.add))
            chain(dve.tensor_copy(dest[:, :, :].rearrange("p k t -> p (k t)"), rowf[:, :]))
            chain(dve.tensor_tensor(behind[:, :, :], end[:, :].unsqueeze(1).broadcast_to([P, J, E0]),
                                    consts["count"][:, 0:J].unsqueeze(2).broadcast_to([P, J, E0]), ALU.is_le))
            chain(dve.tensor_reduce(expf[:, :], behind[:, :, :], AX_X, ALU.add))
            chain(dve.tensor_scalar(expf[:, :], expf[:, :], E0 - 1.0, None, ALU.min))
            chain(dve.tensor_copy(expert[:, :], expf[:, :]))
            chain(dve.tensor_scalar(tile_of[:, :], rowf[:, :], 1.0 / P, -0.5 + 0.5 / P, ALU.mult, ALU.add))
            chain(dve.tensor_scalar(tile_of[:, :], tile_of[:, :], ROUND, -ROUND, ALU.add, ALU.add))
            chain(dve.scalar_tensor_tensor(out=place_of[:, :], in0=tile_of[:, :], scalar=-float(P), in1=rowf[:, :],
                                           op0=ALU.mult, op1=ALU.add))
            dve.sem_inc(dv_pick, 2)
            dve.sem_inc(dv_dest, 1)
            with dve.Fori(0, B // 8) as r2:
                for k in range(2):
                    r = r2 * 2 + k
                    part = bass.ds(r * 4, 4)
                    dve.wait_ge(pe_pick, r2 * 2 + 1 + k)
                    dve.tensor_tensor(here[:, k, :, :], consts["count"][:, 0:P].unsqueeze(1).broadcast_to([P, 4, P]),
                                      place_of[:, part].unsqueeze(2).broadcast_to([P, 4, P]),
                                      ALU.is_equal).then_inc(dv_pick, 1)
                    dve.tensor_tensor(token[:, k, :, :], consts["count"][:, 0:J].unsqueeze(1).broadcast_to([P, 4, J]),
                                      tile_of[:, part].unsqueeze(2).broadcast_to([P, 4, J]),
                                      ALU.is_equal).then_inc(dv_dest, 1)
                    dve.wait_ge(dv_dest, r2 * 2 + 2 + k)
                    dve.tensor_tensor(token[:, k, :, :], token[:, k, :, :],
                                      consts["token"][:, part].unsqueeze(2).broadcast_to([P, 4, J]),
                                      ALU.mult).then_inc(dv_pick, 1)
            dve.wait_ge(pe_pick, B // 4 + 2)
            chain(dve.tensor_copy(index[:, :], table[:, 0:J]))

        @block.scalar
        def _(act):
            split.high(act, 0, 3)
            act.wait_ge(dv_diff, 1)
            act.activation(diff[:, :], diff[:, :], ACT.Exp).then_inc(ac_exp, 1)
            split.high(act, 3)

        @block.sync
        def _(sp):
            split.load(sp)

        @block.gpsimd
        def _(pool):
            split.low(pool)

        @block.tensor
        def _(pe):
            pe.wait_ge(dv_hot, 1)
            pe.matmul(rank[:, :], consts["before"][:, :], hot16[:, :], start=True, stop=True).then_inc(pe_count, 1)
            pe.matmul(total[:, :], consts["ones"][:, :], hot16[:, :], start=True, stop=True).then_inc(pe_count, 1)
            pe.sem_inc(pe_pick, 2)

            def pick(r2, k, first, final):
                pe.wait_ge(dv_pick, (r2 * 2 + k) * 2 + 4)
                for q in range(4):
                    i = pe.matmul(table[:, 0:J], here[:, k, q, :], token[:, k, q, :], start=first and q == 0,
                                  stop=final and q == 3)
                i.then_inc(pe_pick, 1)

            pick(0, 0, True, False)
            pick(0, 1, False, B // 8 == 1)
            if B // 8 > 2:
                with pe.Fori(1, B // 8 - 1) as r2:
                    pick(r2, 0, False, False)
                    pick(r2, 1, False, False)
            if B // 8 > 1:
                pick(B // 8 - 1, 0, False, False)
                pick(B // 8 - 1, 1, False, True)


def experts0(nc, NT, J, y1, w0, w1, wo, expert, index, ident, out):
    with ExitStack() as ctx:
        sb = lambda name, shape, dt=F32: ctx.enter_context(nc.sbuf_tensor(name, shape, dt))
        ps = lambda name: ctx.enter_context(nc.psum_tensor(name, [P, 512], F32))
        sem = lambda name: ctx.enter_context(nc.semaphore("e0_" + name))
        now = sb("e0_now", [P, 2], I32)
        rows = sb("e0_rows", [P, 2, D])
        xT = [sb(f"e0_xT{h}", [P, 2, D], F16) for h in ("hi", "lo")]
        silu = sb("e0_silu", [P, 2, F0])
        inter = sb("e0_inter", [P, 2, F0])
        iT = [sb(f"e0_iT{h}", [P, 2, F0], F16) for h in ("hi", "lo")]
        result = sb("e0_result", [P, 2, D])
        turn_x = ps("e0_turn_x")
        up0 = [ps(f"e0_up0{k}") for k in range(2)]
        up1 = [ps(f"e0_up1{k}") for k in range(2)]
        turn_i = [ps(f"e0_turn_i{k}") for k in range(2)]
        down = ps("e0_down")
        rows_in = [sem(f"rows_in{k}") for k in range(2)]
        rows_out = [sem(f"rows_out{k}") for k in range(2)]
        po_turn = sem("po_turn")
        dv_now = sem("dv_now")
        pe_x = sem("pe_x")
        ac_x = sem("ac_x")
        dv_x = sem("dv_x")
        pe_up0 = sem("pe_up0")
        pe_up1 = sem("pe_up1")
        ac_silu = sem("ac_silu")
        dv_inter = sem("dv_inter")
        pe_i = sem("pe_i")
        ac_i = sem("ac_i")
        dv_i = sem("dv_i")
        pe_down = sem("pe_down")
        dv_down = sem("dv_down")
        block = ctx.enter_context(nc.Block())
        def done(t, ago=0):
            return t + 3 - ago

        def landed(n):
            return n * 16 + 32

        def walk(engine, step):
            step(0, 0, 0, True, False, True)
            with engine.Fori(0, J // 2 - 1) as n:
                step(n * 2 + 1, n, 1, True, True, True)
                step(n * 2 + 2, n + 1, 0, True, True, True)
            step(J - 1, J // 2 - 1, 1, True, True, False)
            step(J, J // 2, 0, False, True, False)

        @block.gpsimd
        def _(pool):
            with pool.Fori(0, J // 2) as n:
                for k in range(2):
                    pool.wait_ge(dv_now, done(n * 2 + k))
                    pool.wait_ge(pe_x, done(n * 2 + k, 2))
                    pool.sem_inc(po_turn, 1)
                    pool.indirect_dma_start(rows[:, k, :], None, y1,
                                            bass.IndirectOffsetOnAxis(ap=now[:, k:k + 1], axis=0)
                                            ).then_inc(rows_in[k], 16)

        @block.sync
        def _(sp):
            for k in range(2):
                sp.sem_inc(rows_out[k], 16)
            with sp.Fori(0, J // 2) as n:
                for k in range(2):
                    sp.wait_ge(dv_down, done(n * 2 + k))
                    sp.dma_start(out[bass.ds((n * 2 + k) * P, P), :], result[:, k, :]).then_inc(rows_out[k], 16)
            for k in range(2):
                sp.wait_ge(rows_out[k], 16 * (J // 2) + 16)

        @block.tensor
        def _(pe):
            for s in (pe_x, pe_up0, pe_up1, pe_i, pe_down):
                pe.sem_inc(s, 2)

            def turn_rows(t, n, k):
                pe.wait_ge(rows_in[k], n * 16 + 16)
                pe.wait_ge(ac_x, done(t, 1))
                pe.wait_ge(dv_x, done(t, 1))
                for c in range(DC):
                    i = pe.transpose(turn_x[:, c * P:(c + 1) * P], rows[:, k, c * P:(c + 1) * P], ident[:, :])
                i.then_inc(pe_x, 1)

            def product(bank, k, left, right, chunks, width, e):
                trio = [(c, a, b) for c in range(chunks) for a, b in ((0, 0), (0, 1), (1, 0))]
                for q, (c, a, b) in enumerate(trio):
                    i = pe.matmul(bank[:, 0:width], left[a][:, k, c * P:(c + 1) * P],
                                  right[b][:, bass.ds(e * (chunks * width) + c * width, width)], start=(q == 0),
                                  stop=(q == len(trio) - 1))
                return i

            def expert_of(t):
                return pe.value_load(expert[0:1, bass.ds(t, 1)], min_val=0, max_val=E0 - 1)

            def step(t, n, k, up, rest, more, e_before, e, ahead=False):
                e_next = None
                if up:
                    pe.wait_ge(ac_x, done(t))
                    pe.wait_ge(dv_x, done(t))
                    pe.wait_ge(ac_silu, done(t, 2))
                    product(up0[k], k, xT, w0, DC, F0, e).then_inc(pe_up0, 1)
                if rest:
                    pe.wait_ge(dv_inter, done(t, 1))
                    pe.wait_ge(ac_i, done(t, 3))
                    pe.wait_ge(dv_i, done(t, 3))
                    for c in range(FC):
                        i = pe.transpose(turn_i[1 - k][:, c * P:(c + 1) * P], inter[:, 1 - k, c * P:(c + 1) * P],
                                         ident[:, :])
                    i.then_inc(pe_i, 1)
                if up:
                    pe.wait_ge(dv_inter, done(t, 2))
                    product(up1[k], k, xT, w1, DC, F0, e).then_inc(pe_up1, 1)
                if ahead:
                    e_next = expert_of(t + 1)
                if more:
                    turn_rows(t + 1, n + k, 1 - k)
                if rest:
                    if e_before is None:
                        e_before = expert_of(t - 1)
                    pe.wait_ge(ac_i, done(t, 1))
                    pe.wait_ge(dv_i, done(t, 1))
                    pe.wait_ge(dv_down, done(t, 2))
                    product(down, 1 - k, iT, wo, FC, D, e_before).then_inc(pe_down, 1)
                return e_next

            turn_rows(0, 0, 0)
            step(0, 0, 0, True, False, True, None, expert_of(0))

            def steps(t, n, count):
                before, e = None, expert_of(t)
                for m in range(count):
                    e_next = step(t + m, n + (m + 1) // 2, (m + 1) % 2, True, True, True, before, e, ahead=m < count - 1)
                    before, e = e, e_next

            with pe.Fori(0, (J - 2) // 4) as q:
                steps(q * 4 + 1, q * 2, 4)
            if (J - 2) % 4:
                steps(J - 3, J // 2 - 2, 2)
            e = expert_of(J - 1)
            step(J - 1, J // 2 - 1, 1, True, True, False, None, e)
            step(J, J // 2, 0, False, True, False, e, None)

        @block.scalar
        def _(act):
            for s in (ac_x, ac_silu, ac_i):
                act.sem_inc(s, 2)

            def high_x(t, k):
                act.wait_ge(pe_x, done(t))
                act.wait_ge(pe_up1, done(t, 2))
                act.activation(xT[0][:, k, :], turn_x[:, 0:D], ACT.Copy).then_inc(ac_x, 1)

            def step(t, n, k, up, rest, more):
                if rest:
                    act.wait_ge(pe_i, done(t, 1))
                    act.wait_ge(pe_down, done(t, 3))
                    act.activation(iT[0][:, 1 - k, :], turn_i[1 - k][:, :], ACT.Copy).then_inc(ac_i, 1)
                if up:
                    act.wait_ge(pe_up0, done(t))
                    act.wait_ge(dv_inter, done(t, 2))
                    act.activation(silu[:, k, :], up0[k][:, :], ACT.Silu, scale=1.0 / WSCALE).then_inc(ac_silu, 1)
                if more:
                    high_x(t + 1, 1 - k)

            high_x(0, 0)
            walk(act, step)

        @block.vector
        def _(dve):
            for s in (dv_now, dv_x, dv_inter, dv_i, dv_down):
                dve.sem_inc(s, 2)

            def fetch(t, n, k):
                if not (isinstance(t, int) and t < 2):
                    dve.wait_ge(rows_in[k], n * 16)
                dve.tensor_scalar(now[:, k:k + 1], index[:, bass.ds(t, 1)], 0.0, None, ALU.add).then_inc(dv_now, 1)

            def low_x(t, k):
                dve.wait_ge(ac_x, done(t))
                dve.tensor_tensor(xT[1][:, k, :], turn_x[:, 0:D], xT[0][:, k, :], ALU.subtract).then_inc(dv_x, 1)

            def step(t, n, k, up, rest, more, fetches=True):
                if rest:
                    dve.wait_ge(ac_i, done(t, 1))
                    dve.tensor_tensor(iT[1][:, 1 - k, :], turn_i[1 - k][:, :], iT[0][:, 1 - k, :],
                                      ALU.subtract).then_inc(dv_i, 1)
                if up:
                    dve.wait_ge(ac_silu, done(t))
                    dve.wait_ge(pe_up1, done(t))
                    dve.wait_ge(pe_i, done(t, 2))
                    dve.tensor_tensor(inter[:, k, :], silu[:, k, :], up1[k][:, :], ALU.mult).then_inc(dv_inter, 1)
                if more:
                    low_x(t + 1, 1 - k)
                if more and fetches:
                    fetch(t + 2, n + 1, k)
                if rest:
                    dve.wait_ge(pe_down, done(t, 1))
                    dve.wait_ge(rows_out[1 - k], landed(n + k) - 32)
                    dve.tensor_scalar(result[:, 1 - k, :], down[:, 0:D], 1.0 / WSCALE**2, None,
                                      ALU.mult).then_inc(dv_down, 1)

            fetch(0, 0, 0)
            fetch(1, 0, 1)
            low_x(0, 0)
            step(0, 0, 0, True, False, True)
            with dve.Fori(0, J // 2 - 2) as n:
                step(n * 2 + 1, n, 1, True, True, True)
                step(n * 2 + 2, n + 1, 0, True, True, True)
            step(J - 3, J // 2 - 2, 1, True, True, True)
            step(J - 2, J // 2 - 1, 0, True, True, True, fetches=False)
            step(J - 1, J // 2 - 1, 1, True, True, False)
            step(J, J // 2, 0, False, True, False)



H1, HD1 = 16, 16
STRIP = 32
STRIPS = P // STRIP
LIMIT = 50.0
SCALE1 = HD1**-0.5


def attention1(nc, NT, a, consts, X, sorted0, dest, weight, wq, wk, wv, router, ident, tgates, logits, yT):
    with ExitStack() as ctx:
        sb = lambda name, shape, dt=F32: ctx.enter_context(nc.sbuf_tensor("a1_" + name, shape, dt))
        ps = lambda name: ctx.enter_context(nc.psum_tensor("a1_" + name, [P, 512], F32))
        sem = lambda name: ctx.enter_context(nc.semaphore("a1_" + name))
        wo = sb("wo", [P, DC, D])
        bq = sb("bq", [P, DC])
        bk = sb("bk", [P, DC])
        bv = sb("bv", [P, D])
        bvz = sb("bvz", [P, D])
        bo = sb("bo", [P, D])
        gamma = sb("gamma", [P, D])
        beta = sb("beta", [P, D])
        rs = sb("rs", [P, 1])
        gates = sb("gates", [P, 4])
        half_neg = sb("half_neg", [P, 1])
        eps = sb("eps", [P, 1])
        mask_i = sb("mask_i", [P, NT, S], I32)
        bound = sb("bound", [P, NT, S])
        share = sb("share", [P, 2, NT])
        now = sb("now", [P, 2], I32)
        rows = sb("rows", [P, 2, D])
        xn = sb("xn", [P, D])
        stats = sb("stats", [P, 6])
        mv = sb("mv", [P, 3, 2])
        rstd = sb("rstd", [P, 3])
        xT = [sb(f"xT{h}", [P, DC, P], F16) for h in ("hi", "lo")]
        ctx32 = sb("ctx32", [P, DC, NB, 2, S])
        cT = [sb(f"cT{h}", [P, DC, NB, 2, S], F16) for h in ("hi", "lo")]
        qT = sb("qT", [P, DC, P])
        kT = sb("kT", [P, DC, P])
        kz = sb("kz", [P, DC, NB, 2, S])
        vz = sb("vz", [P, NB, D])
        E = sb("E", [P, STRIPS, DC, 2, S])
        sums = sb("sums", [P, H1])
        PT = sb("PT", [P, STRIPS, DC, P])
        cxT = sb("cxT", [P, DC, P])
        delta = sb("delta", [P, D])
        yn = sb("yn", [P, D])
        score = [ps(f"score{r}") for r in range(STRIPS)]
        turn = ps("turn")
        proj = ps("proj")
        turnP = ps("turnP")
        outp = ps("outp")

        ctx_in, const_in = map(sem, ("ctx_in", "const_in"))
        rows_in = [sem(f"rows_in{k}") for k in range(2)]
        v_const, a_const, a_turn, v_turn, p_const, p_turn, v_stats = map(sem, (
            "v_const", "a_const", "a_turn", "v_turn", "p_const", "p_turn", "v_stats"))
        e_x, e_qk, e_v, e_sc, e_PT, e_cx, e_d, e_y, e_log = map(sem, (
            "e_x",
            "e_qk",
            "e_v",
            "e_sc",
            "e_PT",
            "e_cx",
            "e_d",
            "e_y",
            "e_log"))
        v_now, v_x2, v_ln, v_xlo, v_cap, v_sum, v_norm, v_d, v_y, v_ylo, v_log = map(sem, (
            "v_now",
            "v_x2",
            "v_ln",
            "v_xlo",
            "v_cap",
            "v_sum",
            "v_norm",
            "v_d",
            "v_y",
            "v_ylo",
            "v_log"))
        a_chi, a_xhi, a_qk, a_exp, a_PT, a_cx, a_v, a_yhi = map(sem, (
            "a_chi",
            "a_xhi",
            "a_qk",
            "a_exp",
            "a_PT",
            "a_cx",
            "a_v",
            "a_yhi"))
        p_clo, p_rstd, p_rstd_d, p_rstd_y, p_kz, p_beta, p_v, p_x3 = map(sem, (
            "p_clo",
            "p_rstd",
            "p_rstd_d",
            "p_rstd_y",
            "p_kz",
            "p_beta",
            "p_v",
            "p_x3"))
        block = ctx.enter_context(nc.Block())

        def row(t):
            return X[:, bass.ds(t, 1), :].rearrange("p o d -> p (o d)")

        def walk(engine, iteration):
            iteration(0, None, None, None, 2)
            iteration(1, 0, None, None, 2)
            iteration(2, 1, 0, None, 2)
            iteration(3, 2, 1, 0, 2)
            with engine.Fori(0, (NT - 6) // 2) as half:
                for k in (1, 2):
                    c = half * 2 + k
                    iteration(c + 3, c + 2, c + 1, c, 2)
            iteration(NT - 2, NT - 3, NT - 4, NT - 5, 1)
            iteration(NT - 1, NT - 2, NT - 3, NT - 4, 0)
            iteration(None, NT - 1, NT - 2, NT - 3, 0)
            iteration(None, None, NT - 1, NT - 2, 0)
            iteration(None, None, None, NT - 1, 0)

        def before(c):
            return None if c is None or (isinstance(c, int) and c == 0) else c - 1

        loads = [(wo[:, :, :], a["a1_wo"].rearrange("p (c d) -> p c d", c=DC)), (bq[:, :], a["a1_bq"]),
                 (bk[:, :], a["a1_bk"])]
        loads += [(dst[:, :], a[name].partition_broadcast(P)) for dst, name in (
            (bv, "a1_bv"), (bo, "a1_bo"), (gamma, "a1_gamma"), (beta, "a1_beta"), (rs, "a1_rs"))]
        loads += [(gates[:, 0:2], a["g_ffn"].partition_broadcast(P)), (gates[:, 2:4], a["g_xattn"].partition_broadcast(P))]
        loads += [(mask_i[b * S:(b + 1) * S, :, :],
                   a["mask"].rearrange("(t b) k -> b t k", b=NB)[b].partition_broadcast(S)) for b in range(NB)]
        LOADED = 16 * len(loads)

        @block.sync
        def _(sp):
            for dst, src in loads:
                sp.dma_start(dst, src).then_inc(const_in, 16)
            sp.sem_inc(ctx_in, 32)

            def load_context(n):
                sp.wait_ge(p_clo, last(1, n, 1))
                for k in range(2):
                    sp.dma_start(ctx32[:, :, :, k, :], a["ctxT"][:, bass.ds(n * D, D)]
                                 .rearrange("p (c b s) -> p c b s", c=DC, b=NB)).then_inc(ctx_in, 16)

            with sp.Fori(0, NT) as n:
                load_context(n)

        @block.gpsimd
        def _(pool):
            pool.memset(half_neg[:, :], -0.5).then_inc(p_const, 1)
            pool.memset(eps[:, :], EPS_LN).then_inc(p_const, 1)
            pool.memset(vz[:, :, :], 0.0).then_inc(p_const, 1)
            for s, n in ((p_clo, 1), (p_rstd, 2), (p_rstd_d, 2), (p_rstd_y, 2), (p_kz, 1), (p_beta, 1), (p_v, 1), (p_x3, 2)):
                pool.sem_inc(s, n)
            pool.wait_ge(p_const, 3)
            pool.wait_ge(v_const, 1)

            def power(n, s, t):
                pool.tensor_tensor(rstd[:, n:n + 1], mv[:, n, 1:2], eps[:, :], ALU.add).then_inc(s, 1)
                pool.wait_ge(s, this(2, t, 1))
                pool.tensor_tensor(rstd[:, n:n + 1], rstd[:, n:n + 1], half_neg[:, :], ALU.pow).then_inc(s, 1)

            def gather(n):
                pool.wait_ge(v_now, this(1, n, 1))
                pool.wait_ge(v_x2, last(2, n, 2))
                pool.sem_inc(p_turn, 1)
                for k in range(2):
                    pool.indirect_dma_start(rows[:, k, :], None, sorted0,
                                            bass.IndirectOffsetOnAxis(ap=now[:, k:k + 1], axis=0)
                                            ).then_inc(rows_in[k], 16)

            def iteration(n, t, p, c, ahead):
                if c is not None:
                    pool.wait_ge(v_d, this(3, c, 2))
                    power(1, p_rstd_d, c)
                if ahead >= 1 and not (isinstance(n, int) and n == 0):
                    gather(n + 1)
                if c is not None:
                    pool.wait_ge(v_d, this(3, c, 3))
                    pool.tensor_tensor(delta[:, :], delta[:, :], gamma[:, :], ALU.mult).then_inc(p_x3, 1)
                    pool.wait_ge(p_x3, this(2, c, 1))
                    pool.tensor_tensor(row(c), row(c), delta[:, :], ALU.add).then_inc(p_x3, 1)
                if t is not None:
                    pool.wait_ge(a_qk, this(1, t, 1))
                    if p is not None:
                        pool.wait_ge(e_sc, this(2, p, 2))
                    for h in range(DC):
                        pair = consts["pair"][:, :].unsqueeze(2).broadcast_to([P, 2, S])
                        for b in range(NB):
                            i = pool.tensor_tensor(kz[:, h, b, :, :], kT[:, h:h + 1, b * S:(b + 1) * S]
                                                   .broadcast_to([P, 2, S]), pair, ALU.mult)
                    i.then_inc(p_kz, 1)
                if c is not None:
                    pool.wait_ge(v_y, this(2, c, 1))
                    power(2, p_rstd_y, c)
                if n is not None:
                    pool.wait_ge(v_ln, this(2, n, 2))
                    pool.tensor_tensor(row(n), row(n), beta[:, :], ALU.add).then_inc(p_beta, 1)
                if ahead >= 1:
                    pool.wait_ge(v_ln, this(2, n + 1, 1))
                    power(0, p_rstd, n + 1)
                if n is not None:
                    pool.wait_ge(a_chi, this(1, n, 1))
                    pool.wait_ge(ctx_in, this(32, n, 32))
                    pool.tensor_tensor(cT[1][:, :, :, :, :], ctx32[:, :, :, :, :], cT[0][:, :, :, :, :],
                                       ALU.subtract).then_inc(p_clo, 1)
                if t is not None:
                    pool.wait_ge(a_v, this(1, t, 1))
                    pool.tensor_tensor(vz[:, :, :], vz[:, :, :], bvz[:, :].unsqueeze(1).broadcast_to([P, NB, D]),
                                       ALU.add).then_inc(p_v, 1)

            gather(0)
            gather(1)
            pool.wait_ge(v_const, 4)
            pool.wait_ge(v_ln, this(2, 0, 1))
            power(0, p_rstd, 0)
            walk(pool, iteration)

        @block.tensor
        def _(pe):
            for s, n in ((e_x, 1), (e_qk, 1), (e_v, 1), (e_sc, 2), (e_PT, 2), (e_cx, 1), (e_d, 1), (e_y, 1), (e_log, 1)):
                pe.sem_inc(s, n)
            pe.wait_ge(const_in, LOADED)
            trio = [(c, i, j) for c in range(DC) for i, j in ((0, 0), (0, 1), (1, 0))]

            def mm3(out, left, right):
                for n, (c, i, j) in enumerate(trio):
                    m = pe.matmul(out, left(c, i), right(c, j), start=(n == 0), stop=(n == len(trio) - 1))
                return m

            def turn_x(n, c):
                pe.wait_ge(v_ln, this(2, n, 2))
                pe.wait_ge(v_xlo, last(1, n, 1))
                if c is not None:
                    pe.wait_ge(v_log, last(1, c, 1))
                for c in range(DC):
                    i = pe.transpose(turn[:, c * P:(c + 1) * P], xn[:, c * P:(c + 1) * P], ident[:, :])
                i.then_inc(e_x, 1)

            def scores(p, half):
                if half == 0:
                    pe.wait_ge(p_kz, this(1, p, 1))
                    pe.wait_ge(a_qk, this(1, p, 1))
                pe.wait_ge(v_cap, last(2, p, half + 1))
                for r in (2 * half, 2 * half + 1):
                    strip = slice(r * STRIP, (r + 1) * STRIP)
                    for b in range(NB):
                        for h in range(DC):
                            i = pe.matmul(score[r][b * S:(b + 1) * S, h * P:(h + 1) * P],
                                          qT[strip, h, b * S:(b + 1) * S], kz[strip, h, b, :, :], start=True, stop=True)
                i.then_inc(e_sc, 1)

            def query_key(t):
                pe.wait_ge(v_xlo, this(1, t, 1))
                pe.wait_ge(p_clo, this(1, t, 1))
                pe.wait_ge(a_v, last(1, t, 1))
                for h in range(DC):
                    part = lambda c: slice(c * D + h * P, c * D + (h + 1) * P)
                    mm3(proj[:, h * P:(h + 1) * P], lambda c, i: wq[i][:, part(c)], lambda c, j: xT[j][:, c, :])
                    i = mm3(proj[:, D + h * P:D + (h + 1) * P], lambda c, i: wk[i][:, part(c)],
                            lambda c, j: cT[j][:, c, :, 0, :])
                i.then_inc(e_qk, 1)

            def value(t, b):
                pe.wait_ge(a_qk, this(1, t, 1))
                i = mm3(proj[:, b * D:(b + 1) * D], lambda c, i: cT[i][:, c, b, :, :],
                        lambda c, j: wv[j][:, c * D:(c + 1) * D])
                if b == NB - 1:
                    i.then_inc(e_v, 1)

            def turn_P(p, half):
                pe.wait_ge(v_norm, this(2, p, half + 1))
                pe.wait_ge(a_PT, last(2, p, 2) if half == 0 else this(2, p, 1))
                for n in range(4):
                    r, h = 2 * half + n // 2, n % 2
                    i = pe.transpose(turnP[:, n * P:(n + 1) * P], E[:, r, h, :, :], ident[:, :])
                i.then_inc(e_PT, 1)

            def weigh(p, half):
                pe.wait_ge(a_PT, this(2, p, half + 1))
                if half == 0:
                    pe.wait_ge(v_d, last(3, p, 1))
                    pe.wait_ge(p_v, this(1, p, 1))
                for r in (2 * half, 2 * half + 1):
                    strip = slice(r * STRIP, (r + 1) * STRIP)
                    for h in range(DC):
                        for b in range(NB):
                            i = pe.matmul(outp[strip, h * P + b * S:h * P + (b + 1) * S],
                                          vz[:, b, h * P + r * STRIP:h * P + (r + 1) * STRIP],
                                          PT[:, r, h, b * S:(b + 1) * S], start=True, stop=True)
                if half == 1:
                    i.then_inc(e_cx, 1)

            def result(p):
                pe.wait_ge(a_cx, this(1, p, 1))
                for h in range(DC):
                    i = pe.matmul(outp[:, 0:D], cxT[:, h, :], wo[:, h, :], start=(h == 0), stop=(h == DC - 1))
                i.then_inc(e_d, 1)

            def turn_y(c, n):
                pe.wait_ge(v_y, this(2, c, 2))
                pe.wait_ge(v_log, last(1, c, 1))
                if n is not None:
                    pe.wait_ge(v_xlo, this(1, n, 1))
                for k in range(DC):
                    i = pe.transpose(turn[:, k * P:(k + 1) * P], yn[:, k * P:(k + 1) * P], ident[:, :])
                i.then_inc(e_y, 1)

            def route(c):
                pe.wait_ge(v_ylo, this(1, c, 1))
                for n, (k, i, j) in enumerate(trio):
                    m = pe.matmul(turn[:, 0:E1], yT[i][:, k, bass.ds(c * P, P)], router[j][:, k * E1:(k + 1) * E1],
                                  start=(n == 0), stop=(n == len(trio) - 1))
                m.then_inc(e_log, 1)

            def iteration(n, t, p, c, ahead):
                if before(c) is not None:
                    route(before(c))
                if t is not None:
                    query_key(t)
                if p is not None:
                    turn_P(p, 0)
                if n is not None:
                    turn_x(n, c)
                if t is not None:
                    value(t, 0)
                if p is not None:
                    weigh(p, 0)
                    turn_P(p, 1)
                if t is not None:
                    value(t, 1)
                if p is not None:
                    weigh(p, 1)
                if t is not None:
                    scores(t, 0)
                if c is not None:
                    turn_y(c, n)
                if p is not None:
                    result(p)
                if t is not None:
                    scores(t, 1)

            walk(pe, iteration)
            route(NT - 1)

        @block.vector
        def _(dve):
            chain = Chain(dve, v_const)
            for s, n in ((v_now, 1), (v_x2, 2), (v_ln, 2), (v_xlo, 1), (v_cap, 2), (v_sum, 6), (v_norm, 2),
                         (v_d, 3), (v_y, 2), (v_ylo, 1), (v_log, 1)):
                dve.sem_inc(s, n)
            dve.wait_ge(const_in, LOADED)
            dve.wait_ge(a_const, 1)
            chain(dve.tensor_scalar(beta[:, :], beta[:, :], tgates[:, 3:4], None, ALU.mult))
            chain(dve.tensor_scalar(gamma[:, :], gamma[:, :], tgates[:, 3:4], None, ALU.mult))
            chain(dve.memset(bvz[:, :], 0.0))
            for j in range(2):
                view = lambda y: y[j * S:(j + 1) * S, :].rearrange("p (m j d) -> p m j d", j=2, d=HD1)[:, :, j, :]
                i = dve.tensor_copy(view(bvz), view(bv))
            chain(i)
            chain(dve.tensor_scalar(rs[:, :], rs[:, :], 0.0, 0.3, ALU.max, ALU.min))
            chain(dve.tensor_scalar(bo[:, :], bo[:, :], rs[:, 0:1], None, ALU.mult))
            chain(dve.tensor_scalar(share[:, :, :], weight[:, :, :], tgates[:, 0:1], None, ALU.mult))
            chain(dve.tensor_scalar(bound[:, :, :], mask_i[:, :, :], 0.5, 2 * LIMIT / SCALE1, ALU.is_gt, ALU.mult))
            chain(dve.tensor_scalar(bound[:, :, :], bound[:, :, :], -LIMIT / SCALE1, None, ALU.add))

            def fetch(t):
                if not (isinstance(t, int) and t == 0):
                    for k in range(2):
                        dve.wait_ge(rows_in[k], t * 16)
                dve.tensor_scalar(now[:, :].unsqueeze(2), dest[:, :, bass.ds(t, 1)], 0.0, None,
                                  ALU.add).then_inc(v_now, 1)

            def sum_x2(t):
                dve.wait_ge(rows_in[0], t * 16 + 16)
                dve.scalar_tensor_tensor(out=row(t), in0=rows[:, 0, :], scalar=share[:, 0, bass.ds(t, 1)],
                                         in1=row(t), op0=ALU.mult, op1=ALU.add).then_inc(v_x2, 1)
                dve.wait_ge(rows_in[1], t * 16 + 16)
                dve.wait_ge(v_x2, this(2, t, 1))
                dve.scalar_tensor_tensor(out=row(t), in0=rows[:, 1, :], scalar=share[:, 1, bass.ds(t, 1)],
                                         in1=row(t), op0=ALU.mult, op1=ALU.add).then_inc(v_x2, 1)

            def moments(n, source, before, value, s):
                dve.sem_clear(v_stats)
                dve.wait_ge(before, value)
                dve.sem_inc(v_turn, 1)
                dve.bn_stats(stats[:, :], source).then_inc(v_stats, 1)
                dve.wait_ge(v_stats, 1)
                dve.bn_aggr(mv[:, n, :], stats[:, :]).then_inc(s, 1)

            def standard(n, out, source, s):
                dve.tensor_scalar(out, source, mv[:, n, 0:1], rstd[:, n:n + 1], ALU.subtract, ALU.mult).then_inc(s, 1)

            def cap(p, half):
                dve.wait_ge(e_sc, this(2, p, half + 1))
                dve.wait_ge(e_PT, last(2, p, half + 1))
                for r in (2 * half, 2 * half + 1):
                    i = dve.scalar_tensor_tensor(
                        out=E[:, r, :, :, :].rearrange("p h j k -> p (h j) k"),
                        in0=score[r][:, 0:D].rearrange("p (n k) -> p n k", k=S), scalar=-LIMIT / SCALE1,
                        in1=bound[:, bass.ds(p, 1), :].broadcast_to([P, 4, S]), op0=ALU.max, op1=ALU.min)
                i.then_inc(v_cap, 1)

            def normalize(p, half):
                dve.wait_ge(a_exp, this(2, p, half + 1))
                e = E[:, 2 * half:2 * half + 2, :, :, :].rearrange("p r h j k -> p (r h j) k")
                s = sums[:, 8 * half:8 * half + 8]
                dve.tensor_reduce(s, e, AX_X, ALU.add).then_inc(v_sum, 1)
                dve.wait_ge(v_sum, this(6, p, 3 * half + 1))
                dve.scalar_tensor_tensor(out=s, in0=s, scalar=1e-8, in1=s, op0=ALU.mult, op1=ALU.add).then_inc(v_sum, 1)
                dve.wait_ge(v_sum, this(6, p, 3 * half + 2))
                dve.reciprocal(s, s).then_inc(v_sum, 1)
                dve.wait_ge(v_sum, this(6, p, 3 * half + 3))
                dve.tensor_tensor(e, e, s.unsqueeze(2).broadcast_to([P, 8, S]), ALU.mult).then_inc(v_norm, 1)

            def result(c):
                dve.wait_ge(e_d, this(1, c, 1))
                dve.wait_ge(p_x3, last(2, c, 2))
                dve.scalar_tensor_tensor(out=delta[:, :], in0=outp[:, 0:D], scalar=rs[:, 0:1], in1=bo[:, :],
                                         op0=ALU.mult, op1=ALU.add).then_inc(v_d, 1)
                moments(1, delta[:, :], v_d, this(3, c, 1), v_d)

            def keep_logits(c):
                dve.wait_ge(e_log, this(1, c, 1))
                dve.tensor_scalar(logits[:, bass.ds(c * E1, E1)], turn[:, 0:E1], 1.0 / WSCALE, None,
                                  ALU.mult).then_inc(v_log, 1)

            def iteration(n, t, p, c, ahead):
                if p is not None:
                    cap(p, 0)
                if c is not None:
                    result(c)
                if before(c) is not None:
                    keep_logits(before(c))
                if p is not None:
                    cap(p, 1)
                    normalize(p, 0)
                if c is not None:
                    dve.wait_ge(p_rstd_d, this(2, c, 2))
                    standard(1, delta[:, :], delta[:, :], v_d)
                if n is not None:
                    dve.wait_ge(p_rstd, this(2, n, 2))
                    dve.wait_ge(e_x, last(1, n, 1))
                    standard(0, xn[:, :], row(n), v_ln)
                if p is not None:
                    normalize(p, 1)
                if n is not None:
                    dve.wait_ge(a_xhi, this(1, n, 1))
                    dve.tensor_tensor(xT[1][:, :, :], turn[:, 0:D].rearrange("p (c k) -> p c k", c=DC), xT[0][:, :, :],
                                      ALU.subtract).then_inc(v_xlo, 1)
                if c is not None:
                    moments(2, row(c), p_x3, this(2, c, 2), v_y)
                if ahead >= 1:
                    sum_x2(n + 1)
                if ahead >= 2:
                    fetch(n + 2)
                if c is not None:
                    dve.wait_ge(p_rstd_y, this(2, c, 2))
                    dve.wait_ge(e_y, last(1, c, 1))
                    standard(2, yn[:, :], row(c), v_y)
                if ahead >= 1:
                    moments(0, row(n + 1), v_x2, this(2, n + 1, 2), v_ln)
                if c is not None:
                    dve.wait_ge(a_yhi, this(1, c, 1))
                    dve.tensor_tensor(yT[1][:, :, bass.ds(c * P, P)], turn[:, 0:D].rearrange("p (c k) -> p c k", c=DC),
                                      yT[0][:, :, bass.ds(c * P, P)], ALU.subtract).then_inc(v_ylo, 1)

            fetch(0)
            sum_x2(0)
            fetch(1)
            moments(0, row(0), v_x2, this(2, 0, 2), v_ln)
            walk(dve, iteration)
            keep_logits(NT - 1)

        @block.scalar
        def _(act):
            for s, n in ((a_chi, 1), (a_xhi, 1), (a_qk, 1), (a_exp, 2), (a_PT, 2), (a_cx, 1), (a_v, 1), (a_yhi, 1)):
                act.sem_inc(s, n)
            act.wait_ge(const_in, LOADED)
            act.activation(tgates[:, :], gates[:, :], ACT.Tanh).then_inc(a_const, 1)

            def high_context(n):
                act.wait_ge(ctx_in, this(32, n, 32))
                act.wait_ge(e_v, last(1, n, 1))
                act.activation(cT[0][:, :, :, :, :], ctx32[:, :, :, :, :], ACT.Copy).then_inc(a_chi, 1)

            def exponentials(p, half):
                act.wait_ge(v_cap, this(2, p, half + 1))
                e = E[:, 2 * half:2 * half + 2, :, :, :]
                act.activation(e, e, ACT.Exp, scale=SCALE1).then_inc(a_exp, 1)

            def keep_value(t):
                act.wait_ge(e_v, this(1, t, 1))
                act.wait_ge(e_cx, last(1, t, 1))
                for j in range(2):
                    half = slice(j * S, (j + 1) * S)
                    view = lambda y: y.rearrange("p (b m j d) -> p (b m) j d", b=NB, j=2, d=HD1)[:, :, j, :]
                    i = act.activation(view(vz[half, :, :].rearrange("p b n -> p (b n)")),
                                       view(proj[half, :]), ACT.Copy, scale=1.0 / WSCALE)
                i.then_inc(a_v, 1)

            def turned_P(p, half):
                act.wait_ge(e_PT, this(2, p, half + 1))
                act.wait_ge(e_cx, last(1, p, 1))
                act.activation(PT[:, 2 * half:2 * half + 2, :, :].rearrange("p r h q -> p (r h) q"),
                               turnP[:, :].rearrange("p (n q) -> p n q", q=P), ACT.Copy).then_inc(a_PT, 1)

            def iteration(n, t, p, c, ahead):
                if p is not None:
                    exponentials(p, 0)
                    exponentials(p, 1)
                if t is not None:
                    act.wait_ge(e_qk, this(1, t, 1))
                    if p is not None:
                        act.wait_ge(e_sc, this(2, p, 2))
                    act.wait_ge(p_kz, last(1, t, 1))
                    for h in range(DC):
                        act.activation(qT[:, h, :], proj[:, h * P:(h + 1) * P], ACT.Identity, bias=bq[:, h:h + 1],
                                       scale=1.0 / WSCALE)
                        i = act.activation(kT[:, h, :], proj[:, D + h * P:D + (h + 1) * P], ACT.Identity,
                                           bias=bk[:, h:h + 1], scale=1.0 / WSCALE)
                    i.then_inc(a_qk, 1)
                if p is not None:
                    turned_P(p, 0)
                if n is not None:
                    act.wait_ge(e_x, this(1, n, 1))
                    act.wait_ge(e_qk, last(1, n, 1))
                    act.activation(xT[0][:, :, :], turn[:, 0:D].rearrange("p (c k) -> p c k", c=DC),
                                   ACT.Copy).then_inc(a_xhi, 1)
                if p is not None:
                    turned_P(p, 1)
                if p is not None:
                    act.wait_ge(e_cx, this(1, p, 1))
                    act.activation(cxT[:, :, :], outp[:, 0:D].rearrange("p (h q) -> p h q", h=DC),
                                   ACT.Copy).then_inc(a_cx, 1)
                if n is not None:
                    high_context(n)
                if c is not None:
                    act.wait_ge(e_y, this(1, c, 1))
                    act.sem_inc(a_turn, 1)
                    act.activation(yT[0][:, :, bass.ds(c * P, P)], turn[:, 0:D].rearrange("p (c k) -> p c k", c=DC),
                                   ACT.Copy).then_inc(a_yhi, 1)
                if t is not None:
                    keep_value(t)

            walk(act, iteration)


def route1(nc, NT, CAP, logits, consts, tgate, share):
    B = 2 * NT
    BANK = 512 // E1
    banks = [(b, min(B, b + BANK)) for b in range(0, B, BANK)]
    with ExitStack() as ctx:
        sb = lambda name, shape, dt=F32: ctx.enter_context(nc.sbuf_tensor("r1_" + name, shape, dt))
        sem = lambda name: ctx.enter_context(nc.semaphore("r1_" + name))
        hot = sb("hot", [P, 2, NT, E1])
        hot16 = sb("hot16", [P, B * E1], F16)
        best = sb("best", [P, 2, NT])
        t = sb("t", [P, NT, E1])
        m = sb("m", [P, NT])
        zero = sb("zero", [P, B])
        count = sb("count", [P, B, E1])
        rank_sb = sb("rank_sb", [P, B, E1])
        upto = sb("upto", [P, E1, B])
        rank = [ctx.enter_context(nc.psum_tensor(f"r1_rank{n}", [P, 512], F32)) for n in range(len(banks))]
        total = [ctx.enter_context(nc.psum_tensor(f"r1_total{n}", [P, 512], F32)) for n in range(len(banks))]
        dv_step, dv_shift, ac_exp, dv_hot, pe_count = map(sem, ("dv_step", "dv_shift", "ac_exp", "dv_hot", "pe_count"))
        block = ctx.enter_context(nc.Block())

        @block.vector
        def _(dve):
            chain = Chain(dve, dv_step)
            values = logits[:, :].rearrange("p (t e) -> p t e", e=E1)
            wide = lambda y: y.unsqueeze(2).broadcast_to([P, NT, E1])
            chain(dve.tensor_reduce(m[:, :], values, AX_X, ALU.max))
            dve.tensor_tensor(values, values, wide(m[:, :]), ALU.subtract).then_inc(dv_shift, 1)
            dve.wait_ge(ac_exp, 1)
            chain(dve.tensor_reduce(m[:, :], values, AX_X, ALU.add))
            chain(dve.reciprocal(m[:, :], m[:, :]))
            chain(dve.tensor_tensor(values, values, wide(m[:, :]), ALU.mult))
            order = consts["order"][:, :].unsqueeze(1).broadcast_to([P, NT, E1])
            top2(dve, chain, values, order, hot, best, t[:, :, :], m[:, :])
            dve.tensor_copy(hot16[:, :], hot[:, :, :, :].rearrange("p k t e -> p (k t e)")).then_inc(dv_hot, 1)
            chain(dve.tensor_tensor(m[:, :], best[:, 0, :], best[:, 1, :], ALU.add))
            chain(dve.reciprocal(m[:, :], m[:, :]))
            chain(dve.tensor_scalar(m[:, :], m[:, :], tgate, None, ALU.mult))
            chain(dve.tensor_tensor(best[:, :, :], best[:, :, :], m[:, :].unsqueeze(1).broadcast_to([P, 2, NT]), ALU.mult))
            chain(dve.memset(zero[:, :], 0.0))
            dve.wait_ge(pe_count, 2 * len(banks))
            for n, (b0, b1) in enumerate(banks):
                dve.tensor_copy(rank_sb[:, b0:b1, :].rearrange("p b e -> p (b e)"), rank[n][:, 0:(b1 - b0) * E1])
                i = dve.tensor_copy(count[:, b0:b1, :].rearrange("p b e -> p (b e)"), total[n][:, 0:(b1 - b0) * E1])
            chain(i)
            for e in range(E1):
                i = dve.tensor_tensor_scan(upto[:, e, :], count[:, :, e], zero[:, :], 0.0, ALU.add, ALU.add)
            chain(i)
            chain(dve.tensor_tensor(count[:, :, :], upto[:, :, :].rearrange("p e b -> p b e"), count[:, :, :], ALU.subtract))
            chain(dve.tensor_tensor(count[:, :, :], count[:, :, :], rank_sb[:, :, :], ALU.add))
            chain(dve.tensor_scalar(count[:, :, :], count[:, :, :], float(CAP), None, ALU.is_lt))
            chain(dve.tensor_tensor(count[:, :, :], count[:, :, :], hot[:, :, :, :].rearrange("p k t e -> p (k t) e"), ALU.mult))
            chain(dve.tensor_tensor(count[:, :, :], count[:, :, :],
                                    best[:, :, :].rearrange("p k t -> p (k t)").unsqueeze(2).broadcast_to([P, B, E1]),
                                    ALU.mult))
            chain(dve.tensor_tensor(share[:, :, :], count[:, 0:NT, :], count[:, NT:B, :], ALU.add))

        @block.scalar
        def _(act):
            act.wait_ge(dv_shift, 1)
            act.activation(logits[:, :], logits[:, :], ACT.Exp).then_inc(ac_exp, 1)

        @block.tensor
        def _(pe):
            pe.wait_ge(dv_hot, 1)
            for n, (b0, b1) in enumerate(banks):
                for out, left in ((rank[n], "before"), (total[n], "ones")):
                    pe.matmul(out[:, 0:(b1 - b0) * E1], consts[left][:, :], hot16[:, b0 * E1:b1 * E1], start=True,
                              stop=True).then_inc(pe_count, 1)


def experts1(nc, NT, yT, w1, w3, w2_dram, share, ident, X, out):
    W = E1 * F1
    WC = W // P
    with ExitStack() as ctx:
        sb = lambda name, shape, dt=F32: ctx.enter_context(nc.sbuf_tensor("e1_" + name, shape, dt))
        ps = lambda name: ctx.enter_context(nc.psum_tensor("e1_" + name, [P, 512], F32))
        sem = lambda name: ctx.enter_context(nc.semaphore("e1_" + name))
        w2 = sb("w2", [P, WC, D])
        first = sb("first", [P, 2, W])
        inter = sb("inter", [P, 2, W])
        iT = sb("iT", [P, 2, W])
        up1 = [ps(f"up1{k}") for k in range(2)]
        up3 = [ps(f"up3{k}") for k in range(2)]
        turn = [ps(f"turn{k}") for k in range(2)]
        down = [ps(f"down{k}") for k in range(2)]
        w2_in = sem("w2_in")
        x4_out = sem("x4_out")
        pe_up1, pe_up3, pe_turn, pe_down, ac_first, ac_silu, ac_iT, dv_ab, dv_share, dv_x4 = map(sem, (
            "pe_up1", "pe_up3", "pe_turn", "pe_down", "ac_first", "ac_silu", "ac_iT", "dv_ab", "dv_share", "dv_x4"))
        block = ctx.enter_context(nc.Block())

        def done(t, ago=0):
            return t + 3 - ago

        def row(t):
            return X[:, bass.ds(t, 1), :].rearrange("p o d -> p (o d)")

        def walk(engine, step):
            step(0, 0, 0, True, False)
            with engine.Fori(0, NT // 2 - 1) as n:
                step(n * 2 + 1, n, 1, True, True)
                step(n * 2 + 2, n + 1, 0, True, True)
            step(NT - 1, NT // 2 - 1, 1, True, True)
            step(NT, NT // 2, 0, False, True)

        @block.sync
        def _(sp):
            sp.dma_start(w2[:, :, :], w2_dram.rearrange("p (c d) -> p c d", c=WC)).then_inc(w2_in, 16)
            with sp.Fori(0, NT) as t:
                sp.wait_ge(dv_x4, t + 3)
                sp.dma_start(out[bass.ds(t * P, P), :], row(t)).then_inc(x4_out, 16)
            sp.wait_ge(x4_out, 16 * NT)

        @block.tensor
        def _(pe):
            for s in (pe_up1, pe_up3, pe_turn, pe_down):
                pe.sem_inc(s, 2)
            pe.wait_ge(w2_in, 16)
            trio = [(c, i, j) for c in range(DC) for i, j in ((0, 0), (0, 1), (1, 0))]

            def up_product(bank, t, w):
                for q, (c, i, j) in enumerate(trio):
                    m = pe.matmul(bank[:, 0:W], yT[i][:, c, bass.ds(t * P, P)], w[j][:, c * W:(c + 1) * W],
                                  start=(q == 0), stop=(q == len(trio) - 1))
                return m

            def step(t, n, k, up, rest):
                if up:
                    pe.wait_ge(ac_first, done(t, 2))
                    up_product(up1[k], t, w1).then_inc(pe_up1, 1)
                if rest:
                    pe.wait_ge(dv_share, done(t, 1))
                    pe.wait_ge(ac_iT, done(t, 3))
                    for c in range(WC):
                        i = pe.transpose(turn[1 - k][:, c * P:(c + 1) * P], inter[:, 1 - k, c * P:(c + 1) * P], ident[:, :])
                    i.then_inc(pe_turn, 1)
                if up:
                    pe.wait_ge(dv_ab, done(t, 2))
                    up_product(up3[k], t, w3).then_inc(pe_up3, 1)
                if rest:
                    pe.wait_ge(ac_iT, done(t, 1))
                    pe.wait_ge(dv_x4, done(t, 3))
                    for c in range(WC):
                        i = pe.matmul(down[1 - k][:, 0:D], iT[:, 1 - k, c * P:(c + 1) * P], w2[:, c, :], start=(c == 0),
                                      stop=(c == WC - 1))
                    i.then_inc(pe_down, 1)

            walk(pe, step)

        @block.scalar
        def _(act):
            for s in (ac_first, ac_silu, ac_iT):
                act.sem_inc(s, 2)

            def step(t, n, k, up, rest):
                if up:
                    act.wait_ge(pe_up1, done(t))
                    act.wait_ge(dv_ab, done(t, 2))
                    act.activation(first[:, k, :], up1[k][:, 0:W], ACT.Copy).then_inc(ac_first, 1)
                if rest:
                    act.wait_ge(pe_turn, done(t, 1))
                    act.wait_ge(pe_down, done(t, 3))
                    act.activation(iT[:, 1 - k, :], turn[1 - k][:, 0:W], ACT.Copy).then_inc(ac_iT, 1)
                if up:
                    act.wait_ge(dv_ab, done(t))
                    act.activation(inter[:, k, :], inter[:, k, :], ACT.Silu, scale=1.0 / WSCALE**2).then_inc(ac_silu, 1)

            walk(act, step)

        @block.vector
        def _(dve):
            for s in (dv_ab, dv_share, dv_x4):
                dve.sem_inc(s, 2)

            def step(t, n, k, up, rest):
                if up:
                    dve.wait_ge(ac_first, done(t))
                    dve.wait_ge(pe_up3, done(t))
                    dve.wait_ge(pe_turn, done(t, 2))
                    dve.tensor_tensor(inter[:, k, :], first[:, k, :], up3[k][:, 0:W], ALU.mult).then_inc(dv_ab, 1)
                    dve.wait_ge(ac_silu, done(t))
                    i = inter[:, k, :].rearrange("p (e f) -> p e f", f=F1)
                    dve.tensor_tensor(i, i, share[:, bass.ds(t, 1), :].rearrange("p o e -> p e o")
                                      .broadcast_to([P, E1, F1]), ALU.mult).then_inc(dv_share, 1)
                if rest:
                    dve.wait_ge(pe_down, done(t, 1))
                    dve.tensor_tensor(row(t - 1), down[1 - k][:, 0:D], row(t - 1), ALU.add).then_inc(dv_x4, 1)

            walk(dve, step)


def program(nc, a, out, NT=32):
    scratch = lambda name, rows: nc.dram_tensor(name, (rows, D), F32, kind="Internal").ap()
    J = (2 * NT * P + E0 * (P - 1)) // P
    J += J % 2
    y1 = scratch("y1", NT * P)
    sorted0 = scratch("sorted0", J * P)
    rope_dram = nc.dram_tensor("rope_tables", (NT * P, 4 * HALF), F32, kind="Internal").ap()
    with ExitStack() as top:
        sb = lambda name, shape, dt=F32: top.enter_context(nc.sbuf_tensor(name, shape, dt))
        X = sb("X", [P, NT, D])
        ident = sb("ident", [P, P])
        logits = sb("logits0", [P, NT * E0])
        dest = sb("dest0", [P, 2, NT], I32)
        weight = sb("weight0", [P, 2, NT])
        consts = {name: sb(name, list(a[name].shape), F16 if name in ("before", "ones") else F32)
                  for name in ("order", "count", "token", "pair", "before", "ones")}
        const_in = top.enter_context(nc.semaphore("const_in"))
        constants = [(ident, a["ident"])] + [(tile, a[name]) for name, tile in consts.items()]

        def pairs(stack, **sizes):
            return {name: tuple(stack.enter_context(nc.sbuf_tensor(f"{name}_{h}", [P, n], F16)) for h in ("hi", "lo"))
                    for name, n in sizes.items()}

        def jobs(weights):
            return [(a[name], *(w[:, :] for w in pair)) for name, pair in weights.items()]

        layer1 = pairs(top, a1_wq=DC * D, a1_wk=DC * D, a1_wv=DC * D, gate1=DC * E1, e1_w1=DC * E1 * F1,
                       e1_w3=DC * E1 * F1)
        with ExitStack() as st:
            w = pairs(st, wq0=DC * H0 * HD0, wk0=DC * KV0 * HD0, wv0=DC * KV0 * HD0, wo0=H0 * D)
            rope_tables(nc, NT, a["pos"], a["freq"], rope_dram, jobs(w) + jobs(layer1),
                        constants, const_in)
            attention0(nc, NT, a["x"], a["ctxT"], rope_dram, a["qnw"], a["knw"], a["g_xattn"], w["wq0"], w["wk0"],
                       w["wv0"], w["wo0"], a["gate0"], ident, X, y1, logits)
        with ExitStack() as st:
            expert = st.enter_context(nc.sbuf_tensor("expert", [P, J], I32))
            index = st.enter_context(nc.sbuf_tensor("index", [P, J], I32))
            w = pairs(st, e0_w0=E0 * DC * F0, e0_w1=E0 * DC * F0, e0_wo=E0 * FC * D)
            route0(nc, NT, J, logits, consts, dest, weight, expert, index, jobs(w))
            experts0(nc, NT, J, y1, w["e0_w0"], w["e0_w1"], w["e0_wo"], expert, index, ident, sorted0)
        CAP = int(np.ceil(NT * P / E1 * 1.25))
        tgates = sb("tgates", [P, 4])
        logits1 = sb("logits1", [P, NT * E1])
        share1 = sb("share1", [P, NT, E1])
        yT = [sb(f"yT{h}", [P, DC, NT * P], F16) for h in ("hi", "lo")]
        attention1(nc, NT, a, consts, X, sorted0, dest, weight, layer1["a1_wq"], layer1["a1_wk"],
                   layer1["a1_wv"], layer1["gate1"], ident, tgates, logits1, yT)
        route1(nc, NT, CAP, logits1, consts, tgates[:, 1:2], share1)
        experts1(nc, NT, yT, layer1["e1_w1"], layer1["e1_w3"], a["e1_w2"], share1, ident, X, out)


def layout(i, NT=32):
    tok = lambda y: np.ascontiguousarray(np.asarray(y).reshape(-1, D)[:NT * P])
    chunks = lambda w: np.ascontiguousarray(w.reshape(-1, P, w.shape[1]).transpose(1, 0, 2).reshape(P, -1))
    rows = lambda w: chunks(np.asarray(w).T)
    columns = lambda y: np.ascontiguousarray(np.asarray(y).reshape(-1, P).T)
    experts = lambda w: np.ascontiguousarray(
        np.asarray(w).reshape(w.shape[0], -1, P, w.shape[2]).transpose(2, 0, 1, 3).reshape(P, -1))
    pos, itok = (np.asarray(i[k]).reshape(-1)[:NT * P].reshape(NT, P) for k in ("pos_BxS2", "itok_BxS_4096_4607"))
    inv = 1.0 / THETA ** (np.arange(0, HD0, 2, dtype=np.float32) / np.float32(HD0))
    c = np.asarray(i["ctx_2048"]).reshape(-1, D)[:NT * P].reshape(NT, P, DC, P)
    return {
        "x": tok(i["x"]),
        "ctxT": np.ascontiguousarray(c.transpose(3, 0, 2, 1).reshape(P, NT * D)),
        "pos": np.ascontiguousarray(np.stack([itok, pos], 1).transpose(2, 0, 1).reshape(P, NT * 2)),
        "freq": np.ascontiguousarray(np.broadcast_to(inv.astype(np.float32), (P, HALF))),
        "ident": np.eye(P, dtype=np.float32),
        "qnw": np.asarray(i["L0_xattn_q_norm_w"]), "knw": np.asarray(i["L0_xattn_k_norm_w"]),
        "g_xattn": np.asarray(i["g_xattn"]),
        "wq0": rows(i["L0_xattn_Wq"]), "wk0": rows(i["L0_xattn_Wk"]), "wv0": rows(i["L0_xattn_Wv"]),
        "order": np.ascontiguousarray(np.broadcast_to(np.arange(E1, 0, -1, dtype=np.float32), (P, E1))),
        "count": np.ascontiguousarray(np.broadcast_to(np.arange(P, dtype=np.float32), (P, P))),
        "token": np.ascontiguousarray(np.tile(np.arange(NT * P, dtype=np.float32).reshape(NT, P).T, (1, 2))),
        "before": np.triu(np.ones((P, P), np.float16), 1), "ones": np.ones((P, P), np.float16),
        "e0_w0": experts(i["L0_ffn_w0_kernel"]), "e0_w1": experts(i["L0_ffn_w1_kernel"]),
        "e0_wo": experts(i["L0_ffn_wo_kernel"]), "g_ffn": np.asarray(i["g_ffn"]),
        "pair": np.ascontiguousarray((np.arange(P)[:, None] % STRIP // HD1 == np.arange(2)).astype(np.float32)),
        "mask": np.asarray(i["mask_BxS2_ik0"])[:NT * NB],
        "a1_wq": rows(i["L1_xattn_Wq"]), "a1_wk": rows(i["L1_xattn_Wk"]), "a1_wv": rows(i["L1_xattn_Wv"]),
        "a1_wo": rows(i["L1_xattn_Wo"]), "a1_bq": columns(i["L1_xattn_bq"]), "a1_bk": columns(i["L1_xattn_bk"]),
        "a1_bv": np.asarray(i["L1_xattn_bv"]), "a1_bo": np.asarray(i["L1_xattn_bo"]),
        "a1_gamma": np.asarray(i["L1_xattn_ln_gamma"]), "a1_beta": np.asarray(i["L1_xattn_ln_beta"]),
        "a1_rs": np.asarray(i["L1_xattn_residual_scale"]).reshape(1),
        "gate1": rows(i["L1_ffn_gate_w"]), "e1_w1": rows(np.asarray(i["L1_ffn_w1"]).reshape(-1, D)),
        "e1_w3": rows(np.asarray(i["L1_ffn_w3"]).reshape(-1, D)),
        "e1_w2": chunks(np.asarray(i["L1_ffn_w2"]).transpose(0, 2, 1).reshape(-1, D)),
        "wo0": rows(i["L0_xattn_Wo"]), "gate0": chunks(np.asarray(i["L0_ffn_gate_kernel"])),
    }


def kernel(**inputs):
    import concourse.bacc as bacc
    from concourse.bass_utils import run_bass_kernel_spmd

    shape = np.asarray(inputs["x"]).shape
    arrays = {name: np.ascontiguousarray(y) for name, y in layout(inputs).items()}
    nc = bacc.Bacc("TRN2", target_bir_lowering=False, num_devices=1)
    a = {name: nc.dram_tensor(f"in_{name}", y.shape, mybir.dt.from_np(y.dtype), kind="ExternalInput").ap()
         for name, y in arrays.items()}
    out = nc.dram_tensor("out", (64 * S, D), F32, kind="ExternalOutput").ap()
    program(nc, a, out)
    result = run_bass_kernel_spmd(nc, [{f"in_{name}": y for name, y in arrays.items()}], core_ids=[0])
    return result.results[0]["out"].reshape(shape)
```
